# Optimizing a Trainium2 kernel written in Bass

```python
import numpy as np
import jax
import jax.numpy as jnp

def _softmax(x, axis=-1):
    return jax.nn.softmax(x, axis=axis)

def _gelu(x):
    return jax.nn.gelu(x, approximate=True)

def _silu(x):
    return jax.nn.silu(x)

def _sigmoid(x):
    return jax.nn.sigmoid(x)

def _layernorm(x, axis=-1, eps=1e-05):
    m = jnp.mean(x, axis=axis, keepdims=True)
    v = jnp.var(x, axis=axis, keepdims=True)
    return (x - m) / jnp.sqrt(v + eps)

def _scatter_add(tgt, idx, src, axis=0):
    return tgt.at[idx].add(src)

def _segment_sum(src, seg, n):
    return jax.ops.segment_sum(src, seg, n)
kernel_name = 'mk_xattn_ffn_d4_seqx_r4_3cb82f'

def setup_inputs(seed: int=0):
    np.random.seed(seed)
    _w = jnp.asarray

    def _rec_inputs():
        import jax
        import jax.numpy as jnp
        _rk = jax.random.key(seed)
        x = -0.0002928 + 1 * jax.random.normal(jax.random.fold_in(_rk, 1), (8, 256, 256), jnp.float32)
        _lenS = 256 - jax.random.randint(jax.random.fold_in(_rk, 7), (8,), 0, max(1, 256 // 4) + 1, jnp.int32)
        _lenS2 = 256 - jax.random.randint(jax.random.fold_in(_rk, 8), (8,), 0, max(1, 256 // 4) + 1, jnp.int32)
        _ctx_1024P = jax.random.normal(jax.random.fold_in(_rk, 11), (8, 16, 256), jnp.float32)
        _ctx_1024c = jax.random.dirichlet(jax.random.fold_in(_rk, 511), 0.3 * jnp.ones((16,), jnp.float32), (8, 256))
        _ctx_1024t = jnp.einsum('bsk,bkd->bsd', _ctx_1024c, _ctx_1024P)
        _ctx_1024t = _ctx_1024t * jax.lax.rsqrt(jnp.mean(jnp.square(_ctx_1024t)) + 1e-12) * 0.953939
        ctx_1024 = -1.39393e-06 + 0.999914 * (_ctx_1024t + 0.3 * jax.random.normal(jax.random.fold_in(_rk, 611), (8, 256, 256), jnp.float32))
        _validS = jnp.arange(256)[None, :] < _lenS[:, None]
        _validS2 = jnp.arange(256)[None, :] < _lenS2[:, None]
        _causal = jnp.tril(jnp.ones((256, 256), dtype=bool))
        mask_BxSxS2_ik1 = jnp.where(jnp.broadcast_to(_validS2[:, None, :], (8, 256, 256)), 1, 0).astype(jnp.int32)
        return (x, ctx_1024, mask_BxSxS2_ik1)
    x, ctx_1024, mask_BxSxS2_ik1 = _rec_inputs()

    def _L0_xattn_setup():
        import jax, jax.numpy as jnp
        import numpy as np
        B, S, D, H = (2, 512, 256, 16)
        DK = D // H

        def _split_heads(x):
            b, s, _ = x.shape
            return x.reshape(b, s, H, DK).transpose(0, 2, 1, 3)
        key = jax.random.key(seed)
        ks = jax.random.split(key, 13)
        scale = 1.0 / np.sqrt(D)
        return {'query': jax.random.normal(ks[0], (B, S, D), jnp.float32), 'key': jax.random.normal(ks[1], (B, S, D), jnp.float32), 'value': jax.random.normal(ks[2], (B, S, D), jnp.float32), 'mask': jax.random.randint(ks[3], (B, S, S), 0, 2, jnp.int32), 'Wq': jax.random.normal(ks[4], (D, D), jnp.float32) * scale, 'bq': jnp.zeros((D,), jnp.float32), 'Wk': jax.random.normal(ks[5], (D, D), jnp.float32) * scale, 'bk': jnp.zeros((D,), jnp.float32), 'Wv': jax.random.normal(ks[6], (D, D), jnp.float32) * scale, 'bv': jnp.zeros((D,), jnp.float32), 'Wo': jax.random.normal(ks[7], (D, D), jnp.float32) * scale, 'bo': jnp.zeros((D,), jnp.float32)}
    _L0_xattn_all = _L0_xattn_setup()
    _L0_xattn_in = {k: v for k, v in _L0_xattn_all.items() if k in ('Wq', 'bq', 'Wk', 'bk', 'Wv', 'bv', 'Wo', 'bo')}
    del _L0_xattn_all

    def _L0_ffn_setup():
        import jax, jax.numpy as jnp
        import numpy as np
        QB = 127.0
        EPS = 1e-05

        def _ste(x, q):
            return x + jax.lax.stop_gradient(q - x)

        def bitlinear(x, W, b):
            w_scale = jnp.clip(jnp.mean(jnp.abs(W)), EPS, None)
            Wq = _ste(W, jnp.clip(jnp.round(W / w_scale), -1.0, 1.0) * w_scale)
            x_scale = jnp.clip(jnp.max(jnp.abs(x), axis=-1, keepdims=True), EPS, None)
            xq = _ste(x, jnp.clip(jnp.round(x * (QB / x_scale)), -QB - 1.0, QB) * (x_scale / QB))
            return jnp.einsum('bnd,hd->bnh', xq, Wq) + b
        key = jax.random.key(seed)
        k0, k1, k2 = jax.random.split(key, 3)
        B, N, D = (8, 1024, 256)
        H = int(D * 4.0)
        x = jax.random.normal(k0, (B, N, D), dtype=jnp.float32)
        W1 = jax.random.normal(k1, (H, D), dtype=jnp.float32) * 0.02
        b1 = jnp.zeros((H,), dtype=jnp.float32)
        W2 = jax.random.normal(k2, (D, H), dtype=jnp.float32) * 0.02
        b2 = jnp.zeros((D,), dtype=jnp.float32)
        return {'x': x, 'W1': W1, 'b1': b1, 'W2': W2, 'b2': b2}
    _L0_ffn_all = _L0_ffn_setup()
    _L0_ffn_in = {k: v for k, v in _L0_ffn_all.items() if k in ('W1', 'b1', 'W2', 'b2')}
    del _L0_ffn_all

    def _L1_xattn_setup():
        import jax, jax.numpy as jnp
        import numpy as np
        DIM = 256
        HEADS = 16
        DIM_HEAD = 64
        INNER = HEADS * DIM_HEAD
        EPS = 1e-05

        def _split_heads(t):
            b, n, _ = t.shape
            return t.reshape(b, n, HEADS, DIM_HEAD).transpose(0, 2, 1, 3)
        key = jax.random.key(seed)
        ks = jax.random.split(key, 9)
        b, n, m = (2, 512, 64)
        s = DIM ** (-0.5)
        return {'x': jax.random.normal(ks[0], (b, n, DIM), jnp.float32), 'memories': jax.random.normal(ks[1], (b, m, DIM), jnp.float32), 'ln_g': jnp.ones((DIM,), jnp.float32), 'ln_b': jnp.zeros((DIM,), jnp.float32), 'Wq': jax.random.normal(ks[2], (DIM, INNER), jnp.float32) * s, 'Wkv': jax.random.normal(ks[3], (DIM, 2 * INNER), jnp.float32) * s, 'Wm': jax.random.normal(ks[4], (DIM, INNER), jnp.float32) * s, 'Wo': jax.random.normal(ks[5], (INNER, DIM), jnp.float32) * s, 'bo': jnp.zeros((DIM,), jnp.float32)}
    _L1_xattn_all = _L1_xattn_setup()
    _L1_xattn_in = {k: v for k, v in _L1_xattn_all.items() if k in ('ln_g', 'ln_b', 'Wq', 'Wkv', 'Wm', 'Wo', 'bo')}
    del _L1_xattn_all

    def _L1_ffn_setup():
        import jax, jax.numpy as jnp
        import numpy as np
        B, S, H, F, E = (8, 512, 256, 1024, 8)
        INIT_LAMBDA = 0.2
        key = jax.random.key(seed)
        ks = jax.random.split(key, 12)
        std = 0.02
        return {'hidden_states': jax.random.normal(ks[0], (B, S, H), jnp.float32), 'gate_w1': jax.random.normal(ks[1], (H, H), jnp.float32) * 0.01, 'gate_b1': jnp.zeros((H,), jnp.float32), 'gate_w2': jax.random.normal(ks[2], (E, H), jnp.float32) * 0.01, 'gate_b2': jnp.full((E,), INIT_LAMBDA, jnp.float32), 'W1': jax.random.normal(ks[3], (F, H), jnp.float32) * std, 'b1': jax.random.normal(ks[4], (F,), jnp.float32) * std, 'W2': jax.random.normal(ks[5], (H, F), jnp.float32) * std, 'b2': jax.random.normal(ks[6], (H,), jnp.float32) * std, 'TW1': jax.random.normal(ks[7], (E, F, H), jnp.float32) * std, 'Tb1': jax.random.normal(ks[8], (E, F), jnp.float32) * std, 'TW2': jax.random.normal(ks[9], (E, H, F), jnp.float32) * std, 'Tb2': jax.random.normal(ks[10], (E, H), jnp.float32) * std}
    _L1_ffn_all = _L1_ffn_setup()
    _L1_ffn_in = {k: v for k, v in _L1_ffn_all.items() if k in ('gate_w1', 'gate_b1', 'gate_w2', 'gate_b2', 'W1', 'b1', 'W2', 'b2', 'TW1', 'Tb1', 'TW2', 'Tb2')}
    del _L1_ffn_all

    def _L2_xattn_setup():
        import jax, jax.numpy as jnp
        import numpy as np
        B, S, D = (8, 512, 256)
        key = jax.random.key(seed)
        ks = jax.random.split(key, 13)
        s = 1.0 / np.sqrt(D)
        return {'queries': jax.random.normal(ks[0], (B, S, D), jnp.float32), 'keys': jax.random.normal(ks[1], (B, S, D), jnp.float32), 'values': jax.random.normal(ks[2], (B, S, D), jnp.float32), 'Wq': jax.random.normal(ks[3], (D, D), jnp.float32) * s, 'bq': jnp.zeros((D,), jnp.float32), 'Wk': jax.random.normal(ks[4], (D, D), jnp.float32) * s, 'bk': jnp.zeros((D,), jnp.float32), 'Wv': jax.random.normal(ks[5], (D, D), jnp.float32) * s, 'bv': jnp.zeros((D,), jnp.float32), 'Wg': jax.random.normal(ks[6], (D, D), jnp.float32) * s, 'bg': jnp.zeros((D,), jnp.float32), 'Wo': jax.random.normal(ks[7], (D, D), jnp.float32) * s, 'bo': jnp.zeros((D,), jnp.float32)}
    _L2_xattn_all = _L2_xattn_setup()
    _L2_xattn_in = {k: v for k, v in _L2_xattn_all.items() if k in ('Wq', 'bq', 'Wk', 'bk', 'Wv', 'bv', 'Wg', 'bg', 'Wo', 'bo')}
    del _L2_xattn_all

    def _L2_ffn_setup():
        import jax, jax.numpy as jnp
        import numpy as np
        H, I, E_ROUTED, TOP_K = (256, 704, 7, 2)
        B, S = (4, 512)

        def _expert(h, g, u, d):
            return jnp.einsum('...i,hi->...h', jax.nn.silu(h @ g.T) * (h @ u.T), d)
        key = jax.random.key(seed)
        ks = jax.random.split(key, 10)
        sc = 0.02
        return {'x': jax.random.normal(ks[0], (B, S, H), dtype=jnp.float32), 'sg': jax.random.normal(ks[1], (I, H), dtype=jnp.float32) * sc, 'su': jax.random.normal(ks[2], (I, H), dtype=jnp.float32) * sc, 'sd': jax.random.normal(ks[3], (H, I), dtype=jnp.float32) * sc, 'rg': jax.random.normal(ks[4], (E_ROUTED, I, H), dtype=jnp.float32) * sc, 'ru': jax.random.normal(ks[5], (E_ROUTED, I, H), dtype=jnp.float32) * sc, 'rd': jax.random.normal(ks[6], (E_ROUTED, H, I), dtype=jnp.float32) * sc, 'wr': jax.random.normal(ks[7], (E_ROUTED, H), dtype=jnp.float32) * sc, 'rb': jnp.zeros((E_ROUTED,), dtype=jnp.float32)}
    _L2_ffn_all = _L2_ffn_setup()
    _L2_ffn_in = {k: v for k, v in _L2_ffn_all.items() if k in ('sg', 'su', 'sd', 'rg', 'ru', 'rd', 'wr', 'rb')}
    del _L2_ffn_all

    def _L3_xattn_setup():
        import jax, jax.numpy as jnp
        import numpy as np
        B, C_LEN, Q_LEN, D = (8, 512, 128, 256)
        key = jax.random.key(seed)
        ks = jax.random.split(key, 10)
        scale = 1.0 / np.sqrt(D)
        return {'c': jax.random.normal(ks[0], (B, C_LEN, D), dtype=jnp.float32), 'q': jax.random.normal(ks[1], (B, Q_LEN, D), dtype=jnp.float32), 'w_cq': jax.random.normal(ks[2], (D,), dtype=jnp.float32) * scale, 'b_cq': jax.random.normal(ks[3], (), dtype=jnp.float32) * scale, 'w_c': jax.random.normal(ks[4], (D,), dtype=jnp.float32) * scale, 'b_c': jax.random.normal(ks[5], (), dtype=jnp.float32) * scale, 'w_q': jax.random.normal(ks[6], (D,), dtype=jnp.float32) * scale, 'b_q': jax.random.normal(ks[7], (), dtype=jnp.float32) * scale, 'W_l': jax.random.normal(ks[8], (D, 4 * D), dtype=jnp.float32) * (1.0 / np.sqrt(4 * D)), 'b_l': jax.random.normal(ks[9], (D,), dtype=jnp.float32) * (1.0 / np.sqrt(4 * D))}
    _L3_xattn_all = _L3_xattn_setup()
    _L3_xattn_in = {k: v for k, v in _L3_xattn_all.items() if k in ('w_cq', 'b_cq', 'w_c', 'b_c', 'w_q', 'b_q', 'W_l', 'b_l')}
    del _L3_xattn_all

    def _L3_ffn_setup():
        import jax, jax.numpy as jnp
        import numpy as np
        D_MODEL, HIDDEN, N_EXPERTS, TOP_K = (256, 512, 8, 2)
        RMS_EPS = 1e-06
        key = jax.random.key(seed)
        ks = jax.random.split(key, 6)
        B, S = (4, 512)
        return {'x': jax.random.normal(ks[0], (B, S, D_MODEL), jnp.float32), 'norm_weight': jnp.ones((D_MODEL,), jnp.float32), 'gate_w': jax.random.normal(ks[1], (N_EXPERTS, D_MODEL), jnp.float32) * 0.02, 'w1': jax.random.normal(ks[2], (N_EXPERTS, HIDDEN, D_MODEL), jnp.float32) * 0.02, 'b1': jnp.zeros((N_EXPERTS, HIDDEN), jnp.float32), 'w2': jax.random.normal(ks[3], (N_EXPERTS, D_MODEL, HIDDEN), jnp.float32) * 0.02, 'b2': jnp.zeros((N_EXPERTS, D_MODEL), jnp.float32)}
    _L3_ffn_all = _L3_ffn_setup()
    _L3_ffn_in = {k: v for k, v in _L3_ffn_all.items() if k in ('norm_weight', 'gate_w', 'w1', 'b1', 'w2', 'b2')}
    del _L3_ffn_all
    return {'x': x, 'ctx_1024': ctx_1024, 'mask_BxSxS2_ik1': mask_BxSxS2_ik1, 'L0_xattn_Wq': _L0_xattn_in['Wq'], 'L0_xattn_bq': _L0_xattn_in['bq'], 'L0_xattn_Wk': _L0_xattn_in['Wk'], 'L0_xattn_bk': _L0_xattn_in['bk'], 'L0_xattn_Wv': _L0_xattn_in['Wv'], 'L0_xattn_bv': _L0_xattn_in['bv'], 'L0_xattn_Wo': _L0_xattn_in['Wo'], 'L0_xattn_bo': _L0_xattn_in['bo'], 'L0_ffn_W1': _L0_ffn_in['W1'], 'L0_ffn_b1': _L0_ffn_in['b1'], 'L0_ffn_W2': _L0_ffn_in['W2'], 'L0_ffn_b2': _L0_ffn_in['b2'], 'L1_xattn_ln_g': _L1_xattn_in['ln_g'], 'L1_xattn_ln_b': _L1_xattn_in['ln_b'], 'L1_xattn_Wq': _L1_xattn_in['Wq'], 'L1_xattn_Wkv': _L1_xattn_in['Wkv'], 'L1_xattn_Wm': _L1_xattn_in['Wm'], 'L1_xattn_Wo': _L1_xattn_in['Wo'], 'L1_xattn_bo': _L1_xattn_in['bo'], 'L1_ffn_gate_w1': _L1_ffn_in['gate_w1'], 'L1_ffn_gate_b1': _L1_ffn_in['gate_b1'], 'L1_ffn_gate_w2': _L1_ffn_in['gate_w2'], 'L1_ffn_gate_b2': _L1_ffn_in['gate_b2'], 'L1_ffn_W1': _L1_ffn_in['W1'], 'L1_ffn_b1': _L1_ffn_in['b1'], 'L1_ffn_W2': _L1_ffn_in['W2'], 'L1_ffn_b2': _L1_ffn_in['b2'], 'L1_ffn_TW1': _L1_ffn_in['TW1'], 'L1_ffn_Tb1': _L1_ffn_in['Tb1'], 'L1_ffn_TW2': _L1_ffn_in['TW2'], 'L1_ffn_Tb2': _L1_ffn_in['Tb2'], 'L2_xattn_Wq': _L2_xattn_in['Wq'], 'L2_xattn_bq': _L2_xattn_in['bq'], 'L2_xattn_Wk': _L2_xattn_in['Wk'], 'L2_xattn_bk': _L2_xattn_in['bk'], 'L2_xattn_Wv': _L2_xattn_in['Wv'], 'L2_xattn_bv': _L2_xattn_in['bv'], 'L2_xattn_Wg': _L2_xattn_in['Wg'], 'L2_xattn_bg': _L2_xattn_in['bg'], 'L2_xattn_Wo': _L2_xattn_in['Wo'], 'L2_xattn_bo': _L2_xattn_in['bo'], 'L2_ffn_sg': _L2_ffn_in['sg'], 'L2_ffn_su': _L2_ffn_in['su'], 'L2_ffn_sd': _L2_ffn_in['sd'], 'L2_ffn_rg': _L2_ffn_in['rg'], 'L2_ffn_ru': _L2_ffn_in['ru'], 'L2_ffn_rd': _L2_ffn_in['rd'], 'L2_ffn_wr': _L2_ffn_in['wr'], 'L2_ffn_rb': _L2_ffn_in['rb'], 'L3_xattn_w_cq': _L3_xattn_in['w_cq'], 'L3_xattn_b_cq': _L3_xattn_in['b_cq'], 'L3_xattn_w_c': _L3_xattn_in['w_c'], 'L3_xattn_b_c': _L3_xattn_in['b_c'], 'L3_xattn_w_q': _L3_xattn_in['w_q'], 'L3_xattn_b_q': _L3_xattn_in['b_q'], 'L3_xattn_W_l': _L3_xattn_in['W_l'], 'L3_xattn_b_l': _L3_xattn_in['b_l'], 'L3_ffn_norm_weight': _L3_ffn_in['norm_weight'], 'L3_ffn_gate_w': _L3_ffn_in['gate_w'], 'L3_ffn_w1': _L3_ffn_in['w1'], 'L3_ffn_b1': _L3_ffn_in['b1'], 'L3_ffn_w2': _L3_ffn_in['w2'], 'L3_ffn_b2': _L3_ffn_in['b2']}

def reference(x, ctx_1024, mask_BxSxS2_ik1, L0_xattn_Wq, L0_xattn_bq, L0_xattn_Wk, L0_xattn_bk, L0_xattn_Wv, L0_xattn_bv, L0_xattn_Wo, L0_xattn_bo, L0_ffn_W1, L0_ffn_b1, L0_ffn_W2, L0_ffn_b2, L1_xattn_ln_g, L1_xattn_ln_b, L1_xattn_Wq, L1_xattn_Wkv, L1_xattn_Wm, L1_xattn_Wo, L1_xattn_bo, L1_ffn_gate_w1, L1_ffn_gate_b1, L1_ffn_gate_w2, L1_ffn_gate_b2, L1_ffn_W1, L1_ffn_b1, L1_ffn_W2, L1_ffn_b2, L1_ffn_TW1, L1_ffn_Tb1, L1_ffn_TW2, L1_ffn_Tb2, L2_xattn_Wq, L2_xattn_bq, L2_xattn_Wk, L2_xattn_bk, L2_xattn_Wv, L2_xattn_bv, L2_xattn_Wg, L2_xattn_bg, L2_xattn_Wo, L2_xattn_bo, L2_ffn_sg, L2_ffn_su, L2_ffn_sd, L2_ffn_rg, L2_ffn_ru, L2_ffn_rd, L2_ffn_wr, L2_ffn_rb, L3_xattn_w_cq, L3_xattn_b_cq, L3_xattn_w_c, L3_xattn_b_c, L3_xattn_w_q, L3_xattn_b_q, L3_xattn_W_l, L3_xattn_b_l, L3_ffn_norm_weight, L3_ffn_gate_w, L3_ffn_w1, L3_ffn_b1, L3_ffn_w2, L3_ffn_b2):
    import jax
    import jax.numpy as jnp

    def _L0_xattn_ref(query, key, value, mask, Wq, bq, Wk, bk, Wv, bv, Wo, bo):
        import jax, jax.numpy as jnp
        import numpy as np
        B, S, D, H = (2, 512, 256, 16)
        DK = D // H

        def _split_heads(x):
            b, s, _ = x.shape
            return x.reshape(b, s, H, DK).transpose(0, 2, 1, 3)
        q = _split_heads(query @ Wq + bq)
        k = _split_heads(key @ Wk + bk)
        v = _split_heads(value @ Wv + bv)
        scores = jnp.einsum('bhqd,bhkd->bhqk', q, k) / jnp.sqrt(jnp.float32(DK))
        scores = jnp.where(mask[:, None, :, :] == 0, jnp.float32(-1000000000.0), scores)
        p_attn = jax.nn.softmax(scores, axis=-1)
        x = jnp.einsum('bhqk,bhkd->bhqd', p_attn, v)
        x = x.transpose(0, 2, 1, 3).reshape(query.shape[0], -1, D)
        return x @ Wo + bo

    def _L0_ffn_ref(x, W1, b1, W2, b2):
        import jax, jax.numpy as jnp
        import numpy as np
        QB = 127.0
        EPS = 1e-05

        def _ste(x, q):
            return x + jax.lax.stop_gradient(q - x)

        def bitlinear(x, W, b):
            w_scale = jnp.clip(jnp.mean(jnp.abs(W)), EPS, None)
            Wq = _ste(W, jnp.clip(jnp.round(W / w_scale), -1.0, 1.0) * w_scale)
            x_scale = jnp.clip(jnp.max(jnp.abs(x), axis=-1, keepdims=True), EPS, None)
            xq = _ste(x, jnp.clip(jnp.round(x * (QB / x_scale)), -QB - 1.0, QB) * (x_scale / QB))
            return jnp.einsum('bnd,hd->bnh', xq, Wq) + b
        h = bitlinear(x, W1, b1)
        h = jax.nn.gelu(h, approximate=False)
        return bitlinear(h, W2, b2)

    def _L1_xattn_ref(x, memories, ln_g, ln_b, Wq, Wkv, Wm, Wo, bo):
        import jax, jax.numpy as jnp
        import numpy as np
        DIM = 256
        HEADS = 16
        DIM_HEAD = 64
        INNER = HEADS * DIM_HEAD
        EPS = 1e-05

        def _split_heads(t):
            b, n, _ = t.shape
            return t.reshape(b, n, HEADS, DIM_HEAD).transpose(0, 2, 1, 3)
        mu = jnp.mean(x, axis=-1, keepdims=True)
        var = jnp.mean(jnp.square(x - mu), axis=-1, keepdims=True)
        xn = (x - mu) * jax.lax.rsqrt(var + EPS) * ln_g + ln_b
        q = _split_heads(xn @ Wq)
        kv = xn @ Wkv
        k = _split_heads(kv[..., :INNER])
        v = _split_heads(kv[..., INNER:])
        mem = _split_heads(memories @ Wm)
        k = jnp.concatenate([k, mem], axis=2)
        v = jnp.concatenate([v, mem], axis=2)
        scale = DIM_HEAD ** (-0.5)
        dots = jnp.einsum('bhid,bhjd->bhij', q, k) * scale
        attn = jax.nn.softmax(dots, axis=-1)
        out = jnp.einsum('bhij,bhjd->bhid', attn, v)
        b, h, n, d = out.shape
        out = out.transpose(0, 2, 1, 3).reshape(b, n, h * d)
        return out @ Wo + bo

    def _L1_ffn_ref(hidden_states, gate_w1, gate_b1, gate_w2, gate_b2, W1, b1, W2, b2, TW1, Tb1, TW2, Tb2):
        import jax, jax.numpy as jnp
        import numpy as np
        B, S, H, F, E = (8, 512, 256, 1024, 8)
        INIT_LAMBDA = 0.2
        x = hidden_states
        h = jax.nn.relu(jnp.einsum('bsh,oh->bso', x, gate_w1) + gate_b1)
        g = jnp.einsum('bso,eo->bse', h, gate_w2) + gate_b2
        g = g.mean(axis=1)
        mW1 = W1 + jnp.einsum('be,efh->bfh', g, TW1)
        mb1 = b1 + g @ Tb1
        mW2 = W2 + jnp.einsum('be,ehf->bhf', g, TW2)
        mb2 = b2 + g @ Tb2
        u = jax.nn.gelu(jnp.einsum('bsh,bfh->bsf', x, mW1) + mb1[:, None, :])
        out = jnp.einsum('bsf,bhf->bsh', u, mW2) + mb2[:, None, :]
        return out

    def _L2_xattn_ref(queries, keys, values, Wq, bq, Wk, bk, Wv, bv, Wg, bg, Wo, bo):
        import jax, jax.numpy as jnp
        import numpy as np
        B, S, D = (8, 512, 256)
        q = queries @ Wq + bq
        k = keys @ Wk + bk
        v = values @ Wv + bv
        scores = jnp.einsum('bqd,bkd->bqk', q, k)
        attn = jax.nn.softmax(scores, axis=-1)
        context = jnp.einsum('bqk,bkd->bqd', attn, v)
        gate = jax.nn.sigmoid(queries @ Wg + bg)
        return context * gate @ Wo + bo

    def _L2_ffn_ref(x, sg, su, sd, rg, ru, rd, wr, rb):
        import jax, jax.numpy as jnp
        import numpy as np
        H, I, E_ROUTED, TOP_K = (256, 704, 7, 2)
        B, S = (4, 512)

        def _expert(h, g, u, d):
            return jnp.einsum('...i,hi->...h', jax.nn.silu(h @ g.T) * (h @ u.T), d)
        shared_out = _expert(x, sg, su, sd)
        logits = x @ wr.T + rb
        probs = jax.nn.softmax(logits, axis=-1)
        scores, idx = jax.lax.top_k(probs, TOP_K)
        scores = scores / scores.sum(axis=-1, keepdims=True)
        w = jnp.sum(scores[..., None] * jax.nn.one_hot(idx, E_ROUTED, dtype=x.dtype), axis=-2)
        out = shared_out
        for e in range(E_ROUTED):
            out = out + w[..., e:e + 1] * _expert(x, rg[e], ru[e], rd[e])
        return out

    def _L3_xattn_ref(c, q, w_cq, b_cq, w_c, b_c, w_q, b_q, W_l, b_l):
        import jax, jax.numpy as jnp
        import numpy as np
        B, C_LEN, Q_LEN, D = (8, 512, 128, 256)
        cq = jnp.einsum('bcd,bqd,d->bcq', c, q, w_cq) + b_cq
        s = (c @ w_c + b_c)[:, :, None] + (q @ w_q + b_q)[:, None, :] + cq
        a = jax.nn.softmax(s, axis=2)
        c2q_att = jnp.einsum('bcq,bqd->bcd', a, q)
        b_att = jax.nn.softmax(jnp.max(s, axis=2), axis=1)
        q2c_att = jnp.einsum('bc,bcd->bd', b_att, c)[:, None, :]
        x = jnp.concatenate([c, c2q_att, c * c2q_att, c * q2c_att], axis=-1)
        z = x @ W_l.T + b_l
        return z

    def _L3_ffn_ref(x, norm_weight, gate_w, w1, b1, w2, b2):
        import jax, jax.numpy as jnp
        import numpy as np
        D_MODEL, HIDDEN, N_EXPERTS, TOP_K = (256, 512, 8, 2)
        RMS_EPS = 1e-06
        B, S, D = x.shape
        E = gate_w.shape[0]
        t = x * jax.lax.rsqrt(jnp.mean(x * x, axis=-1, keepdims=True) + RMS_EPS) * norm_weight
        tokens = t.reshape(-1, D)
        T = tokens.shape[0]
        gate_logits = tokens @ gate_w.T
        gate_scores, expert_idx = jax.lax.top_k(gate_logits, TOP_K)
        routing_weights = jax.nn.softmax(gate_scores, axis=-1)
        combine = jnp.zeros((T, E), tokens.dtype).at[jnp.arange(T)[:, None], expert_idx].add(routing_weights)

        def body(acc, params):
            W1, B1, W2, B2, c = params
            h = jax.nn.gelu(tokens @ W1.T + B1, approximate=False)
            o = h @ W2.T + B2
            return (acc + c[:, None] * o, None)
        out, _ = jax.lax.scan(body, jnp.zeros_like(tokens), (w1, b1, w2, b2, combine.T))
        return x + out.reshape(B, S, D)
    x = x + _L0_xattn_ref(_layernorm(x, axis=-1), ctx_1024, ctx_1024, mask_BxSxS2_ik1, L0_xattn_Wq, L0_xattn_bq, L0_xattn_Wk, L0_xattn_bk, L0_xattn_Wv, L0_xattn_bv, L0_xattn_Wo, L0_xattn_bo)
    x = x + _L0_ffn_ref(_layernorm(x, axis=-1), L0_ffn_W1, L0_ffn_b1, L0_ffn_W2, L0_ffn_b2)
    x = x + _L1_xattn_ref(_layernorm(x, axis=-1), ctx_1024, L1_xattn_ln_g, L1_xattn_ln_b, L1_xattn_Wq, L1_xattn_Wkv, L1_xattn_Wm, L1_xattn_Wo, L1_xattn_bo)
    x = x + _L1_ffn_ref(_layernorm(x, axis=-1), L1_ffn_gate_w1, L1_ffn_gate_b1, L1_ffn_gate_w2, L1_ffn_gate_b2, L1_ffn_W1, L1_ffn_b1, L1_ffn_W2, L1_ffn_b2, L1_ffn_TW1, L1_ffn_Tb1, L1_ffn_TW2, L1_ffn_Tb2)
    x = x + _L2_xattn_ref(_layernorm(x, axis=-1), ctx_1024, ctx_1024, L2_xattn_Wq, L2_xattn_bq, L2_xattn_Wk, L2_xattn_bk, L2_xattn_Wv, L2_xattn_bv, L2_xattn_Wg, L2_xattn_bg, L2_xattn_Wo, L2_xattn_bo)
    x = x + _L2_ffn_ref(_layernorm(x, axis=-1), L2_ffn_sg, L2_ffn_su, L2_ffn_sd, L2_ffn_rg, L2_ffn_ru, L2_ffn_rd, L2_ffn_wr, L2_ffn_rb)
    x = x + _L3_xattn_ref(_layernorm(x, axis=-1), ctx_1024, L3_xattn_w_cq, L3_xattn_b_cq, L3_xattn_w_c, L3_xattn_b_c, L3_xattn_w_q, L3_xattn_b_q, L3_xattn_W_l, L3_xattn_b_l)
    x = x + _L3_ffn_ref(_layernorm(x, axis=-1), L3_ffn_norm_weight, L3_ffn_gate_w, L3_ffn_w1, L3_ffn_b1, L3_ffn_w2, L3_ffn_b2)
    return x

_drawn_inputs = setup_inputs


def setup_inputs(seed=0):
    import zlib

    import numpy as np

    out = dict(_drawn_inputs(seed))
    spreads = {'L0_xattn_bq': (0.0, 0.1),
     'L0_xattn_bk': (0.0, 0.8),
     'L0_xattn_bv': (0.0, 0.1),
     'L0_xattn_bo': (0.0, 0.1),
     'L0_ffn_b1': (0.0, 0.1),
     'L0_ffn_b2': (0.0, 0.1),
     'L1_xattn_ln_g': (1.0, 0.2),
     'L1_xattn_ln_b': (0.0, 0.1),
     'L1_xattn_bo': (0.0, 0.1),
     'L1_ffn_gate_b1': (0.0, 0.8),
     'L1_ffn_gate_b2': (0.20000000298023224, 0.2),
     'L2_xattn_bq': (0.0, 0.1),
     'L2_xattn_bk': (0.0, 0.8),
     'L2_xattn_bv': (0.0, 0.1),
     'L2_xattn_bg': (0.0, 0.457),
     'L2_xattn_bo': (0.0, 0.1),
     'L2_ffn_rb': (0.0, 0.8),
     'L3_ffn_norm_weight': (1.0, 0.6),
     'L3_ffn_b1': (0.0, 0.8),
     'L3_ffn_b2': (0.0, 0.31)}
    factors = {'L1_ffn_gate_w1': 8.0,
     'L1_ffn_gate_w2': 5.04,
     'L1_ffn_b1': 6.233,
     'L1_ffn_Tb1': 8.0,
     'L1_ffn_Tb2': 4.186,
     'L2_ffn_sg': 2.97,
     'L2_ffn_su': 2.795,
     'L2_ffn_sd': 2.809,
     'L2_ffn_rg': 4.233,
     'L2_ffn_ru': 4.233,
     'L2_ffn_rd': 4.202,
     'L2_ffn_wr': 5.076,
     'L3_xattn_b_l': 2.972}
    for name, (base, spread) in spreads.items():
        noise = np.random.default_rng([zlib.crc32(name.encode()), seed]).standard_normal(out[name].shape)
        drawn = base * np.exp(spread * noise) if base else spread * noise
        out[name] = jnp.asarray(drawn.astype(out[name].dtype))
    for name, factor in factors.items():
        out[name] = (out[name] * factor).astype(out[name].dtype)
    return out
```

```python
from contextlib import ExitStack

import concourse.bass as bass
from concourse import mybir

F32 = mybir.dt.float32
BF16 = mybir.dt.bfloat16
I32 = mybir.dt.int32
U32 = mybir.dt.uint32
ALU = mybir.AluOpType
ACT = mybir.ActivationFunctionType
AX = mybir.AxisListType

P = 128
B, S, D = 8, 256, 256
TOK = B * S
NT = TOK // P
TPB = S // P
KD = D // P
H = 16
DK0, PAD0 = D // H, 32
M0 = H * PAD0 // P
DH1, INNER1 = 64, H * 64
M1 = INNER1 // P
F0, F1 = 1024, 1024
E1, R1 = 8, 16
I2, E2 = 704, 7
F3, E3 = 512, 8
NE = 8
LN_EPS = 1e-5
RMS_EPS = 1e-6
QB = 127.0
QEPS = 1e-5
ROUND = 1.5 * 2.0 ** 23
MASKED = -(2.0 ** 30)
NEVER = -3.0e38


class Shared:
    pass


def semaphores(nc, ctx, stage, names):
    names = names.split()
    free = sorted(nc.free_semaphores)
    first = next(n for n in free if all(n + i in free for i in range(len(names))))
    sems = [nc.alloc_semaphore(f"{stage}_{n}", first + i) for i, n in enumerate(names)]

    def end():
        nc.all_engine_barrier(sems_to_clear=range(first, first + len(sems)))
        for s in sems:
            nc.release_semaphore(s)

    ctx.callback(end)
    return sems


def x_tile(sh, t):
    return sh.X[:, bass.ds(t * D, D)]


def x_batch(sh, b):
    return sh.X[:, bass.ds(b * TPB * D, TPB * D)]


def tiles(ap, n=TPB):
    return ap.rearrange("p (t d) -> p t d", t=n)


def over_tiles(ap, n=TPB):
    return ap.unsqueeze(1).to_broadcast([P, n, ap.shape[1]])


def layernorm_vector(dve, sh, src, dst, stats, stats_ready, rstd_ready, normed, b, eps=LN_EPS, per=1, k=0):
    for t in range(TPB):
        ins = dve.bn_stats(sh.bn6[:, t, :], src(t))
    ins.then_inc(stats, 1)
    dve.wait_ge(stats, b * (3 * per) + 3 * k + 1)
    dve.sem_inc(stats, 1)
    for t in range(TPB):
        ins = dve.bn_aggr(sh.mv[:, t, :], sh.bn6[:, t, :])
    ins.then_inc(stats, 1)
    dve.wait_ge(stats, b * (3 * per) + 3 * k + 3)
    dve.tensor_scalar(sh.var[:], sh.mv[:, :, 1], eps, None, ALU.add).then_inc(stats_ready, 1)
    dve.wait_ge(rstd_ready, b * per + k + 1)
    for t in range(TPB):
        ins = dve.tensor_scalar(dst[:, t, :], src(t), sh.mv[:, t, 0:1], sh.rstd[:, t:t + 1], ALU.subtract, ALU.mult)
    ins.then_inc(normed, 1)


def layernorm_pool(pool, sh, stats_ready, rstd_ready, n):
    pool.wait_ge(stats_ready, n + 1)
    pool.tensor_tensor(sh.rstd[:], sh.var[:], sh.minus_half[:], ALU.pow).then_inc(rstd_ready, 1)


def transpose_batch(pe, sh, out, src, n_rows=TPB, n_cols=KD):
    for c in range(n_cols):
        for t in range(n_rows):
            ins = pe.transpose(out[:, (c * n_rows + t) * P:(c * n_rows + t + 1) * P], src[:, t, c * P:(c + 1) * P], sh.ident[:])
    return ins


def product(pe, out, lhsT, rhs):
    n = len(lhsT)
    for k in range(n):
        ins = pe.matmul(out, lhsT[k], rhs[k], start=(k == 0), stop=(k == n - 1))
    return ins


def stage_start(nc, sh, d):
    with ExitStack() as ctx:
        x_loaded, zeroed, made = semaphores(nc, ctx, "st", "x_loaded zeroed made")
        block = ctx.enter_context(nc.Block())

        @block.sync
        def _(sp):
            sp.dma_start(tiles(sh.X[:], NT), d["x"]).then_inc(x_loaded, 16)
            sp.wait_ge(x_loaded, 16)

        @block.gpsimd
        def _(pool):
            pool.memset(sh.ident[:], 0.0).then_inc(zeroed, 1)
            pool.wait_ge(zeroed, 1)
            pool.affine_select(out=sh.ident[:], in_=sh.ident[:], compare_op=ALU.not_equal, fill=1.0, base=0,
                               pattern=[[-1, P]], channel_multiplier=1).then_inc(made, 1)
            pool.memset(sh.minus_half[:], -0.5).then_inc(made, 1)
            pool.memset(sh.ones[:], 1.0).then_inc(made, 1)
            pool.wait_ge(made, 3)
            pool.tensor_copy(sh.ident16[:], sh.ident[:]).then_inc(made, 1)
            pool.wait_ge(made, 4)


def stage_l0_attention(nc, sh, d):
    with ExitStack() as ctx:
        def sb(name, shape, dt=F32):
            return ctx.enter_context(nc.sbuf_tensor("a_" + name, shape, dt))

        wq, wk = sb("wq", [P, KD, H * PAD0]), sb("wk", [P, KD, H * PAD0])
        wv, wo = sb("wv", [P, KD, D]), sb("wo", [P, KD, D])
        bq, bqs, bk = sb("bq", [P, M0]), sb("bqs", [P, M0]), sb("bk", [P, M0])
        bv, bo = sb("bv", [P, D]), sb("bo", [P, D])
        ctxT = sb("ctxT", [P, KD, S])
        mask = sb("mask", [P, TPB, S], I32)
        lowered = sb("lowered", [P, TPB * S])
        xn = sb("xn", [P, TPB, D])
        xnT, qT, kT = sb("xnT", [P, KD, S]), sb("qT", [P, M0, S]), sb("kT", [P, M0, S])
        v = sb("v", [P, TPB, D])
        sm, probs, probsT = sb("sm", [P, 2, TPB, S]), sb("probs", [P, 2, TPB, S]), sb("probsT", [P, 2, TPB, S])
        negmax, sums, rsums = sb("negmax", [P, 2, TPB]), sb("sums", [P, TPB, H]), sb("rsums", [P, TPB, H])
        att, attT = sb("att", [P, TPB, D]), sb("attT", [P, KD, S])
        xo = sb("xo", [P, TPB, D])
        (w_loaded, ctx_loaded, mask_loaded, ctx_used, mask_used, stats, stats_ready, rstd_ready, xn_ready, xnT_ps,
         xnT_ready, k_ps, k_ready, v_ps, v_ready, q_ps, q_ready, s_ps, s_masked, max_ready, exp_ready, probsT_ps,
         probsT_ready, head_done, rsums_ready, att_ready, attT_ps, attT_ready, out_ps, out_read, x_done,
         bias_ready) = semaphores(
            nc, ctx, "a", "w_loaded ctx_loaded mask_loaded ctx_used mask_used stats stats_ready rstd_ready xn_ready "
            "xnT_ps xnT_ready k_ps k_ready v_ps v_ready q_ps q_ready s_ps s_masked max_ready exp_ready probsT_ps "
            "probsT_ready head_done rsums_ready att_ready attT_ps attT_ready out_ps out_read x_done bias_ready")
        bank = sh.bank
        xnT_p, k_p, v_p, q_p = bank[0], [bank[1], bank[2]], bank[3], [bank[4], bank[5]]
        s_p, probsT_p, o_p, attT_p, out_p = [bank[6], bank[7]], [bank[0], bank[1]], bank[2], bank[3], bank[4]
        WEIGHTS = [(wq, "L0_wq"), (wk, "L0_wk"), (wv, "L0_wv"), (wo, "L0_wo"), (bq, "L0_bq"), (bk, "L0_bk"),
                   (bv, "L0_bv"), (bo, "L0_bo")]
        block = ctx.enter_context(nc.Block())

        @block.sync
        def _(sp):
            for dst, name in WEIGHTS:
                sp.dma_start(dst[:], d[name]).then_inc(w_loaded, 16)
            with sp.Fori(0, B) as b:
                sp.wait_ge(ctx_used, b + 1)
                sp.dma_start(ctxT[:], d["ctxT"][:, bass.ds(b * KD, KD), :]).then_inc(ctx_loaded, 16)
                sp.wait_ge(mask_used, b + 1)
                sp.dma_start(mask[:], d["mask"][:, bass.ds(b * TPB, TPB), :]).then_inc(mask_loaded, 16)

        @block.gpsimd
        def _(pool):
            with pool.Fori(0, B) as b:
                layernorm_pool(pool, sh, stats_ready, rstd_ready, b)

        @block.vector
        def _(dve):
            dve.sem_inc(mask_used, 1)
            dve.wait_ge(w_loaded, 16 * len(WEIGHTS))
            dve.tensor_scalar(bqs[:], bq[:], DK0 ** -0.5, None, ALU.mult).then_inc(bias_ready, 1)
            with dve.Fori(0, B) as b:
                layernorm_vector(dve, sh, lambda t: x_tile(sh, b * TPB + t), xn, stats, stats_ready, rstd_ready, xn_ready, b)
                dve.wait_ge(mask_loaded, b * 16 + 16)
                dve.tensor_scalar(tiles(lowered[:]), mask[:], 0.0, MASKED, ALU.is_equal, ALU.mult).then_inc(mask_used, 1)
                dve.wait_ge(v_ps, b + 1)
                dve.tensor_tensor(v[:], tiles(v_p[:]), over_tiles(bv[:]), ALU.add).then_inc(v_ready, 1)
                dve.wait_ge(mask_used, b + 2)
                for h in range(H):
                    dve.wait_ge(s_ps, b * H + h + 1)
                    if h >= 2:
                        dve.wait_ge(exp_ready, b * H + h - 1)
                    dve.tensor_tensor(sm[:, h % 2].rearrange("p t s -> p (t s)"), s_p[h % 2][:], lowered[:], ALU.add)\
                       .then_inc(s_masked, 1)
                    dve.wait_ge(s_masked, b * H + h + 1)
                    dve.tensor_reduce(negmax[:, h % 2], sm[:, h % 2], AX.X, ALU.max, negate=True).then_inc(max_ready, 1)
                dve.wait_ge(exp_ready, b * H + H)
                dve.reciprocal(rsums[:], sums[:]).then_inc(rsums_ready, 1)
                dve.wait_ge(rsums_ready, b + 1)
                dve.wait_ge(head_done, b * H + H)
                for t in range(TPB):
                    ins = dve.tensor_tensor(att[:, t].rearrange("p (h e) -> p h e", h=H),
                                            o_p[:, t * D:(t + 1) * D].rearrange("p (h e) -> p h e", h=H),
                                            rsums[:, t].unsqueeze(2).to_broadcast([P, H, DK0]), ALU.mult)
                ins.then_inc(att_ready, 1)
                dve.wait_ge(out_ps, b + 1)
                dve.tensor_tensor(xo[:], tiles(out_p[:]), over_tiles(bo[:]), ALU.add).then_inc(out_read, 1)
                dve.wait_ge(out_read, b + 1)
                dve.tensor_tensor(x_batch(sh, b), x_batch(sh, b), xo[:].rearrange("p t d -> p (t d)"), ALU.add).then_inc(x_done, 1)
            dve.wait_ge(x_done, B)

        @block.scalar
        def _(act):
            act.wait_ge(bias_ready, 1)
            with act.Fori(0, B) as b:
                act.wait_ge(xnT_ps, b + 1)
                act.activation(xnT[:].rearrange("p c s -> p (c s)"), xnT_p[:], ACT.Copy).then_inc(xnT_ready, 1)
                act.wait_ge(k_ps, b + 1)
                for m in range(M0):
                    ins = act.activation(kT[:, m], k_p[m // 2][:, m % 2 * S:(m % 2 + 1) * S], ACT.Identity, bias=bk[:, m:m + 1])
                ins.then_inc(k_ready, 1)
                act.wait_ge(q_ps, b + 1)
                for m in range(M0):
                    ins = act.activation(qT[:, m], q_p[m // 2][:, m % 2 * S:(m % 2 + 1) * S], ACT.Identity,
                                         bias=bqs[:, m:m + 1], scale=DK0 ** -0.5)
                ins.then_inc(q_ready, 1)

                def exp(h):
                    act.wait_ge(max_ready, b * H + h + 1)
                    if h >= 2:
                        act.wait_ge(probsT_ps, b * H + h - 1)
                    for t in range(TPB):
                        ins = act.activation(probs[:, h % 2, t], sm[:, h % 2, t], ACT.Exp, bias=negmax[:, h % 2, t:t + 1],
                                             accum_out=sums[:, t, h:h + 1])
                    ins.then_inc(exp_ready, 1)

                exp(0)
                for h in range(H):
                    if h + 1 < H:
                        exp(h + 1)
                    act.wait_ge(probsT_ps, b * H + h + 1)
                    if h >= 2:
                        act.wait_ge(head_done, b * H + h - 1)
                    act.activation(probsT[:, h % 2].rearrange("p c s -> p (c s)"), probsT_p[h % 2][:], ACT.Copy)\
                       .then_inc(probsT_ready, 1)
                act.wait_ge(attT_ps, b + 1)
                act.activation(attT[:].rearrange("p c s -> p (c s)"), attT_p[:], ACT.Copy).then_inc(attT_ready, 1)

        @block.tensor
        def _(pe):
            pe.sem_inc(ctx_used, 1)
            pe.wait_ge(w_loaded, 16 * len(WEIGHTS))
            with pe.Fori(0, B) as b:
                pe.wait_ge(xn_ready, b + 1)
                transpose_batch(pe, sh, xnT_p, xn).then_inc(xnT_ps, 1)
                pe.wait_ge(ctx_loaded, b * 16 + 16)
                for m in range(M0):
                    ins = product(pe, k_p[m // 2][:, m % 2 * S:(m % 2 + 1) * S],
                                  [wk[:, c, m * P:(m + 1) * P] for c in range(KD)], [ctxT[:, c] for c in range(KD)])
                ins.then_inc(k_ps, 1)
                for t in range(TPB):
                    ins = product(pe, v_p[:, t * D:(t + 1) * D], [ctxT[:, c, t * P:(t + 1) * P] for c in range(KD)],
                                  [wv[:, c] for c in range(KD)])
                ins.then_inc(v_ps, 1)
                pe.wait_ge(v_ps, b + 1)
                pe.sem_inc(ctx_used, 1)
                pe.wait_ge(xnT_ready, b + 1)
                for m in range(M0):
                    ins = product(pe, q_p[m // 2][:, m % 2 * S:(m % 2 + 1) * S],
                                  [wq[:, c, m * P:(m + 1) * P] for c in range(KD)], [xnT[:, c] for c in range(KD)])
                ins.then_inc(q_ps, 1)

                def scores(h):
                    r = h % 4 * PAD0
                    if h >= 2:
                        pe.wait_ge(s_masked, b * H + h - 1)
                    for t in range(TPB):
                        ins = pe.matmul(s_p[h % 2][:, t * S:(t + 1) * S], qT[r:r + DK0, h // 4, t * P:(t + 1) * P],
                                        kT[r:r + DK0, h // 4], start=True, stop=True)
                    ins.then_inc(s_ps, 1)

                def turn(h):
                    pe.wait_ge(exp_ready, b * H + h + 1)
                    if h >= 2:
                        pe.wait_ge(probsT_ready, b * H + h - 1)
                    transpose_batch(pe, sh, probsT_p[h % 2], probs[:, h % 2]).then_inc(probsT_ps, 1)

                def values(h):
                    pe.wait_ge(probsT_ready, b * H + h + 1)
                    for t in range(TPB):
                        ins = product(pe, o_p[:, t * D + h * DK0:t * D + (h + 1) * DK0],
                                      [probsT[:, h % 2, c, t * P:(t + 1) * P] for c in range(TPB)],
                                      [v[:, c, h * DK0:(h + 1) * DK0] for c in range(TPB)])
                    ins.then_inc(head_done, 1)

                pe.wait_ge(k_ready, b + 1)
                pe.wait_ge(q_ready, b + 1)
                scores(0)
                scores(1)
                pe.wait_ge(v_ready, b + 1)
                for h in range(H):
                    turn(h)
                    if h + 2 < H:
                        scores(h + 2)
                    if h >= 1:
                        values(h - 1)
                values(H - 1)
                pe.wait_ge(att_ready, b + 1)
                transpose_batch(pe, sh, attT_p, att).then_inc(attT_ps, 1)
                pe.wait_ge(attT_ready, b + 1)
                for t in range(TPB):
                    ins = product(pe, out_p[:, t * D:(t + 1) * D], [attT[:, c, t * P:(t + 1) * P] for c in range(KD)],
                                  [wo[:, c] for c in range(KD)])
                ins.then_inc(out_ps, 1)


def stage_l0_ffn(nc, sh, d):
    with ExitStack() as ctx:
        def sb(name, shape, dt=F32):
            return ctx.enter_context(nc.sbuf_tensor("b_" + name, shape, dt))

        KF = F0 // P
        w, wq = sb("w", [P, 2, KD * F0]), sb("wq", [P, 2, KD * F0], BF16)
        wsum, wscale, winv = sb("wsum", [P, 2]), sb("wscale", [P, 2]), sb("winv", [P, 2])
        b1, b2 = sb("b1", [P, F0]), sb("b2", [P, D])
        xn, xr, xq, xqT = sb("xn", [P, TPB, D]), sb("xr", [P, TPB, D]), sb("xq", [P, TPB, D], BF16), sb("xqT", [P, TPB, D], BF16)
        h, hr, hq = sb("h", [P, TPB, F0]), sb("hr", [P, TPB, F0]), sb("hq", [P, TPB, F0], BF16)
        hqT = sb("hqT", [P, TPB, F0], BF16)
        xa, xinv, xscale = sb("xa", [P, TPB]), sb("xinv", [P, TPB]), sb("xscale", [P, TPB])
        ha, hinv, hscale = sb("ha", [P, TPB]), sb("hinv", [P, TPB]), sb("hscale", [P, TPB])
        xo = sb("xo", [P, TPB, D])
        (w_loaded, chain, sum_ready, total_ps, weights_ready, stats, stats_ready, rstd_ready, xn_ready, xq_ready,
         xqT_ps, xqT_ready, h_ps, h_scaled, gelu_done, hq_ready, hqT_ps, hqT_ready, out_ps, step) = semaphores(
            nc, ctx, "b", "w_loaded chain sum_ready total_ps weights_ready stats stats_ready rstd_ready xn_ready xq_ready "
            "xqT_ps xqT_ready h_ps h_scaled gelu_done hq_ready hqT_ps hqT_ready out_ps step")
        bank = sh.bank
        total_p, xqT_p, h_p = bank[0], bank[0], [[bank[1], bank[2]], [bank[3], bank[4]]]
        hqT_p, out_p = [bank[5], bank[6]], bank[7]
        w1q = wq[:, 0].rearrange("p (c f) -> p c f", c=KD)
        w2q = wq[:, 1].rearrange("p (c f) -> p c f", c=KF)
        STEPS = 11
        block = ctx.enter_context(nc.Block())

        @block.sync
        def _(sp):
            for dst, name in [(w[:, 0], "L0_w1"), (w[:, 1], "L0_w2"), (b1[:], "L0_b1"), (b2[:], "L0_b2")]:
                sp.dma_start(dst, d[name]).then_inc(w_loaded, 16)

        @block.gpsimd
        def _(pool):
            with pool.Fori(0, B) as b:
                layernorm_pool(pool, sh, stats_ready, rstd_ready, b)

        @block.vector
        def _(dve):
            dve.wait_ge(w_loaded, 4 * 16)
            dve.tensor_reduce(wsum[:], w[:], AX.X, ALU.add, apply_absolute_value=True).then_inc(sum_ready, 1)
            dve.wait_ge(total_ps, 1)
            dve.tensor_scalar(wscale[:], total_p[:, 0:2], 1.0 / (D * F0), QEPS, ALU.mult, ALU.max).then_inc(chain, 1)
            dve.wait_ge(chain, 1)
            dve.reciprocal(winv[:], wscale[:]).then_inc(chain, 1)
            dve.wait_ge(chain, 2)
            for k in range(2):
                dve.tensor_scalar(w[:, k], w[:, k], winv[:, k:k + 1], ROUND, ALU.mult, ALU.add).then_inc(chain, 1)
            dve.wait_ge(chain, 4)
            dve.tensor_scalar(w[:], w[:], ROUND, 1.0, ALU.subtract, ALU.min).then_inc(chain, 1)
            dve.wait_ge(chain, 5)
            dve.tensor_scalar(wq[:], w[:], -1.0, None, ALU.max).then_inc(weights_ready, 1)

            with dve.Fori(0, B) as b:
                s0 = b * STEPS

                def quantize(x, absmax, inv, scale, k, rounded, q, ready, s):
                    dve.tensor_reduce(absmax[:], x[:], AX.X, ALU.max, apply_absolute_value=True).then_inc(step, 1)
                    dve.wait_ge(step, s + 1)
                    dve.tensor_scalar(absmax[:], absmax[:], QEPS, None, ALU.max).then_inc(step, 1)
                    dve.wait_ge(step, s + 2)
                    dve.tensor_scalar(scale[:], absmax[:], wscale[:, k:k + 1], 1.0 / QB, ALU.mult, ALU.mult)
                    dve.reciprocal(inv[:], absmax[:]).then_inc(step, 1)
                    dve.wait_ge(step, s + 3)
                    dve.tensor_scalar(inv[:], inv[:], QB, None, ALU.mult).then_inc(step, 1)
                    dve.wait_ge(step, s + 4)
                    for t in range(TPB):
                        ins = dve.tensor_scalar(rounded[:, t], x[:, t], inv[:, t:t + 1], ROUND, ALU.mult, ALU.add)
                    ins.then_inc(step, 1)
                    dve.wait_ge(step, s + 5)
                    for t in range(TPB):
                        ins = dve.tensor_scalar(q[:, t], rounded[:, t], ROUND, QB, ALU.subtract, ALU.min)
                    ins.then_inc(ready, 1)
                    dve.wait_ge(ready, 2 * b + 1)
                    dve.tensor_scalar(q[:], q[:], -QB - 1.0, None, ALU.max).then_inc(ready, 1)

                layernorm_vector(dve, sh, lambda t: x_tile(sh, b * TPB + t), xn, stats, stats_ready, rstd_ready, xn_ready, b)
                dve.wait_ge(xn_ready, b + 1)
                quantize(xn, xa, xinv, xscale, 0, xr, xq, xq_ready, s0)
                dve.wait_ge(xqT_ps, b + 1)
                dve.tensor_copy(xqT[:].rearrange("p t d -> p (t d)"), xqT_p[:].bitcast(BF16)[:, 0:TPB * D]).then_inc(xqT_ready, 1)
                for t in range(TPB):
                    dve.wait_ge(h_ps, b * TPB + t + 1)
                    for n in range(2):
                        ins = dve.scalar_tensor_tensor(h[:, t, n * 512:(n + 1) * 512], h_p[t][n][:], xscale[:, t:t + 1],
                                                       b1[:, n * 512:(n + 1) * 512], ALU.mult, ALU.add)
                    ins.then_inc(h_scaled, 1)
                dve.wait_ge(gelu_done, b * TPB + TPB)
                quantize(h, ha, hinv, hscale, 1, hr, hq, hq_ready, s0 + 5)
                dve.wait_ge(out_ps, b + 1)
                for t in range(TPB):
                    ins = dve.scalar_tensor_tensor(xo[:, t], out_p[:, t * D:(t + 1) * D], hscale[:, t:t + 1], b2[:], ALU.mult, ALU.add)
                ins.then_inc(step, 1)
                dve.wait_ge(step, s0 + STEPS)
                dve.tensor_tensor(x_batch(sh, b), x_batch(sh, b), xo[:].rearrange("p t d -> p (t d)"), ALU.add)

        @block.scalar
        def _(act):
            with act.Fori(0, B) as b:
                for t in range(TPB):
                    act.wait_ge(h_scaled, b * TPB + t + 1)
                    act.activation(h[:, t], h[:, t], ACT.Gelu).then_inc(gelu_done, 1)
                for t in range(TPB):
                    act.wait_ge(hqT_ps, b * TPB + t + 1)
                    act.activation(hqT[:, t], hqT_p[t][:].bitcast(BF16), ACT.Copy).then_inc(hqT_ready, 1)

        @block.tensor
        def _(pe):
            pe.wait_ge(sum_ready, 1)
            pe.matmul(total_p[:, 0:2], sh.ones[:], wsum[:], start=True, stop=True).then_inc(total_ps, 1)
            pe.wait_ge(weights_ready, 1)
            with pe.Fori(0, B) as b:
                pe.wait_ge(xq_ready, 2 * b + 2)
                for t in range(TPB):
                    for c in range(KD):
                        at = (t * KD + c) * P
                        ins = pe.transpose(xqT_p[:].bitcast(BF16)[:, at:at + P], xq[:, t, c * P:(c + 1) * P], sh.ident16[:])
                ins.then_inc(xqT_ps, 1)
                pe.wait_ge(xqT_ready, b + 1)
                for t in range(TPB):
                    for n in range(2):
                        ins = product(pe, h_p[t][n][:], [xqT[:, t, c * P:(c + 1) * P] for c in range(KD)],
                                      [w1q[:, c, n * 512:(n + 1) * 512] for c in range(KD)])
                    ins.then_inc(h_ps, 1)
                pe.wait_ge(hq_ready, 2 * b + 2)
                for t in range(TPB):
                    for c in range(KF):
                        ins = pe.transpose(hqT_p[t][:].bitcast(BF16)[:, c * P:(c + 1) * P], hq[:, t, c * P:(c + 1) * P], sh.ident16[:])
                    ins.then_inc(hqT_ps, 1)
                for t in range(TPB):
                    pe.wait_ge(hqT_ready, b * TPB + t + 1)
                    ins = product(pe, out_p[:, t * D:(t + 1) * D], [hqT[:, t, c * P:(c + 1) * P] for c in range(KF)],
                                  [w2q[:, c] for c in range(KF)])
                ins.then_inc(out_ps, 1)


def stage_l1_attention(nc, sh, d):
    with ExitStack() as ctx:
        def sb(name, shape, dt=F32):
            return ctx.enter_context(nc.sbuf_tensor("c_" + name, shape, dt))

        SK = 2 * S
        KC = SK // P
        wq, wk, wv, wm = [sb(n, [P, KD, INNER1]) for n in ("wq", "wk", "wv", "wm")]
        wo = sb("wo", [P, M1, D])
        gain, shift, bo = sb("gain", [P, KD]), sb("shift", [P, KD]), sb("bo", [P, D])
        ctxT = sb("ctxT", [P, KD, S])
        x1, xn = sb("x1", [P, TPB, D]), sb("xn", [P, TPB, D])
        xnT = sb("xnT", [P, KD, S])
        qT, kT, v = sb("qT", [P, M1, S]), sb("kT", [P, M1, SK]), sb("v", [P, KC, INNER1])
        probs, probsT = sb("probs", [P, 2, SK]), sb("probsT", [P, 2, KC, P])
        negmax, sums, rsums = sb("negmax", [P, 2]), sb("sums", [P, TPB, H]), sb("rsums", [P, TPB, H])
        att, attT = sb("att", [P, TPB, INNER1]), sb("attT", [P, M1, S])
        xo = sb("xo", [P, TPB, D])
        (w_loaded, ctx_loaded, ctx_used, stats, stats_ready, rstd_ready, xn_ready, xnT_ps, xnT_ready, proj_ps, evac_a,
         evac_v, s_ps, max_ready, exp_ready, probsT_ps, probsT_a, probsT_v, head_done, rsums_ready, att_ready, attT_ps,
         attT_a, attT_v, out_ps, out_read) = semaphores(
            nc, ctx, "c", "w_loaded ctx_loaded ctx_used stats stats_ready rstd_ready xn_ready xnT_ps xnT_ready proj_ps "
            "evac_a evac_v s_ps max_ready exp_ready probsT_ps probsT_a probsT_v head_done rsums_ready att_ready attT_ps "
            "attT_a attT_v out_ps out_read")
        bank = sh.bank
        xnT_p, s_p, probsT_p = bank[4], [bank[5], bank[6]], [bank[0], bank[1]]
        o_p = [[bank[2], bank[3]], [bank[4], bank[7]]]
        attT_p, out_p = [bank[0], bank[1], bank[5], bank[6]], bank[2]
        WEIGHTS = [(wq, "L1_wq"), (wk, "L1_wk"), (wv, "L1_wv"), (wm, "L1_wm"), (wo, "L1_wo"), (gain, "L1_g"),
                   (shift, "L1_b"), (bo, "L1_bo")]
        jobs = []
        for m in range(M1):
            col = slice(m * P, (m + 1) * P)
            jobs.append(([(slice(0, S), [wk[:, c, col] for c in range(KD)], [xnT[:, c] for c in range(KD)]),
                          (slice(S, SK), [wm[:, c, col] for c in range(KD)], [ctxT[:, c] for c in range(KD)])],
                         kT[:, m], 1.0))
        for m in range(0, M1, 2):
            jobs.append(([(slice(i * S, (i + 1) * S), [wq[:, c, (m + i) * P:(m + i + 1) * P] for c in range(KD)],
                           [xnT[:, c] for c in range(KD)]) for i in range(2)],
                         qT[:, m:m + 2].rearrange("p m s -> p (m s)"), DH1 ** -0.5))
        for c4 in range(KC):
            src, w = (xnT, wv) if c4 < TPB else (ctxT, wm)
            row = slice(c4 % TPB * P, (c4 % TPB + 1) * P)
            for n in range(INNER1 // 512):
                col = slice(n * 512, (n + 1) * 512)
                jobs.append(([(slice(0, 512), [src[:, c, row] for c in range(KD)], [w[:, c, col] for c in range(KD)])],
                             v[:, c4, col], 1.0))
        NJ, NU = len(jobs), TPB * H
        NPB = 4
        block = ctx.enter_context(nc.Block())

        @block.sync
        def _(sp):
            for dst, name in WEIGHTS:
                sp.dma_start(dst[:], d[name]).then_inc(w_loaded, 16)
            with sp.Fori(0, B) as b:
                sp.wait_ge(ctx_used, b + 1)
                sp.dma_start(ctxT[:], d["ctxT"][:, bass.ds(b * KD, KD), :]).then_inc(ctx_loaded, 16)

        @block.gpsimd
        def _(pool):
            with pool.Fori(0, B) as b:
                layernorm_pool(pool, sh, stats_ready, rstd_ready, b * 2)
                layernorm_pool(pool, sh, stats_ready, rstd_ready, b * 2 + 1)

        @block.vector
        def _(dve):
            dve.wait_ge(w_loaded, 16 * len(WEIGHTS))
            with dve.Fori(0, B) as b:
                layernorm_vector(dve, sh, lambda t: x_tile(sh, b * TPB + t), x1, stats, stats_ready, rstd_ready, xn_ready, b, per=2)
                dve.wait_ge(xn_ready, 2 * b + 1)
                layernorm_vector(dve, sh, lambda t: x1[:, t], xn, stats, stats_ready, rstd_ready, xn_ready, b, per=2, k=1)
                for j in range(1, NJ, 2):
                    dve.wait_ge(proj_ps, b * NJ + j + 1)
                    dve.tensor_scalar(jobs[j][1], bank[j % NPB][:], jobs[j][2], None, ALU.mult).then_inc(evac_v, 1)

                def row_max(u):
                    dve.wait_ge(s_ps, b * NU + u + 1)
                    if u >= 2:
                        dve.wait_ge(exp_ready, b * NU + u - 1)
                    dve.tensor_reduce(negmax[:, u % 2:u % 2 + 1], s_p[u % 2][:], AX.X, ALU.max, negate=True).then_inc(max_ready, 1)

                row_max(0)
                row_max(1)
                for u in range(NU):
                    if u % 2:
                        dve.wait_ge(probsT_ps, b * NU + u + 1)
                        if u >= 2:
                            dve.wait_ge(head_done, b * NU + u - 1)
                        dve.tensor_copy(probsT[:, 1].rearrange("p c s -> p (c s)"), probsT_p[1][:]).then_inc(probsT_v, 1)
                    if u + 2 < NU:
                        row_max(u + 2)
                dve.reciprocal(rsums[:], sums[:]).then_inc(rsums_ready, 1)
                dve.wait_ge(rsums_ready, b + 1)
                dve.wait_ge(head_done, b * NU + NU)
                for t in range(TPB):
                    for n in range(2):
                        ins = dve.tensor_tensor(att[:, t, n * 512:(n + 1) * 512].rearrange("p (h e) -> p h e", e=DH1),
                                                o_p[t][n][:].rearrange("p (h e) -> p h e", e=DH1),
                                                rsums[:, t, n * 8:(n + 1) * 8].unsqueeze(2).to_broadcast([P, 8, DH1]), ALU.mult)
                ins.then_inc(att_ready, 1)
                for i in (1, 3):
                    dve.wait_ge(attT_ps, b * 4 + i + 1)
                    dve.tensor_copy(attT[:, 2 * i:2 * i + 2].rearrange("p c s -> p (c s)"), attT_p[i][:]).then_inc(attT_v, 1)
                dve.wait_ge(out_ps, b + 1)
                dve.tensor_tensor(xo[:], tiles(out_p[:]), over_tiles(bo[:]), ALU.add).then_inc(out_read, 1)
                dve.wait_ge(out_read, b + 1)
                dve.tensor_tensor(x_batch(sh, b), x_batch(sh, b), xo[:].rearrange("p t d -> p (t d)"), ALU.add)

        @block.scalar
        def _(act):
            act.wait_ge(w_loaded, 16 * len(WEIGHTS))
            with act.Fori(0, B) as b:
                act.wait_ge(xnT_ps, b + 1)
                for c in range(KD):
                    ins = act.activation(xnT[:, c], xnT_p[:, c * S:(c + 1) * S], ACT.Identity, bias=shift[:, c:c + 1],
                                         scale=gain[:, c:c + 1])
                ins.then_inc(xnT_ready, 1)
                for j in range(0, NJ, 2):
                    act.wait_ge(proj_ps, b * NJ + j + 1)
                    act.activation(jobs[j][1], bank[j % NPB][:], ACT.Copy, scale=jobs[j][2]).then_inc(evac_a, 1)

                def exp(u):
                    act.wait_ge(max_ready, b * NU + u + 1)
                    if u >= 2:
                        act.wait_ge(probsT_ps, b * NU + u - 1)
                    act.activation(probs[:, u % 2], s_p[u % 2][:], ACT.Exp, bias=negmax[:, u % 2:u % 2 + 1],
                                   accum_out=sums[:, u // H, u % H:u % H + 1]).then_inc(exp_ready, 1)

                exp(0)
                for u in range(NU):
                    if u + 1 < NU:
                        exp(u + 1)
                    if u % 2 == 0:
                        act.wait_ge(probsT_ps, b * NU + u + 1)
                        if u >= 2:
                            act.wait_ge(head_done, b * NU + u - 1)
                        act.activation(probsT[:, 0].rearrange("p c s -> p (c s)"), probsT_p[0][:], ACT.Copy).then_inc(probsT_a, 1)
                for i in (0, 2):
                    act.wait_ge(attT_ps, b * 4 + i + 1)
                    act.activation(attT[:, 2 * i:2 * i + 2].rearrange("p c s -> p (c s)"), attT_p[i][:], ACT.Copy).then_inc(attT_a, 1)

        @block.tensor
        def _(pe):
            pe.sem_inc(ctx_used, 1)
            pe.wait_ge(w_loaded, 16 * len(WEIGHTS))
            with pe.Fori(0, B) as b:
                pe.wait_ge(xn_ready, 2 * b + 2)
                transpose_batch(pe, sh, xnT_p, xn).then_inc(xnT_ps, 1)
                pe.wait_ge(ctx_loaded, b * 16 + 16)
                pe.wait_ge(xnT_ready, b + 1)
                for j, (parts, _, _) in enumerate(jobs):
                    if j >= NPB:
                        pe.wait_ge(evac_v if j % 2 else evac_a, b * (NJ // 2) + (j - NPB) // 2 + 1)
                    for cols, lhsT, rhs in parts:
                        ins = product(pe, bank[j % NPB][:, cols], lhsT, rhs)
                    ins.then_inc(proj_ps, 1)
                pe.wait_ge(proj_ps, b * NJ + NJ)
                pe.sem_inc(ctx_used, 1)
                pe.wait_ge(evac_a, (b + 1) * (NJ // 2))
                pe.wait_ge(evac_v, (b + 1) * (NJ // 2))

                def scores(u):
                    t, h = u // H, u % H
                    r = h % 2 * DH1
                    if u >= 2:
                        pe.wait_ge(exp_ready, b * NU + u - 1)
                    pe.matmul(s_p[u % 2][:], qT[r:r + DH1, h // 2, t * P:(t + 1) * P], kT[r:r + DH1, h // 2], start=True, stop=True)\
                      .then_inc(s_ps, 1)

                def turn(u):
                    pe.wait_ge(exp_ready, b * NU + u + 1)
                    if u >= 2:
                        pe.wait_ge(probsT_v if u % 2 else probsT_a, b * (NU // 2) + u // 2)
                    for c in range(KC):
                        ins = pe.transpose(probsT_p[u % 2][:, c * P:(c + 1) * P], probs[:, u % 2, c * P:(c + 1) * P], sh.ident[:])
                    ins.then_inc(probsT_ps, 1)

                def values(u):
                    t, h = u // H, u % H
                    pe.wait_ge(probsT_v if u % 2 else probsT_a, b * (NU // 2) + u // 2 + 1)
                    product(pe, o_p[t][h // 8][:, h % 8 * DH1:(h % 8 + 1) * DH1], [probsT[:, u % 2, c] for c in range(KC)],
                            [v[:, c, h * DH1:(h + 1) * DH1] for c in range(KC)]).then_inc(head_done, 1)

                scores(0)
                scores(1)
                for u in range(NU):
                    turn(u)
                    if u + 2 < NU:
                        scores(u + 2)
                    if u >= 1:
                        values(u - 1)
                values(NU - 1)
                pe.wait_ge(att_ready, b + 1)
                for i in range(4):
                    for k in range(2):
                        for t in range(TPB):
                            ins = pe.transpose(attT_p[i][:, (k * TPB + t) * P:(k * TPB + t + 1) * P],
                                               att[:, t, (2 * i + k) * P:(2 * i + k + 1) * P], sh.ident[:])
                    ins.then_inc(attT_ps, 1)
                pe.wait_ge(attT_a, b * 2 + 2)
                pe.wait_ge(attT_v, b * 2 + 2)
                for t in range(TPB):
                    ins = product(pe, out_p[:, t * D:(t + 1) * D], [attT[:, c, t * P:(t + 1) * P] for c in range(M1)],
                                  [wo[:, c] for c in range(M1)])
                ins.then_inc(out_ps, 1)


def stage_l1_ffn(nc, sh, d):
    with ExitStack() as ctx:
        def sb(name, shape, dt=F32):
            return ctx.enter_context(nc.sbuf_tensor("d_" + name, shape, dt))

        KF = F1 // P
        FB, HB = F1 // R1, D // R1
        NCH = 16
        FPC = FB // NCH
        gw1, gb1 = sb("gw1", [P, KD, D]), sb("gb1", [P, KD])
        gw2r, gb2r = sb("gw2r", [P, KD, P]), sb("gb2r", [P, 1])
        gw2a, gb2a = sb("gw2a", [P, KD, E1 + 1]), sb("gb2a", [E1 + 1, 1])
        tb1, tb2 = sb("tb1", [E1 + 1, F1]), sb("tb2", [E1 + 1, D])
        w1, w2 = sb("w1", [P, KD, F1]), sb("w2", [P, KF, D])
        pieces = sb("pieces", [P, 4 * 1024])
        tw = [pieces[:, i * 1024:(i + 1) * 1024] for i in range(4)]
        w1b = pieces[:, 0:KD * F1].rearrange("p (c f) -> p c f", c=KD)
        w2b = pieces[:, KD * F1:KD * F1 + KF * D].rearrange("p (c f) -> p c f", c=KF)
        m1, m2 = sb("m1", [P, KD, B, F1]), sb("m2", [P, KF, B, D])
        xnT = sb("xnT", [P, KD, TOK])
        xn, xTb, hrelu = [m1[:, 0, i, :].rearrange("p (t d) -> p t d", t=2)[:, :, 0:D] for i in range(3)]
        hsum, hsums = sb("hsum", [P, KD]), sb("hsums", [P, KD, B])
        gcol, dup, G, gT = sb("gcol", [P, B]), sb("dup", [P, R1]), sb("G", [P, B, R1]), sb("gT", [E1 + 1, B])
        gTb, mb1, mb1b = sb("gTb", [E1 + 1, P]), sb("mb1", [P, KF, B]), sb("mb1b", [P, KF])
        hT = w1[:].rearrange("p c f -> p (c f)").rearrange("p (c s) -> p c s", c=KF)
        (w_loaded, stats, stats_ready, rstd_ready, xn_ready, xnT_ps, xTb_ready, xnT_kept, hg_ps, relu_done, hsum_kept,
         gates_ps, gates_ready, chain, mb1_ps, mb1_ready, tw_used, merged_ps, merged, w1b_ready, w2b_ready, xb_ready,
         h_ps, gelu_done, out_ps, x_done, tick) = semaphores(
            nc, ctx, "d", "w_loaded stats stats_ready rstd_ready xn_ready xnT_ps xTb_ready xnT_kept hg_ps relu_done "
            "hsum_kept gates_ps gates_ready chain mb1_ps mb1_ready tw_used merged_ps merged w1b_ready w2b_ready xb_ready "
            "h_ps gelu_done out_ps x_done tick")
        tw_loaded = semaphores(nc, ctx, "d", "tw_loaded0 tw_loaded1 tw_loaded2 tw_loaded3")
        bank = sh.bank
        WEIGHTS = [(gw1, "L1_gw1"), (gb1, "L1_gb1"), (gw2r, "L1_gw2r"), (gb2r, "L1_gb2r"), (gw2a, "L1_gw2a"),
                   (gb2a, "L1_gb2a"), (tb1, "L1_tb1"), (tb2, "L1_tb2"), (w1, "L1_w1"), (w2, "L1_w2")]
        block = ctx.enter_context(nc.Block())

        @block.sync
        def _(sp):
            for dst, name in WEIGHTS:
                sp.dma_start(dst[:], d[name]).then_inc(w_loaded, 16)
            with sp.Fori(0, NCH // 2) as i:
                for k in range(4):
                    sp.wait_ge(tw_used, 4 * i + k + 1)
                    sp.dma_start(tw[k], d["L1_tw1" if k < 2 else "L1_tw2"][:, bass.ds((2 * i + k % 2) * 1024, 1024)])\
                      .then_inc(tw_loaded[k], 16)

        @block.gpsimd
        def _(pool):
            with pool.Fori(0, B) as b:
                layernorm_pool(pool, sh, stats_ready, rstd_ready, b)

        @block.vector
        def _(dve):
            dve.wait_ge(w_loaded, 16 * len(WEIGHTS))
            with dve.Fori(0, B) as b:
                layernorm_vector(dve, sh, lambda t: x_tile(sh, b * TPB + t), xn, stats, stats_ready, rstd_ready, xn_ready, b)
                dve.wait_ge(xTb_ready, b + 1)
                dve.tensor_scalar(xnT[:, :, bass.ds(b * S, S)], xTb, 1.0, None, ALU.mult).then_inc(xnT_kept, 1)
                dve.wait_ge(relu_done, b + 1)
                dve.tensor_scalar(hsums[:, :, bass.ds(b, 1)], hsum[:].unsqueeze(2), 1.0 / S, None, ALU.mult).then_inc(hsum_kept, 1)
            dve.wait_ge(hsum_kept, B)
            dve.tensor_reduce(dup[:], sh.ident[:].rearrange("p (e r) -> p r e", r=R1), AX.X, ALU.add).then_inc(chain, 1)
            dve.wait_ge(gates_ps, 1)
            dve.tensor_scalar(gcol[:], bank[0][:, 0:B], gb2r[:, 0:1], None, ALU.add).then_inc(chain, 1)
            dve.tensor_scalar(gT[:], bank[1][0:E1 + 1, 0:B], gb2a[:, 0:1], None, ALU.add).then_inc(gates_ready, 1)
            dve.wait_ge(chain, 2)
            dve.tensor_tensor(G[:], gcol[:].unsqueeze(2).to_broadcast([P, B, R1]), dup[:].unsqueeze(1).to_broadcast([P, B, R1]),
                              ALU.mult).then_inc(gates_ready, 1)
            dve.wait_ge(mb1_ps, 1)
            dve.tensor_copy(mb1[:].rearrange("p c b -> p (c b)"), bank[2][:, 0:KF * B]).then_inc(mb1_ready, 1)
            dve.sem_inc(merged, 8)
            with dve.Fori(0, NCH // 2) as i:
                for k in range(4):
                    for n in range(2):
                        j = 2 * k + n
                        ch = 2 * i + k % 2
                        if k < 2:
                            cols = bass.ds(ch * FPC * R1, FPC * R1)
                            dst = m1[:, n, :, cols].rearrange("p b (f r) -> p f b r", r=R1)
                            base = w1[:, n, cols].rearrange("p (f r) -> p f r", r=R1)
                        else:
                            cols = bass.ds(ch * R1, R1)
                            dst = m2[:, 4 * n:4 * n + 4, :, cols]
                            base = w2[:, 4 * n:4 * n + 4, cols]
                        dve.wait_ge(merged_ps, 8 * i + j + 1)
                        dve.tensor_tensor(dst, bank[j][:].rearrange("p (f b r) -> p f b r", f=4, b=B),
                                          base.unsqueeze(2).to_broadcast([P, 4, B, R1]), ALU.add).then_inc(merged, 1)
            dve.wait_ge(merged, 8 + 4 * NCH)
            dve.sem_inc(out_ps, 1)
            with dve.Fori(0, B) as b:
                dve.wait_ge(out_ps, b + 1)
                dve.tensor_copy(gTb[:], gT[:, bass.ds(b, 1)].to_broadcast([E1 + 1, P]))
                dve.tensor_copy(mb1b[:], mb1[:, :, bass.ds(b, 1)].rearrange("p c b -> p (c b)")).then_inc(xb_ready, 1)
                dve.tensor_copy(w2b, m2[:, :, bass.ds(b, 1), :].rearrange("p c b d -> p (c b) d")).then_inc(w2b_ready, 1)
                dve.wait_ge(out_ps, b + 2)
                dve.tensor_tensor(x_batch(sh, b), x_batch(sh, b), bank[4][:], ALU.add).then_inc(x_done, 1)

        @block.scalar
        def _(act):
            act.wait_ge(w_loaded, 16 * len(WEIGHTS))
            with act.Fori(0, B) as b:
                act.wait_ge(xnT_ps, b + 1)
                act.activation(xTb, tiles(bank[0][:], KD), ACT.Copy).then_inc(xTb_ready, 1)
                act.wait_ge(hg_ps, b + 1)
                for m in range(KD):
                    ins = act.activation(hrelu[:, m], bank[1][:, m * S:(m + 1) * S], ACT.Relu, bias=gb1[:, m:m + 1],
                                         accum_out=hsum[:, m:m + 1])
                ins.then_inc(relu_done, 1)
            act.wait_ge(merged, 8 + 4 * NCH)
            act.sem_inc(h_ps, 1)
            with act.Fori(0, B) as b:
                act.wait_ge(h_ps, b * (KF // 2) + 1)
                act.sem_inc(tick, 1)
                act.activation(w1b, m1[:, :, bass.ds(b, 1), :].rearrange("p c b d -> p (c b) d"), ACT.Copy).then_inc(w1b_ready, 1)
                act.wait_ge(xb_ready, b + 1)
                for m in range(KF):
                    act.wait_ge(h_ps, b * (KF // 2) + m // 2 + 2)
                    act.activation(hT[:, m], bank[m // 2][:, m % 2 * S:(m % 2 + 1) * S], ACT.Gelu_apprx_tanh,
                                   bias=mb1b[:, m:m + 1]).then_inc(gelu_done, 1)

        @block.tensor
        def _(pe):
            pe.wait_ge(w_loaded, 16 * len(WEIGHTS))
            with pe.Fori(0, B) as b:
                pe.wait_ge(xn_ready, b + 1)
                transpose_batch(pe, sh, bank[0], xn).then_inc(xnT_ps, 1)
                pe.wait_ge(xTb_ready, b + 1)
                for m in range(KD):
                    ins = product(pe, bank[1][:, m * S:(m + 1) * S], [gw1[:, c, m * P:(m + 1) * P] for c in range(KD)],
                                  [xTb[:, c] for c in range(KD)])
                ins.then_inc(hg_ps, 1)
            pe.wait_ge(hsum_kept, B)
            product(pe, bank[0][:, 0:B], [gw2r[:, c] for c in range(KD)], [hsums[:, c] for c in range(KD)])
            product(pe, bank[1][0:E1 + 1, 0:B], [gw2a[:, c] for c in range(KD)], [hsums[:, c] for c in range(KD)]).then_inc(gates_ps, 1)
            pe.wait_ge(gates_ready, 2)
            for m in range(KF):
                ins = pe.matmul(bank[2][:, m * B:(m + 1) * B], tb1[:, m * P:(m + 1) * P], gT[:], start=True, stop=True)
            ins.then_inc(mb1_ps, 1)
            pe.wait_ge(mb1_ready, 1)
            pe.sem_inc(tw_used, 4)
            with pe.Fori(0, NCH // 2) as i:
                for k in range(4):
                    pe.wait_ge(tw_loaded[k], 16 * i + 16)
                    for n in range(2):
                        j = 2 * k + n
                        pe.wait_ge(merged, 8 * i + j + 1)
                        for f in range(4):
                            at = f * D + n * P if k < 2 else (4 * n + f) * P
                            ins = pe.matmul(bank[j][:, f * P:(f + 1) * P], tw[k][:, at:at + P],
                                            G[:].rearrange("p b r -> p (b r)"), start=True, stop=True)
                        ins.then_inc(merged_ps, 1)
                    pe.wait_ge(merged_ps, 8 * i + 2 * k + 2)
                    pe.sem_inc(tw_used, 1)
            pe.wait_ge(merged, 8 + 4 * NCH)
            with pe.Fori(0, B) as b:
                pe.wait_ge(w1b_ready, b + 1)
                for m in range(KF):
                    ins = product(pe, bank[m // 2][:, m % 2 * S:(m % 2 + 1) * S], [w1b[:, c, m * P:(m + 1) * P] for c in range(KD)],
                                  [xnT[:, c, bass.ds(b * S, S)] for c in range(KD)])
                    if m % 2:
                        ins.then_inc(h_ps, 1)
                pe.wait_ge(w2b_ready, b + 1)
                pe.wait_ge(gelu_done, b * KF + KF)
                for t in range(TPB):
                    ins = product(pe, bank[4][:, t * D:(t + 1) * D],
                                  [gTb[:]] + [hT[:, c, t * P:(t + 1) * P] for c in range(KF)], [tb2[:]] + [w2b[:, c] for c in range(KF)])
                ins.then_inc(out_ps, 1)


def stage_l2_attention(nc, sh, d):
    with ExitStack() as ctx:
        def sb(name, shape, dt=F32):
            return ctx.enter_context(nc.sbuf_tensor("e_" + name, shape, dt))

        wq, wk, wv, wg, wo = [sb(n, [P, KD, D]) for n in ("wq", "wk", "wv", "wg", "wo")]
        bq, bk, bg, bgn = [sb(n, [P, KD]) for n in ("bq", "bk", "bg", "bgn")]
        bv, bo = sb("bv", [P, D]), sb("bo", [P, D])
        ctxT = sb("ctxT", [P, KD, S])
        xn, v, probs, xo = [sb(n, [P, TPB, D]) for n in ("xn", "v", "probs", "xo")]
        xnT, qT, kT, gate, probsT, att = [sb(n, [P, KD, S]) for n in ("xnT", "qT", "kT", "gate", "probsT", "att")]
        negmax, sums, rsums = sb("negmax", [P, TPB]), sb("sums", [P, TPB]), sb("rsums", [P, TPB])
        (w_loaded, ctx_loaded, ctx_used, stats, stats_ready, rstd_ready, xn_ready, xnT_ps, xnT_ready, k_ps, v_ps, q_ps,
         g_ps, k_ready, v_ready, q_ready, gate_exp, step, gate_ready, s_ps, max_ready, exp_ready, probs_ready, probsT_ps,
         probsT_ready, att_ps, att_ready, out_ps, out_read, bias_ready) = semaphores(
            nc, ctx, "e", "w_loaded ctx_loaded ctx_used stats stats_ready rstd_ready xn_ready xnT_ps xnT_ready k_ps v_ps "
            "q_ps g_ps k_ready v_ready q_ready gate_exp step gate_ready s_ps max_ready exp_ready probs_ready probsT_ps "
            "probsT_ready att_ps att_ready out_ps out_read bias_ready")
        xnT_p, k_p, v_p, q_p, g_p, s_p, probsT_p, att_p = sh.bank
        out_p = xnT_p
        WEIGHTS = [(wq, "L2_wq"), (wk, "L2_wk"), (wv, "L2_wv"), (wg, "L2_wg"), (wo, "L2_wo"), (bq, "L2_bq"),
                   (bk, "L2_bk"), (bg, "L2_bg"), (bv, "L2_bv"), (bo, "L2_bo")]
        block = ctx.enter_context(nc.Block())

        @block.sync
        def _(sp):
            for dst, name in WEIGHTS:
                sp.dma_start(dst[:], d[name]).then_inc(w_loaded, 16)
            with sp.Fori(0, B) as b:
                sp.wait_ge(ctx_used, b + 1)
                sp.dma_start(ctxT[:], d["ctxT"][:, bass.ds(b * KD, KD), :]).then_inc(ctx_loaded, 16)

        @block.gpsimd
        def _(pool):
            with pool.Fori(0, B) as b:
                layernorm_pool(pool, sh, stats_ready, rstd_ready, b)

        @block.vector
        def _(dve):
            dve.wait_ge(w_loaded, 16 * len(WEIGHTS))
            dve.tensor_scalar(bgn[:], bg[:], -1.0, None, ALU.mult).then_inc(bias_ready, 1)
            with dve.Fori(0, B) as b:
                layernorm_vector(dve, sh, lambda t: x_tile(sh, b * TPB + t), xn, stats, stats_ready, rstd_ready, xn_ready, b)
                dve.wait_ge(v_ps, b + 1)
                dve.tensor_tensor(v[:], tiles(v_p[:]), over_tiles(bv[:]), ALU.add).then_inc(v_ready, 1)
                dve.wait_ge(s_ps, b + 1)
                dve.tensor_reduce(negmax[:], tiles(s_p[:]), AX.X, ALU.max, negate=True).then_inc(max_ready, 1)
                dve.wait_ge(gate_exp, b + 1)
                dve.tensor_scalar(gate[:], gate[:], 1.0, None, ALU.add).then_inc(step, 1)
                dve.wait_ge(step, 2 * b + 1)
                dve.reciprocal(gate[:], gate[:]).then_inc(gate_ready, 1)
                dve.wait_ge(exp_ready, b * TPB + TPB)
                dve.reciprocal(rsums[:], sums[:]).then_inc(step, 1)
                dve.wait_ge(step, 2 * b + 2)
                for t in range(TPB):
                    dve.tensor_scalar(probs[:, t], probs[:, t], rsums[:, t:t + 1], None, ALU.mult).then_inc(probs_ready, 1)
                dve.wait_ge(att_ps, b + 1)
                dve.wait_ge(gate_ready, b + 1)
                dve.tensor_tensor(att[:], tiles(att_p[:], KD), gate[:], ALU.mult).then_inc(att_ready, 1)
                dve.wait_ge(out_ps, b + 1)
                dve.tensor_tensor(xo[:], tiles(out_p[:]), over_tiles(bo[:]), ALU.add).then_inc(out_read, 1)
                dve.wait_ge(out_read, b + 1)
                dve.tensor_tensor(x_batch(sh, b), x_batch(sh, b), xo[:].rearrange("p t d -> p (t d)"), ALU.add)

        @block.scalar
        def _(act):
            act.wait_ge(bias_ready, 1)
            with act.Fori(0, B) as b:
                act.wait_ge(k_ps, b + 1)
                for m in range(KD):
                    ins = act.activation(kT[:, m], k_p[:, m * S:(m + 1) * S], ACT.Identity, bias=bk[:, m:m + 1])
                ins.then_inc(k_ready, 1)
                act.wait_ge(xnT_ps, b + 1)
                act.activation(xnT[:].rearrange("p c s -> p (c s)"), xnT_p[:], ACT.Copy).then_inc(xnT_ready, 1)
                act.wait_ge(q_ps, b + 1)
                for m in range(KD):
                    ins = act.activation(qT[:, m], q_p[:, m * S:(m + 1) * S], ACT.Identity, bias=bq[:, m:m + 1])
                ins.then_inc(q_ready, 1)
                act.wait_ge(g_ps, b + 1)
                for m in range(KD):
                    ins = act.activation(gate[:, m], g_p[:, m * S:(m + 1) * S], ACT.Exp, bias=bgn[:, m:m + 1], scale=-1.0)
                ins.then_inc(gate_exp, 1)
                act.wait_ge(max_ready, b + 1)
                for t in range(TPB):
                    act.activation(probs[:, t], s_p[:, t * S:(t + 1) * S], ACT.Exp, bias=negmax[:, t:t + 1],
                                   accum_out=sums[:, t:t + 1]).then_inc(exp_ready, 1)
                act.wait_ge(probsT_ps, b + 1)
                act.activation(probsT[:].rearrange("p c s -> p (c s)"), probsT_p[:], ACT.Copy).then_inc(probsT_ready, 1)

        @block.tensor
        def _(pe):
            pe.sem_inc(ctx_used, 1)
            pe.wait_ge(w_loaded, 16 * len(WEIGHTS))

            def turned(out, w, src):
                for m in range(KD):
                    ins = product(pe, out[:, m * S:(m + 1) * S], [w[:, c, m * P:(m + 1) * P] for c in range(KD)],
                                  [src[:, c] for c in range(KD)])
                return ins

            with pe.Fori(0, B) as b:
                pe.wait_ge(ctx_loaded, b * 16 + 16)
                pe.wait_ge(xn_ready, b + 1)
                transpose_batch(pe, sh, xnT_p, xn).then_inc(xnT_ps, 1)
                turned(k_p, wk, ctxT).then_inc(k_ps, 1)
                for t in range(TPB):
                    ins = product(pe, v_p[:, t * D:(t + 1) * D], [ctxT[:, c, t * P:(t + 1) * P] for c in range(KD)],
                                  [wv[:, c] for c in range(KD)])
                ins.then_inc(v_ps, 1)
                pe.wait_ge(v_ps, b + 1)
                pe.sem_inc(ctx_used, 1)
                pe.wait_ge(xnT_ready, b + 1)
                turned(q_p, wq, xnT).then_inc(q_ps, 1)
                turned(g_p, wg, xnT).then_inc(g_ps, 1)
                pe.wait_ge(k_ready, b + 1)
                pe.wait_ge(q_ready, b + 1)
                for t in range(TPB):
                    ins = product(pe, s_p[:, t * S:(t + 1) * S], [qT[:, c, t * P:(t + 1) * P] for c in range(KD)],
                                  [kT[:, c] for c in range(KD)])
                ins.then_inc(s_ps, 1)
                pe.wait_ge(probs_ready, b * TPB + TPB)
                transpose_batch(pe, sh, probsT_p, probs).then_inc(probsT_ps, 1)
                pe.wait_ge(v_ready, b + 1)
                pe.wait_ge(probsT_ready, b + 1)
                turned(att_p, v, probsT).then_inc(att_ps, 1)
                pe.wait_ge(att_ready, b + 1)
                for t in range(TPB):
                    ins = product(pe, out_p[:, t * D:(t + 1) * D], [att[:, c, t * P:(t + 1) * P] for c in range(KD)],
                                  [wo[:, c] for c in range(KD)])
                ins.then_inc(out_ps, 1)


def stage_l3_attention(nc, sh, d):
    with ExitStack() as ctx:
        def sb(name, shape, dt=F32):
            return ctx.enter_context(nc.sbuf_tensor("g_" + name, shape, dt))

        wl = sb("wl", [P, 4 * KD, D])
        wcq, wc, wqv = sb("wcq", [P, KD]), sb("wc", [P, KD]), sb("wqv", [P, KD])
        b3, bsum, bl = sb("b3", [P, 3]), sb("bsum", [P, 1]), sb("bl", [P, D])
        ctxT, cx = sb("ctxT", [P, KD, S]), sb("cx", [P, TPB, D])
        xn, probs, xo = [sb(n, [P, TPB, D]) for n in ("xn", "probs", "xo")]
        xnT, lq, probsT, c2qT, cc, cq = [sb(n, [P, KD, S]) for n in ("xnT", "lq", "probsT", "c2qT", "cc", "cq")]
        negmax, sums, rsums, smax = [sb(n, [P, TPB]) for n in ("negmax", "sums", "rsums", "smax")]
        row, rmax, rsum, bcol, q2c = sb("row", [1, S]), sb("rmax", [1, 1]), sb("rsum", [1, 1]), sb("bcol", [P, TPB]), sb("q2c", [P, KD])
        (w_loaded, ctx_loaded, ctx_used, stats, stats_ready, rstd_ready, xn_ready, xnT_ps, xnT_ready, lq_ready, s_ps,
         max_ready, exp_ready, sums_ready, probs_ready, probsT_ps, probsT_ready, c2q_ps, c2q_ready, cc_ready, smax_ready,
         row_ps, rmax_ready, row_exp, rsum_ready, row_ready, bcol_ps, bcol_ready, q2c_ps, q2c_ready, cq_ready, out_ps,
         out_read, bias_ready) = semaphores(
            nc, ctx, "g", "w_loaded ctx_loaded ctx_used stats stats_ready rstd_ready xn_ready xnT_ps xnT_ready lq_ready "
            "s_ps max_ready exp_ready sums_ready probs_ready probsT_ps probsT_ready c2q_ps c2q_ready cc_ready smax_ready "
            "row_ps rmax_ready row_exp rsum_ready row_ready bcol_ps bcol_ready q2c_ps q2c_ready cq_ready out_ps out_read "
            "bias_ready")
        xnT_p, s_p, r_p, probsT_p, c2q_p, row_p, col_p, out_p = sh.bank

        def c2q2(p):
            return p[:, 4:4 + KD]

        WEIGHTS = [(wl, "L3_wl"), (wcq, "L3_wcq"), (wc, "L3_wc"), (wqv, "L3_wqv"), (b3, "L3_b3"), (bl, "L3_bl")]
        block = ctx.enter_context(nc.Block())

        @block.sync
        def _(sp):
            for dst, name in WEIGHTS:
                sp.dma_start(dst[:], d[name]).then_inc(w_loaded, 16)
            with sp.Fori(0, B) as b:
                sp.wait_ge(ctx_used, b + 1)
                sp.dma_start(ctxT[:], d["ctxT"][:, bass.ds(b * KD, KD), :]).then_inc(ctx_loaded, 16)
                sp.dma_start(cx[:], d["ctx"][:, bass.ds(b * TPB, TPB), :]).then_inc(ctx_loaded, 16)

        @block.gpsimd
        def _(pool):
            with pool.Fori(0, B) as b:
                layernorm_pool(pool, sh, stats_ready, rstd_ready, b)

        @block.vector
        def _(dve):
            dve.wait_ge(w_loaded, 16 * len(WEIGHTS))
            dve.tensor_reduce(bsum[:], b3[:], AX.X, ALU.add).then_inc(bias_ready, 1)
            dve.wait_ge(bias_ready, 1)
            with dve.Fori(0, B) as b:
                layernorm_vector(dve, sh, lambda t: x_tile(sh, b * TPB + t), xn, stats, stats_ready, rstd_ready, xn_ready, b)
                dve.wait_ge(xnT_ready, b + 1)
                for c in range(KD):
                    ins = dve.tensor_scalar(lq[:, c], xnT[:, c], wcq[:, c:c + 1], wqv[:, c:c + 1], ALU.mult, ALU.add)
                ins.then_inc(lq_ready, 1)
                dve.wait_ge(s_ps, b + 1)
                dve.tensor_reduce(negmax[:], tiles(s_p[:]), AX.X, ALU.max, negate=True).then_inc(max_ready, 1)
                dve.wait_ge(max_ready, b + 1)
                dve.scalar_tensor_tensor(smax[:], r_p[:, 0:TPB], bsum[:, 0:1], negmax[:], ALU.add, ALU.subtract).then_inc(smax_ready, 1)
                dve.wait_ge(exp_ready, b + 1)
                dve.reciprocal(rsums[:], sums[:]).then_inc(sums_ready, 1)
                dve.wait_ge(sums_ready, b + 1)
                for t in range(TPB):
                    ins = dve.tensor_scalar(probs[:, t], probs[:, t], rsums[:, t:t + 1], None, ALU.mult)
                ins.then_inc(probs_ready, 1)
                dve.wait_ge(row_ps, b + 1)
                dve.tensor_reduce(rmax[:], row_p[0:1, 0:S], AX.X, ALU.max, negate=True).then_inc(rmax_ready, 1)
                dve.wait_ge(row_exp, b + 1)
                dve.reciprocal(rsum[:], rsum[:]).then_inc(rsum_ready, 1)
                dve.wait_ge(rsum_ready, b + 1)
                dve.tensor_scalar(row[:], row[:], rsum[0:1, 0:1], None, ALU.mult).then_inc(row_ready, 1)
                dve.wait_ge(bcol_ps, b + 1)
                dve.tensor_scalar(bcol[:], col_p[:, 0:TPB], 1.0, None, ALU.mult).then_inc(bcol_ready, 1)
                dve.wait_ge(c2q_ready, b + 1)
                dve.tensor_tensor(cc[:], xnT[:], c2qT[:], ALU.mult).then_inc(cc_ready, 1)
                dve.wait_ge(q2c_ps, b + 1)
                dve.tensor_scalar(q2c[:], c2q2(col_p), 1.0, None, ALU.mult).then_inc(q2c_ready, 1)
                dve.wait_ge(q2c_ready, b + 1)
                for c in range(KD):
                    ins = dve.tensor_scalar(cq[:, c], xnT[:, c], q2c[:, c:c + 1], None, ALU.mult)
                ins.then_inc(cq_ready, 1)
                dve.wait_ge(out_ps, b + 1)
                dve.tensor_tensor(xo[:], tiles(out_p[:]), over_tiles(bl[:]), ALU.add).then_inc(out_read, 1)
                dve.wait_ge(out_read, b + 1)
                dve.tensor_tensor(x_batch(sh, b), x_batch(sh, b), xo[:].rearrange("p t d -> p (t d)"), ALU.add)

        @block.scalar
        def _(act):
            with act.Fori(0, B) as b:
                act.wait_ge(xnT_ps, b + 1)
                act.activation(xnT[:].rearrange("p c s -> p (c s)"), xnT_p[:], ACT.Copy).then_inc(xnT_ready, 1)
                act.wait_ge(max_ready, b + 1)
                for t in range(TPB):
                    ins = act.activation(probs[:, t], s_p[:, t * S:(t + 1) * S], ACT.Exp, bias=negmax[:, t:t + 1],
                                         accum_out=sums[:, t:t + 1])
                ins.then_inc(exp_ready, 1)
                act.wait_ge(rmax_ready, b + 1)
                act.activation(row[:], row_p[0:1, 0:S], ACT.Exp, bias=rmax[0:1, 0:1], accum_out=rsum[:]).then_inc(row_exp, 1)
                act.wait_ge(probsT_ps, b + 1)
                act.activation(probsT[:].rearrange("p c s -> p (c s)"), probsT_p[:], ACT.Copy).then_inc(probsT_ready, 1)
                act.wait_ge(c2q_ps, b + 1)
                act.activation(c2qT[:].rearrange("p c s -> p (c s)"), c2q_p[:], ACT.Copy).then_inc(c2q_ready, 1)

        @block.tensor
        def _(pe):
            pe.sem_inc(ctx_used, 1)
            pe.wait_ge(w_loaded, 16 * len(WEIGHTS))
            with pe.Fori(0, B) as b:
                pe.wait_ge(xn_ready, b + 1)
                transpose_batch(pe, sh, xnT_p, xn).then_inc(xnT_ps, 1)
                pe.wait_ge(xnT_ready, b + 1)
                for t in range(TPB):
                    product(pe, r_p[:, t:t + 1], [xnT[:, c, t * P:(t + 1) * P] for c in range(KD)], [wc[:, c:c + 1] for c in range(KD)])
                pe.wait_ge(ctx_loaded, b * 32 + 32)
                pe.wait_ge(lq_ready, b + 1)
                for t in range(TPB):
                    ins = product(pe, s_p[:, t * S:(t + 1) * S], [lq[:, c, t * P:(t + 1) * P] for c in range(KD)],
                                  [ctxT[:, c] for c in range(KD)])
                ins.then_inc(s_ps, 1)
                pe.wait_ge(smax_ready, b + 1)
                for t in range(TPB):
                    ins = pe.matmul(row_p[0:1, t * P:(t + 1) * P], smax[:, t:t + 1], sh.ident[:], start=True, stop=True)
                ins.then_inc(row_ps, 1)
                pe.wait_ge(probs_ready, b + 1)
                transpose_batch(pe, sh, probsT_p, probs).then_inc(probsT_ps, 1)
                pe.wait_ge(row_ready, b + 1)
                for t in range(TPB):
                    ins = pe.matmul(col_p[:, t:t + 1], row[0:1, t * P:(t + 1) * P], sh.ones[0:1, 0:1], start=True, stop=True)
                ins.then_inc(bcol_ps, 1)
                pe.wait_ge(probsT_ready, b + 1)
                for m in range(KD):
                    ins = product(pe, c2q_p[:, m * S:(m + 1) * S], [cx[:, c, m * P:(m + 1) * P] for c in range(TPB)],
                                  [probsT[:, c] for c in range(TPB)])
                ins.then_inc(c2q_ps, 1)
                pe.wait_ge(c2q_ps, b + 1)
                pe.sem_inc(ctx_used, 1)
                pe.wait_ge(bcol_ready, b + 1)
                for m in range(KD):
                    ins = product(pe, c2q2(col_p)[:, m:m + 1], [xn[:, t, m * P:(m + 1) * P] for t in range(TPB)],
                                  [bcol[:, t:t + 1] for t in range(TPB)])
                ins.then_inc(q2c_ps, 1)
                pe.wait_ge(cc_ready, b + 1)
                pe.wait_ge(cq_ready, b + 1)
                for t in range(TPB):
                    tok = slice(t * P, (t + 1) * P)
                    ins = product(pe, out_p[:, t * D:(t + 1) * D],
                                  [src[:, c, tok] for src in (xnT, c2qT, cc, cq) for c in range(KD)], [wl[:, k] for k in range(4 * KD)])
                ins.then_inc(out_ps, 1)


def stage_l2_ffn(nc, sh, d):
    experts(nc, sh, d, "f", "L2", I2, gated=True)


def stage_l3_ffn(nc, sh, d):
    experts(nc, sh, d, "h", "L3", F3, gated=False)


def experts(nc, sh, d, tag, layer, width, gated):
    with ExitStack() as ctx:
        def sb(name, shape, dt=F32):
            return ctx.enter_context(nc.sbuf_tensor(f"{tag}_{name}", shape, dt))

        NC = -(-width // P)
        size = [min(P, width - c * P) for c in range(NC)]
        NIN = 2 if gated else 1
        WCOLS = NIN * KD * width + NC * D + (0 if gated else NC)
        BLK, NB = 512, TOK // 512
        wbuf = [sb(f"w{k}", [P, WCOLS]) for k in range(2)]

        def w_in(k, m):
            return wbuf[k][:, m * KD * width:(m + 1) * KD * width].rearrange("p (c f) -> p c f", c=KD)

        def w_out(k):
            return wbuf[k][:, NIN * KD * width:NIN * KD * width + NC * D].rearrange("p (c f) -> p c f", c=NC)

        def bias_in(k, c):
            at = NIN * KD * width + NC * D + c
            return wbuf[k][:, at:at + 1]

        wr, small = sb("wr", [P, KD, NE]), sb("small", [P, NE])
        nw, b2 = sb("nw", [P, KD]), sb("b2", [NE, D])
        iota_i, iota = sb("iota_i", [P, NE], I32), sb("iota", [P, NE])
        xn, square = sb("xn", [P, TPB, D]), sb("square", [P, TPB, D])
        ms, rms = sb("ms", [P, TPB]), sb("rms", [P, TPB])
        xnT = sb("xnT", [P, KD, TOK])
        hT = sb("hT", [P, 2, NC, BLK])
        act_out = sb("act_out", [P, 2, BLK])
        logits, top, topi, topf = sb("logits", [P, NT, NE]), sb("top", [P, NT, 8]), sb("topi", [P, NT, 8], U32), sb("topf", [P, NT, 8])
        dl, rw1, rw2 = sb("dl", [P, NT]), sb("rw1", [P, NT]), sb("rw2", [P, NT])
        wt1, wt2, wts, wcol = sb("wt1", [P, NT, NE]), sb("wt2", [P, NT, NE]), sb("wts", [P, NT, NE]), sb("wcol", [P, 2, NT])
        wtsT = sb("wtsT", [NE, TOK])
        (s_loaded, stats, stats_ready, rstd_ready, xn_ready, ms_ready, rms_ready, t_ready, xnT_ps, xnT_kept, logits_ps,
         iota_ready, step, top_ready, exp_ready, wts_ready, wcol_ready, act_ready, h_done, in_ps, down_ps, acc_done,
         wtsT_ps, wtsT_ready, bias_ps) = semaphores(
            nc, ctx, tag, "s_loaded stats stats_ready rstd_ready xn_ready ms_ready rms_ready t_ready xnT_ps xnT_kept "
            "logits_ps iota_ready step top_ready exp_ready wts_ready wcol_ready act_ready h_done in_ps down_ps acc_done "
            "wtsT_ps wtsT_ready bias_ps")
        w_loaded = semaphores(nc, ctx, tag, "w_loaded0 w_loaded1")
        bank = sh.bank
        in_p = [[bank[0], bank[2]], [bank[1], bank[3]]]
        down_p = [bank[4], bank[5], bank[6], bank[7]]
        SMALL = [(wr, layer + "_wr"), (small, layer + "_small")] + ([] if gated else [(nw, layer + "_nw"), (b2, layer + "_b2")])
        n_step_bias = 9
        STEPS = 2 * NB
        block = ctx.enter_context(nc.Block())

        @block.sync
        def _(sp):
            for dst, name in SMALL:
                sp.dma_start(dst[:], d[name]).then_inc(s_loaded, 16)
            for k in range(2):
                sp.dma_start(wbuf[k][:], d[layer + "_w"][:, k]).then_inc(w_loaded[k], 16)
            with sp.Fori(0, NE // 2 - 1) as i:
                for k in range(2):
                    sp.wait_ge(down_ps, 2 * (STEPS * i + (k + 1) * NB))
                    sp.dma_start(wbuf[k][:], d[layer + "_w"][:, bass.ds(2 * i + 2 + k, 1), :].rearrange("p e w -> p (e w)"))\
                      .then_inc(w_loaded[k], 16)

        @block.gpsimd
        def _(pool):
            pool.iota(iota_i[:], [[1, NE]], base=0, channel_multiplier=0).then_inc(iota_ready, 1)
            with pool.Fori(0, B) as b:
                layernorm_pool(pool, sh, stats_ready, rstd_ready, b)
                if not gated:
                    pool.wait_ge(ms_ready, b + 1)
                    pool.tensor_tensor(rms[:], ms[:], sh.minus_half[:], ALU.pow).then_inc(rms_ready, 1)

        @block.vector
        def _(dve):
            dve.wait_ge(s_loaded, 16 * len(SMALL))
            with dve.Fori(0, B) as b:
                layernorm_vector(dve, sh, lambda t: x_tile(sh, b * TPB + t), xn, stats, stats_ready, rstd_ready, xn_ready, b)
                if not gated:
                    dve.wait_ge(xn_ready, b + 1)
                    dve.tensor_tensor(x_batch(sh, b), x_batch(sh, b), xn[:].rearrange("p t d -> p (t d)"), ALU.add)
                    dve.wait_ge(t_ready, 2 * b + 1)
                    dve.tensor_scalar(ms[:], ms[:], 1.0 / D, RMS_EPS, ALU.mult, ALU.add).then_inc(ms_ready, 1)
                    dve.wait_ge(rms_ready, b + 1)
                    for t in range(TPB):
                        ins = dve.tensor_scalar(xn[:, t], xn[:, t], rms[:, t:t + 1], None, ALU.mult)
                    ins.then_inc(t_ready, 1)
                dve.wait_ge(xnT_ps, b + 1)
                for c in range(KD):
                    ins = dve.tensor_scalar(xnT[:, c, bass.ds(b * S, S)], bank[0][:, c * S:(c + 1) * S],
                                            1.0 if gated else nw[:, c:c + 1], None, ALU.mult)
                ins.then_inc(xnT_kept, 1)
            n_step = [0]

            def link(ins):
                n_step[0] += 1
                ins.then_inc(step, 1)
                dve.wait_ge(step, n_step[0])

            dve.wait_ge(iota_ready, 1)
            dve.tensor_copy(iota[:], iota_i[:])
            dve.wait_ge(logits_ps, 1)
            link(dve.tensor_tensor(logits[:], bank[1][:, 0:NT * NE].rearrange("p (t e) -> p t e", e=NE),
                                   small[:].unsqueeze(1).to_broadcast([P, NT, NE]), ALU.add))
            for t in range(NT):
                ins = dve.max(top[:, t], logits[:, t])
            link(ins)
            for t in range(NT):
                ins = dve.max_index(topi[:, t], top[:, t], logits[:, t])
            link(ins)
            dve.tensor_copy(topf[:], topi[:])
            dve.tensor_tensor(dl[:], top[:, :, 1], top[:, :, 0], ALU.subtract).then_inc(top_ready, 1)
            dve.wait_ge(exp_ready, 1)
            link(dve.tensor_scalar(rw1[:], rw2[:], 1.0, None, ALU.add))
            link(dve.reciprocal(rw1[:], rw1[:]))
            link(dve.tensor_tensor(rw2[:], rw2[:], rw1[:], ALU.mult))
            over_e = lambda ap: ap.to_broadcast([P, NT, NE])
            iota_t = iota[:].unsqueeze(1).to_broadcast([P, NT, NE])
            dve.tensor_tensor(wt1[:], iota_t, over_e(topf[:, :, 0:1]), ALU.is_equal)
            link(dve.tensor_tensor(wt2[:], iota_t, over_e(topf[:, :, 1:2]), ALU.is_equal))
            dve.tensor_tensor(wt1[:], wt1[:], over_e(rw1[:].unsqueeze(2)), ALU.mult)
            link(dve.tensor_tensor(wt2[:], wt2[:], over_e(rw2[:].unsqueeze(2)), ALU.mult))
            link(dve.tensor_tensor(wts[:], wt1[:], wt2[:], ALU.add))
            if gated:
                link(dve.memset(wts[:, :, NE - 1:NE], 1.0))
            dve.tensor_scalar(wt1[:], wts[:], 1.0, None, ALU.mult).then_inc(wts_ready, 1)
            if not gated:
                for n in range(NT // 4):
                    dve.wait_ge(wtsT_ps, n + 1)
                    dve.tensor_copy(wtsT[:, n * 512:(n + 1) * 512], bank[4 + n][0:NE, :]).then_inc(wtsT_ready, 1)
                for n in range(NT // 2):
                    dve.wait_ge(bias_ps, n + 1)
                    link(dve.tensor_tensor(sh.X[:, n * 512:(n + 1) * 512], sh.X[:, n * 512:(n + 1) * 512], bank[n % 4][:], ALU.add))

            dve.wait_ge(wts_ready, 1)
            dve.sem_inc(acc_done, 4)
            if gated:
                dve.sem_inc(h_done, 2)
            with dve.Fori(0, NE // 2) as i:
                def accumulate(s, half):
                    a = 2 * s + half
                    dve.wait_ge(down_ps, 2 * STEPS * i + a + 1)
                    dve.wait_ge(acc_done, 2 * STEPS * i + a + 4)
                    for q in range(2):
                        tile = s % NB * 4 + 2 * half + q
                        xt = sh.X[:, tile * D:(tile + 1) * D]
                        ins = dve.scalar_tensor_tensor(xt, down_p[a % 4][:, q * D:(q + 1) * D], wcol[:, s // NB, tile:tile + 1],
                                                       xt, ALU.mult, ALU.add)
                    ins.then_inc(acc_done, 1)

                for s in range(STEPS):
                    if s % NB == 0:
                        dve.tensor_copy(wcol[:, s // NB], wts[:, :, bass.ds(2 * i + s // NB, 1)].rearrange("p t e -> p (t e)"))\
                           .then_inc(wcol_ready, 1)
                        dve.wait_ge(wcol_ready, 2 * i + s // NB + 1)
                    if gated:
                        for c in range(NC):
                            j = s * NC + c
                            dve.wait_ge(act_ready, STEPS * NC * i + j + 1)
                            if c == 0 and s >= 2:
                                dve.wait_ge(down_ps, 2 * STEPS * i + 2 * (s - 1))
                            dve.tensor_tensor(hT[0:size[c], s % 2, c], in_p[c % 2][1][0:size[c], :], act_out[0:size[c], c % 2],
                                              ALU.mult).then_inc(h_done, 1)
                            if s >= 1 and c in (2, 3):
                                accumulate(s - 1, c - 2)
                    elif s >= 1:
                        accumulate(s - 1, 0)
                        accumulate(s - 1, 1)
                accumulate(STEPS - 1, 0)
                accumulate(STEPS - 1, 1)
            dve.wait_ge(acc_done, 4 + NE * NB * 2)

        @block.scalar
        def _(act):
            if not gated:
                with act.Fori(0, B) as b:
                    act.wait_ge(xn_ready, b + 1)
                    for t in range(TPB):
                        ins = act.activation(square[:, t], xn[:, t], ACT.Square, accum_out=ms[:, t:t + 1])
                    ins.then_inc(t_ready, 1)
            act.wait_ge(top_ready, 1)
            act.activation(rw2[:], dl[:], ACT.Exp).then_inc(exp_ready, 1)
            if not gated:
                act.sem_inc(h_done, 2)
            with act.Fori(0, NE // 2) as i:
                for s in range(STEPS):
                    for c in range(NC):
                        j = s * NC + c
                        act.wait_ge(in_ps, STEPS * NC * i + j + 1)
                        if gated:
                            act.wait_ge(h_done, STEPS * NC * i + j + 1)
                            act.activation(act_out[0:size[c], c % 2], in_p[c % 2][0][0:size[c], :], ACT.Silu).then_inc(act_ready, 1)
                        else:
                            if c == 0 and s >= 2:
                                act.wait_ge(down_ps, 2 * STEPS * i + 2 * (s - 1))
                            act.activation(hT[:, s % 2, c], in_p[c % 2][0][:], ACT.Gelu, bias=bias_in(s // NB, c)).then_inc(h_done, 1)

        @block.tensor
        def _(pe):
            pe.wait_ge(s_loaded, 16 * len(SMALL))
            with pe.Fori(0, B) as b:
                pe.wait_ge(xn_ready if gated else t_ready, b + 1 if gated else 2 * b + 2)
                transpose_batch(pe, sh, bank[0], xn).then_inc(xnT_ps, 1)
            pe.wait_ge(xnT_kept, B)
            for t in range(NT):
                ins = product(pe, bank[1][:, t * NE:(t + 1) * NE], [xnT[:, c, t * P:(t + 1) * P] for c in range(KD)],
                              [wr[:, c] for c in range(KD)])
            ins.then_inc(logits_ps, 1)
            pe.wait_ge(wts_ready, 1)
            if not gated:
                for n in range(NT // 4):
                    for q in range(4):
                        ins = pe.transpose(bank[4 + n][0:NE, q * P:(q + 1) * P], wts[:, 4 * n + q], sh.ident[:])
                    ins.then_inc(wtsT_ps, 1)
                pe.wait_ge(wtsT_ready, NT // 4)
                for n in range(NT // 2):
                    if n >= 4:
                        pe.wait_ge(step, n_step_bias + n - 3)
                    for q in range(2):
                        t = 2 * n + q
                        ins = pe.matmul(bank[n % 4][:, q * D:(q + 1) * D], wtsT[:, t * P:(t + 1) * P], b2[:], start=True, stop=True)
                    ins.then_inc(bias_ps, 1)
                pe.wait_ge(step, n_step_bias + NT // 2)
            with pe.Fori(0, NE // 2) as i:
                def down(s):
                    pe.wait_ge(h_done, STEPS * NC * i + (s + 1) * NC + 2)
                    for half in range(2):
                        a = 2 * s + half
                        pe.wait_ge(acc_done, 2 * STEPS * i + a + 1)
                        for q in range(2):
                            tok = slice((2 * half + q) * P, (2 * half + q + 1) * P)
                            ins = product(pe, down_p[a % 4][:, q * D:(q + 1) * D], [hT[0:size[c], s % 2, c, tok] for c in range(NC)],
                                          [w_out(s // NB)[0:size[c], c] for c in range(NC)])
                        ins.then_inc(down_ps, 1)

                for s in range(STEPS):
                    if s % NB == 0:
                        pe.wait_ge(w_loaded[s // NB], 16 * i + 16)
                    for c in range(NC):
                        j = s * NC + c
                        pe.wait_ge(h_done, STEPS * NC * i + j + 1)
                        for m in range(NIN):
                            ins = product(pe, in_p[c % 2][m][0:size[c], :],
                                          [w_in(s // NB, m)[:, k, c * P:c * P + size[c]] for k in range(KD)],
                                          [xnT[:, k, s % NB * BLK:(s % NB + 1) * BLK] for k in range(KD)])
                        ins.then_inc(in_ps, 1)
                        if c == 1 and s >= 1:
                            down(s - 1)
                down(STEPS - 1)

STAGES = [stage_l0_attention, stage_l0_ffn, stage_l1_attention, stage_l1_ffn,
          stage_l2_attention, stage_l2_ffn, stage_l3_attention, stage_l3_ffn]


def program(nc, d, out, n_stages=99):
    with ExitStack() as ctx:
        def sb(name, shape, dt=F32):
            return ctx.enter_context(nc.sbuf_tensor(name, shape, dt))

        sh = Shared()
        sh.X = sb("X", [P, NT * D])
        sh.ident, sh.ident16 = sb("ident", [P, P]), sb("ident16", [P, P], BF16)
        sh.ones, sh.minus_half = sb("ones", [P, P]), sb("minus_half", [P, TPB])
        sh.bn6, sh.mv = sb("bn6", [P, TPB, 6]), sb("mv", [P, TPB, 2])
        sh.var, sh.rstd = sb("var", [P, TPB]), sb("rstd", [P, TPB])
        sh.bank = [ctx.enter_context(nc.psum_tensor(f"bank{i}", [P, 512], F32)) for i in range(8)]
        stage_start(nc, sh, d)
        for stage in STAGES[:n_stages]:
            stage(nc, sh, d)
        stored = ctx.enter_context(nc.semaphore("stored"))
        block = ctx.enter_context(nc.Block())

        @block.sync
        def _(sp):
            sp.dma_start(out, tiles(sh.X[:], NT)).then_inc(stored, 16)
            sp.wait_ge(stored, 16)


def laid_out(inputs):
    import numpy as np

    g = {k: np.asarray(v) for k, v in inputs.items()}

    def rows(w, n=None):
        k, n = w.shape
        return np.ascontiguousarray(w.reshape(k // P, P, n).transpose(1, 0, 2))

    def column(v):
        return np.ascontiguousarray(v.reshape(-1, P).T)

    def everywhere(v):
        return np.ascontiguousarray(np.broadcast_to(v.reshape(1, -1), (P, v.size)))

    def tokens(a):
        return rows(a.reshape(TOK, -1))

    def heads(w):
        out = np.zeros(w.shape[:-1] + (H, PAD0), w.dtype)
        out[..., :DK0] = w.reshape(w.shape[:-1] + (H, DK0))
        return out.reshape(w.shape[:-1] + (H * PAD0,))

    a = {}
    a["x"] = tokens(g["x"])
    a["ctx"] = tokens(g["ctx_1024"])
    a["ctxT"] = np.ascontiguousarray(g["ctx_1024"].reshape(B, S, KD, P).transpose(3, 0, 2, 1).reshape(P, B * KD, S))
    a["mask"] = tokens(g["mask_BxSxS2_ik1"])
    p = "L0_xattn_"
    a["L0_wq"], a["L0_wk"] = rows(heads(g[p + "Wq"])), rows(heads(g[p + "Wk"]))
    a["L0_bq"], a["L0_bk"] = column(heads(g[p + "bq"])), column(heads(g[p + "bk"]))
    a["L0_wv"], a["L0_wo"] = rows(g[p + "Wv"]), rows(g[p + "Wo"])
    a["L0_bv"], a["L0_bo"] = everywhere(g[p + "bv"]), everywhere(g[p + "bo"])
    p = "L0_ffn_"
    a["L0_w1"], a["L0_w2"] = rows(g[p + "W1"].T).reshape(P, -1), rows(g[p + "W2"].T).reshape(P, -1)
    a["L0_b1"], a["L0_b2"] = everywhere(g[p + "b1"]), everywhere(g[p + "b2"])
    p = "L1_xattn_"
    a["L1_wq"], a["L1_wk"], a["L1_wv"] = rows(g[p + "Wq"]), rows(g[p + "Wkv"][:, :INNER1]), rows(g[p + "Wkv"][:, INNER1:])
    a["L1_wm"], a["L1_wo"], a["L1_bo"] = rows(g[p + "Wm"]), rows(g[p + "Wo"]), everywhere(g[p + "bo"])
    a["L1_g"], a["L1_b"] = column(g[p + "ln_g"]), column(g[p + "ln_b"])
    p = "L1_ffn_"
    a["L1_gw1"], a["L1_gb1"] = rows(g[p + "gate_w1"].T), column(g[p + "gate_b1"])
    gw2T = g[p + "gate_w2"].T
    a["L1_gw2r"] = rows(np.repeat(gw2T, R1, axis=1))
    a["L1_gb2r"] = np.repeat(g[p + "gate_b2"], R1).reshape(P, 1)
    a["L1_gw2a"] = rows(np.concatenate([gw2T, np.zeros((D, 1), gw2T.dtype)], axis=1))
    a["L1_gb2a"] = np.concatenate([g[p + "gate_b2"], np.ones(1, gw2T.dtype)]).reshape(E1 + 1, 1)
    a["L1_tb1"] = np.concatenate([g[p + "Tb1"], g[p + "b1"][None]])
    a["L1_tb2"] = np.concatenate([g[p + "Tb2"], g[p + "b2"][None]])
    a["L1_w1"], a["L1_w2"] = rows(g[p + "W1"].T), rows(g[p + "W2"].T)
    blocks = lambda w: np.ascontiguousarray(w.reshape(E1, -1, R1, w.shape[2]).transpose(0, 2, 1, 3)).reshape(P, -1)
    a["L1_tw1"], a["L1_tw2"] = blocks(g[p + "TW1"]), blocks(g[p + "TW2"])
    p = "L2_xattn_"
    for n in ("q", "k", "v", "g", "o"):
        a["L2_w" + n] = rows(g[p + "W" + n])
        a["L2_b" + n] = everywhere(g[p + "b" + n]) if n in "vo" else column(g[p + "b" + n])
    p = "L2_ffn_"
    wr = np.concatenate([g[p + "wr"].T, np.zeros((D, NE - E2), np.float32)], axis=1)
    a["L2_wr"] = rows(wr)
    a["L2_small"] = everywhere(np.concatenate([g[p + "rb"], np.full(NE - E2, NEVER, np.float32)]))

    def expert(w_in, w_out, tail=()):
        n = -(-w_out.shape[1] // P) * P
        out = np.zeros((n, D), w_out.dtype)
        out[:w_out.shape[1]] = w_out.T
        return np.concatenate([rows(w.T).reshape(P, -1) for w in w_in] + [rows(out).reshape(P, -1), *tail], axis=1)

    a["L2_w"] = np.stack([expert([g[p + "rg"][e], g[p + "ru"][e]], g[p + "rd"][e]) for e in range(E2)]
                         + [expert([g[p + "sg"], g[p + "su"]], g[p + "sd"])], axis=1)
    p = "L3_xattn_"
    a["L3_wl"], a["L3_bl"] = rows(g[p + "W_l"].T), everywhere(g[p + "b_l"])
    a["L3_wcq"], a["L3_wc"], a["L3_wqv"] = column(g[p + "w_cq"]), column(g[p + "w_c"]), column(g[p + "w_q"])
    a["L3_b3"] = everywhere(np.stack([g[p + "b_c"], g[p + "b_q"], g[p + "b_cq"]]))
    p = "L3_ffn_"
    a["L3_nw"], a["L3_wr"] = column(g[p + "norm_weight"]), rows(g[p + "gate_w"].T)
    a["L3_small"], a["L3_b2"] = np.zeros((P, NE), np.float32), g[p + "b2"]
    a["L3_w"] = np.stack([expert([g[p + "w1"][e]], g[p + "w2"][e], [column(g[p + "b1"][e])]) for e in range(E3)], axis=1)
    return {k: np.ascontiguousarray(v) for k, v in a.items()}


def kernel(**inputs):
    import numpy as np
    import concourse.bacc as bacc
    from concourse.bass_utils import run_bass_kernel_spmd

    nc = bacc.Bacc("TRN2", target_bir_lowering=False, num_devices=1)
    arrays = laid_out(inputs)
    d = {name: nc.dram_tensor("in_" + name, a.shape, mybir.dt.from_np(a.dtype), kind="ExternalInput").ap()
         for name, a in arrays.items()}
    out = nc.dram_tensor("out_x", (P, NT, D), F32, kind="ExternalOutput").ap()
    program(nc, d, out)
    r = run_bass_kernel_spmd(nc, [{"in_" + name: a for name, a in arrays.items()}], core_ids=[0])
    return np.ascontiguousarray(r.results[0]["out_x"].transpose(1, 0, 2)).reshape(B, S, D)
```

```python
from contextlib import ExitStack

import concourse.bass as bass
from concourse import mybir

F32 = mybir.dt.float32
F32R = mybir.dt.float32r
BF16 = mybir.dt.bfloat16
I32 = mybir.dt.int32
U32 = mybir.dt.uint32
ALU = mybir.AluOpType
ACT = mybir.ActivationFunctionType
AX = mybir.AxisListType

P = 128
B, S, D = 8, 256, 256
TOK = B * S
NT = TOK // P
TPB = S // P
GROUP = NT // 2
KD = D // P
H = 16
DK0, PAD0 = D // H, 32
M0 = H * PAD0 // P
DH1, INNER1 = 64, H * 64
M1 = INNER1 // P
F0, F1 = 1024, 1024
E1, R1 = 8, 16
I2, E2 = 704, 7
F3, E3 = 512, 8
NE = 8
LN_EPS = 1e-5
RMS_EPS = 1e-6
QB = 127.0
QEPS = 1e-5
ROUND = 1.5 * 2.0 ** 23
MASKED = -(2.0 ** 30)
NEVER = -3.0e38


class Shared:
    pass


def semaphores(nc, ctx, stage, names):
    names = names.split()
    free = sorted(nc.free_semaphores)
    first = next(n for n in free if all(n + i in free for i in range(len(names))))
    sems = [nc.alloc_semaphore(f"{stage}_{n}", first + i) for i, n in enumerate(names)]

    def end():
        nc.all_engine_barrier(sems_to_clear=range(first, first + len(sems)))
        for s in sems:
            nc.release_semaphore(s)

    ctx.callback(end)
    return sems


def x_tile(sh, t):
    return sh.X[:, bass.ds(t * D, D)]


def x_batch(sh, b):
    return sh.X[:, bass.ds(b * TPB * D, TPB * D)]


def tiles(ap, n=TPB):
    return ap.rearrange("p (t d) -> p t d", t=n)


def over_tiles(ap, n=TPB):
    return ap.unsqueeze(1).to_broadcast([P, n, ap.shape[1]])


def layernorm_vector(dve, sh, src, dst, stats, stats_ready, rstd_ready, normed, b, eps=LN_EPS, per=1, k=0, n=TPB):
    for t in range(n):
        ins = dve.bn_stats(sh.bn6[:, t, :], src(t))
    ins.then_inc(stats, 1)
    dve.wait_ge(stats, b * (3 * per) + 3 * k + 1)
    dve.sem_inc(stats, 1)
    for t in range(n):
        ins = dve.bn_aggr(sh.mv[:, t, :], sh.bn6[:, t, :])
    ins.then_inc(stats, 1)
    dve.wait_ge(stats, b * (3 * per) + 3 * k + 3)
    dve.tensor_scalar(sh.var[:, 0:n], sh.mv[:, 0:n, 1], eps, None, ALU.add).then_inc(stats_ready, 1)
    dve.wait_ge(rstd_ready, b * per + k + 1)
    for t in range(n):
        ins = dve.tensor_scalar(dst[:, t, :], src(t), sh.mv[:, t, 0:1], sh.rstd[:, t:t + 1], ALU.subtract, ALU.mult)
    ins.then_inc(normed, 1)


def layernorm_pool(pool, sh, stats_ready, rstd_ready, k, n=TPB):
    pool.wait_ge(stats_ready, k + 1)
    pool.tensor_tensor(sh.rstd[:, 0:n], sh.var[:, 0:n], sh.minus_half[:, 0:n], ALU.pow).then_inc(rstd_ready, 1)


def transpose_batch(pe, sh, out, src, n_rows=TPB, n_cols=KD):
    for c in range(n_cols):
        for t in range(n_rows):
            ins = pe.transpose(out[:, (c * n_rows + t) * P:(c * n_rows + t + 1) * P], src[:, t, c * P:(c + 1) * P], sh.ident[:])
    return ins


def product(pe, out, lhsT, rhs):
    n = len(lhsT)
    for k in range(n):
        ins = pe.matmul(out, lhsT[k], rhs[k], start=(k == 0), stop=(k == n - 1))
    return ins


def product_split(pe, out, lhsT, rhs):
    n = len(lhsT)
    for k in range(n):
        pe.matmul(out, lhsT[k][0], rhs[k][0], start=(k == 0), stop=False)
        pe.matmul(out, lhsT[k][0], rhs[k][1], start=False, stop=False)
        ins = pe.matmul(out, lhsT[k][1], rhs[k][0], start=False, stop=(k == n - 1))
    return ins


def product_full(pe, out, lhsT, rhs):
    n = len(lhsT)
    for k in range(n):
        for a in range(2):
            for b in range(2):
                ins = pe.matmul(out, lhsT[k][a], rhs[k][b], start=(k == a == b == 0), stop=(k == n - 1 and a == b == 1))
    return ins


def stage_start(nc, sh, d):
    with ExitStack() as ctx:
        x_loaded, zeroed, made = semaphores(nc, ctx, "st", "x_loaded zeroed made")
        block = ctx.enter_context(nc.Block())

        @block.sync
        def _(sp):
            sp.dma_start(tiles(sh.X[:], NT), d["x"]).then_inc(x_loaded, 16)
            sp.wait_ge(x_loaded, 16)

        @block.gpsimd
        def _(pool):
            pool.memset(sh.ident[:], 0.0).then_inc(zeroed, 1)
            pool.wait_ge(zeroed, 1)
            pool.affine_select(out=sh.ident[:], in_=sh.ident[:], compare_op=ALU.not_equal, fill=1.0, base=0,
                               pattern=[[-1, P]], channel_multiplier=1).then_inc(made, 1)
            pool.memset(sh.minus_half[:], -0.5).then_inc(made, 1)
            pool.memset(sh.ones[:], 1.0).then_inc(made, 1)
            pool.wait_ge(made, 3)
            pool.tensor_copy(sh.ident16[:], sh.ident[:]).then_inc(made, 1)
            pool.wait_ge(made, 4)


def stage_l0_attention(nc, sh, d):
    with ExitStack() as ctx:
        def sb(name, shape, dt=F32):
            return ctx.enter_context(nc.sbuf_tensor("a_" + name, shape, dt))

        wq, wk, wv, wo = sb("wq", [P, KD, H * PAD0]), sb("wk", [P, KD, H * PAD0]), sb("wv", [P, KD, D]), sb("wo", [P, KD, D])
        wq_split, wk_split = sb("wq_split", [P, 2, KD, H * PAD0], F32R), sb("wk_split", [P, 2, KD, H * PAD0], F32R)
        wv_split = sb("wv_split", [P, 2, KD, D], F32R)
        bq, bqs, bk = sb("bq", [P, M0]), sb("bqs", [P, M0]), sb("bk", [P, M0])
        bv, bo, low_rows = sb("bv", [P, D]), sb("bo", [P, D]), sb("low_rows", [P, 1])
        ctxT, ctx_split = sb("ctxT", [P, KD, S]), sb("ctx_split", [P, 2, KD, S], F32R)
        mask = sb("mask", [P, TPB, S], I32)
        lowered = sb("lowered", [P, TPB * S])
        xn = sb("xn", [P, TPB, D])
        xnT = sb("xnT", [P, 2, KD, S], F32R)
        q_full, q_high = sb("q_full", [P, 2, S]), sb("q_high", [P, 2, S], F32R)
        qT, kT = sb("qT", [P, M0, S], F32R), sb("kT", [P, 2, M0, S], F32R)
        v = sb("v", [P, TPB, D])
        sm, probs, probsT = sb("sm", [P, 4, TPB, S]), sb("probs", [P, 2, TPB, S]), sb("probsT", [P, 2, TPB, S])
        negmax, sums, rsums = sb("negmax", [P, 4, TPB]), sb("sums", [P, TPB, H]), sb("rsums", [P, TPB, H])
        att, attT = sb("att", [P, TPB, D]), sb("attT", [P, KD, S])
        xo = sb("xo", [P, TPB, D])
        (w_loaded, w_high, w_low, ctx_loaded, mask_loaded, ctx_high, ctx_ready, mask_used, stats, stats_ready, rstd_ready,
         xn_ready, xnT_ps, xnT_high, xnT_ready, kq_ps, kq_high, kq_ready, v_ps, v_ready, s_ps, s_masked, max_ready, exp_ready,
         probsT_ps, probsT_ready, head_done, rsums_ready, att_ready, attT_ps, attT_ready, out_ps, out_read, x_done,
         bias_ready, ctx_taken) = semaphores(
            nc, ctx, "a", "w_loaded w_high w_low ctx_loaded mask_loaded ctx_high ctx_ready mask_used stats stats_ready "
            "rstd_ready xn_ready xnT_ps xnT_high xnT_ready kq_ps kq_high kq_ready v_ps v_ready s_ps s_masked max_ready "
            "exp_ready probsT_ps probsT_ready head_done rsums_ready att_ready attT_ps attT_ready out_ps out_read x_done "
            "bias_ready ctx_taken")
        bank = sh.bank
        s_p, probsT_p, o_p, kq_p, xnT_p, v_p = [bank[0], bank[1]], [bank[2], bank[3]], bank[4], [bank[5], bank[6]], bank[7], bank[7]
        attT_p, out_p = bank[5], bank[6]
        WEIGHTS = [(wq, "L0_wq"), (wk, "L0_wk"), (wv, "L0_wv"), (wo, "L0_wo"), (bq, "L0_bq"), (bk, "L0_bk"),
                   (bv, "L0_bv"), (bo, "L0_bo"), (low_rows, "L0_low_rows")]
        SPLITS = [(wq, wq_split), (wk, wk_split), (wv, wv_split)]
        T_AT, KQ_AT, V_AT = 2, {4: 0, 7: 1, 10: 2, 14: 3}, 8
        block = ctx.enter_context(nc.Block())

        @block.sync
        def _(sp):
            for dst, name in WEIGHTS:
                sp.dma_start(dst[:], d[name]).then_inc(w_loaded, 16)
            sp.dma_start(ctxT[:], d["ctxT"][:, 0:KD, :]).then_inc(ctx_loaded, 16)
            sp.dma_start(mask[:], d["mask"][:, 0:TPB, :]).then_inc(mask_loaded, 16)
            with sp.Fori(1, B) as b:
                sp.wait_ge(ctx_ready, b)
                sp.dma_start(ctxT[:], d["ctxT"][:, bass.ds(b * KD, KD), :]).then_inc(ctx_loaded, 16)
                sp.wait_ge(mask_used, b)
                sp.dma_start(mask[:], d["mask"][:, bass.ds(b * TPB, TPB), :]).then_inc(mask_loaded, 16)

        @block.gpsimd
        def _(pool):
            def split_context(b):
                pool.wait_ge(ctx_loaded, b * 16 + 16)
                pool.sem_inc(ctx_taken, 1)
                pool.tensor_copy(ctx_split[:, 0], ctxT[:]).then_inc(ctx_high, 1)
                pool.wait_ge(ctx_high, b + 1)
                pool.tensor_tensor(ctx_split[:, 1], ctxT[:], ctx_split[:, 0].bitcast(F32), ALU.subtract).then_inc(ctx_ready, 1)

            for n, (w, w_split) in enumerate(SPLITS):
                pool.wait_ge(w_high, n + 1)
                pool.tensor_tensor(w_split[:, 1], w[:], w_split[:, 0].bitcast(F32), ALU.subtract).then_inc(w_low, 1)
            layernorm_pool(pool, sh, stats_ready, rstd_ready, 0)
            split_context(0)
            with pool.Fori(1, B) as b:
                layernorm_pool(pool, sh, stats_ready, rstd_ready, b)
                pool.wait_ge(kq_ps, b * M0)
                split_context(b)

        @block.vector
        def _(dve):
            def norm(b):
                layernorm_vector(dve, sh, lambda t: x_tile(sh, b * TPB + t), xn, stats, stats_ready, rstd_ready, xn_ready, b)

            def low_xnT(b):
                dve.wait_ge(xnT_high, b + 1)
                dve.tensor_tensor(xnT[:, 1].rearrange("p c s -> p (c s)"), xnT_p[:],
                                  xnT[:, 0].rearrange("p c s -> p (c s)").bitcast(F32), ALU.subtract).then_inc(xnT_ready, 1)

            def low_kq(b, m):
                dve.wait_ge(kq_high, b * M0 + m + 1)
                dve.scalar_tensor_tensor(kT[:, 1, m], kq_p[m % 2][:, 0:S], bk[:, m:m + 1], kT[:, 0, m].bitcast(F32),
                                         ALU.add, ALU.subtract)
                dve.scalar_tensor_tensor(qT[:, m], q_high[:, m % 2].bitcast(F32), low_rows[:], q_full[:, m % 2],
                                         ALU.mult, ALU.add).then_inc(kq_ready, 1)

            def keep_v(b):
                dve.wait_ge(v_ps, b + 1)
                dve.tensor_tensor(v[:], tiles(v_p[:]), over_tiles(bv[:]), ALU.add).then_inc(v_ready, 1)

            def lower(b):
                dve.wait_ge(mask_loaded, b * 16 + 16)
                dve.tensor_scalar(tiles(lowered[:]), mask[:], 0.0, MASKED, ALU.is_equal, ALU.mult).then_inc(mask_used, 1)
                dve.wait_ge(mask_used, b + 1)

            def row_max(b, h, first=False):
                dve.wait_ge(s_ps, b * H + h + 1)
                if not first:
                    dve.wait_ge(exp_ready, b * H + max(h - 3, 0))
                dve.tensor_tensor(sm[:, h % 4].rearrange("p t s -> p (t s)"), s_p[h % 2][:], lowered[:], ALU.add)\
                   .then_inc(s_masked, 1)
                dve.wait_ge(s_masked, b * H + h + 1)
                dve.tensor_reduce(negmax[:, h % 4], sm[:, h % 4], AX.X, ALU.max, negate=True).then_inc(max_ready, 1)

            def batch(b, last):
                for h in range(H):
                    if h + 2 == H and not last:
                        lower(b + 1)
                    if h + 2 < H or not last:
                        row_max(b, h + 2)
                    if last:
                        continue
                    if h == T_AT - 2:
                        norm(b + 1)
                    if h == T_AT + 1:
                        low_xnT(b + 1)
                    if h - 1 in KQ_AT:
                        low_kq(b + 1, KQ_AT[h - 1])
                dve.wait_ge(exp_ready, b * H + H)
                dve.reciprocal(rsums[:], sums[:]).then_inc(rsums_ready, 1)
                dve.wait_ge(rsums_ready, b + 1)
                dve.wait_ge(head_done, b * H + H)
                for t in range(TPB):
                    ins = dve.tensor_tensor(att[:, t].rearrange("p (h e) -> p h e", h=H),
                                            o_p[:, t * D:(t + 1) * D].rearrange("p (h e) -> p h e", h=H),
                                            rsums[:, t].unsqueeze(2).to_broadcast([P, H, DK0]), ALU.mult)
                ins.then_inc(att_ready, 1)
                if not last:
                    keep_v(b + 1)
                dve.wait_ge(out_ps, b + 1)
                dve.tensor_tensor(xo[:], tiles(out_p[:]), over_tiles(bo[:]), ALU.add).then_inc(out_read, 1)
                dve.wait_ge(out_read, b + 1)
                dve.tensor_tensor(x_batch(sh, b), x_batch(sh, b), xo[:].rearrange("p t d -> p (t d)"), ALU.add).then_inc(x_done, 1)

            dve.wait_ge(w_loaded, 16 * len(WEIGHTS))
            dve.tensor_scalar(bqs[:], bq[:], DK0 ** -0.5, None, ALU.mult).then_inc(bias_ready, 1)
            norm(0)
            low_xnT(0)
            for m in range(M0):
                low_kq(0, m)
            keep_v(0)
            lower(0)
            row_max(0, 0, first=True)
            row_max(0, 1, first=True)
            with dve.Fori(0, B - 1) as b:
                batch(b, last=False)
            batch(B - 1, last=True)
            dve.wait_ge(x_done, B)

        @block.scalar
        def _(act):
            def high_xnT(b):
                act.wait_ge(xnT_ps, b + 1)
                act.activation(xnT[:, 0].rearrange("p c s -> p (c s)"), xnT_p[:], ACT.Copy).then_inc(xnT_high, 1)

            def high_kq(b, m):
                act.wait_ge(kq_ps, b * M0 + m + 1)
                act.activation(kT[:, 0, m], kq_p[m % 2][:, 0:S], ACT.Identity, bias=bk[:, m:m + 1])
                act.activation(q_full[:, m % 2], kq_p[m % 2][:, S:2 * S], ACT.Identity, bias=bqs[:, m:m + 1], scale=DK0 ** -0.5)
                act.activation(q_high[:, m % 2], kq_p[m % 2][:, S:2 * S], ACT.Identity, bias=bqs[:, m:m + 1],
                               scale=DK0 ** -0.5).then_inc(kq_high, 1)

            def exp(b, h, first=False):
                act.wait_ge(max_ready, b * H + h + 1)
                if not first:
                    act.wait_ge(probsT_ps, b * H + h - 1)
                if h == H:
                    act.wait_ge(rsums_ready, b + 1)
                for t in range(TPB):
                    ins = act.activation(probs[:, h % 2, t], sm[:, h % 4, t], ACT.Exp, bias=negmax[:, h % 4, t:t + 1],
                                         accum_out=sums[:, t, h % H:h % H + 1])
                ins.then_inc(exp_ready, 1)

            def batch(b, last):
                for h in range(H):
                    if h + 1 < H:
                        exp(b, h + 1, first=(h == 0))
                    act.wait_ge(probsT_ps, b * H + h + 1)
                    if h >= 2:
                        act.wait_ge(head_done, b * H + h - 1)
                    act.activation(probsT[:, h % 2].rearrange("p c s -> p (c s)"), probsT_p[h % 2][:], ACT.Copy)\
                       .then_inc(probsT_ready, 1)
                    if last:
                        continue
                    if h == T_AT + 1:
                        high_xnT(b + 1)
                    if h - 1 in KQ_AT:
                        high_kq(b + 1, KQ_AT[h - 1])
                if not last:
                    exp(b, H)
                act.wait_ge(attT_ps, b + 1)
                act.activation(attT[:].rearrange("p c s -> p (c s)"), attT_p[:], ACT.Copy).then_inc(attT_ready, 1)

            act.wait_ge(w_loaded, 16 * len(WEIGHTS))
            for w, w_split in SPLITS:
                act.activation(w_split[:, 0], w[:], ACT.Copy).then_inc(w_high, 1)
            act.wait_ge(bias_ready, 1)
            high_xnT(0)
            for m in range(M0):
                if m >= 2:
                    act.wait_ge(kq_ready, m - 1)
                high_kq(0, m)
            exp(0, 0, first=True)
            with act.Fori(0, B - 1) as b:
                batch(b, last=False)
            batch(B - 1, last=True)

        @block.tensor
        def _(pe):
            def turn_x(b):
                pe.wait_ge(xn_ready, b + 1)
                transpose_batch(pe, sh, xnT_p, xn).then_inc(xnT_ps, 1)

            def project_kq(b, m):
                for w, src, col in ((wk_split, ctx_split, 0), (wq_split, xnT, S)):
                    ins = product_split(pe, kq_p[m % 2][:, col:col + S],
                                        [[w[:, hl, c, m * P:(m + 1) * P] for hl in range(2)] for c in range(KD)],
                                        [[src[:, hl, c] for hl in range(2)] for c in range(KD)])
                ins.then_inc(kq_ps, 1)

            def project_v(b):
                for t in range(TPB):
                    ins = product_split(pe, v_p[:, t * D:(t + 1) * D],
                                        [[ctx_split[:, hl, c, t * P:(t + 1) * P] for hl in range(2)] for c in range(KD)],
                                        [[wv_split[:, hl, c] for hl in range(2)] for c in range(KD)])
                ins.then_inc(v_ps, 1)

            def scores(b, h, first=False):
                r, m = h % 4 * PAD0, h % H // 4
                if not first:
                    pe.wait_ge(s_masked, b * H + h - 1)
                for t in range(TPB):
                    for hl in range(2):
                        ins = pe.matmul(s_p[h % 2][:, t * S:(t + 1) * S], qT[r:r + PAD0, m, t * P:(t + 1) * P],
                                        kT[r:r + PAD0, hl, m], start=(hl == 0), stop=(hl == 1))
                ins.then_inc(s_ps, 1)

            def turn(b, h):
                pe.wait_ge(exp_ready, b * H + h + 1)
                if h >= 2:
                    pe.wait_ge(probsT_ready, b * H + h - 1)
                transpose_batch(pe, sh, probsT_p[h % 2], probs[:, h % 2]).then_inc(probsT_ps, 1)

            def values(b, h):
                pe.wait_ge(probsT_ready, b * H + h + 1)
                for t in range(TPB):
                    ins = product(pe, o_p[:, t * D + h * DK0:t * D + (h + 1) * DK0],
                                  [probsT[:, h % 2, c, t * P:(t + 1) * P] for c in range(TPB)],
                                  [v[:, c, h * DK0:(h + 1) * DK0] for c in range(TPB)])
                ins.then_inc(head_done, 1)

            def batch(b, last):
                for h in range(H):
                    if h + 2 < H or not last:
                        if h + 2 == H:
                            pe.wait_ge(kq_ready, (b + 1) * M0 + 3)
                        scores(b, h + 2)
                    turn(b, h)
                    if h == 1:
                        pe.wait_ge(v_ready, b + 1)
                    if h >= 1:
                        values(b, h - 1)
                    if last:
                        continue
                    if h == T_AT:
                        pe.wait_ge(v_ready, b + 1)
                        turn_x(b + 1)
                    if h in KQ_AT:
                        if KQ_AT[h] == 0:
                            pe.wait_ge(xnT_ready, b + 2)
                            pe.wait_ge(ctx_ready, b + 2)
                        if KQ_AT[h] == 1 :
                            pe.wait_ge(out_read, b)
                        if KQ_AT[h] >= 2:
                            pe.wait_ge(kq_ready, (b + 1) * M0 + KQ_AT[h] - 1)
                        project_kq(b + 1, KQ_AT[h])
                    if h == V_AT:
                        project_v(b + 1)
                values(b, H - 1)
                pe.wait_ge(att_ready, b + 1)
                transpose_batch(pe, sh, attT_p, att).then_inc(attT_ps, 1)
                pe.wait_ge(attT_ready, b + 1)
                pe.wait_ge(kq_ready, (b + 1) * M0 if last else (b + 2) * M0)
                for t in range(TPB):
                    ins = product(pe, out_p[:, t * D:(t + 1) * D], [attT[:, c, t * P:(t + 1) * P] for c in range(KD)],
                                  [wo[:, c] for c in range(KD)])
                ins.then_inc(out_ps, 1)

            pe.wait_ge(w_loaded, 16 * len(WEIGHTS))
            turn_x(0)
            pe.wait_ge(w_low, len(SPLITS))
            pe.wait_ge(xnT_ready, 1)
            pe.wait_ge(ctx_ready, 1)
            for m in range(M0):
                if m >= 2:
                    pe.wait_ge(kq_ready, m - 1)
                project_kq(0, m)
            project_v(0)
            pe.wait_ge(kq_ready, M0)
            scores(0, 0, first=True)
            scores(0, 1, first=True)
            with pe.Fori(0, B - 1) as b:
                batch(b, last=False)
            batch(B - 1, last=True)


def stage_l0_ffn(nc, sh, d):
    with ExitStack() as ctx:
        def sb(name, shape, dt=F32):
            return ctx.enter_context(nc.sbuf_tensor("b_" + name, shape, dt))

        KF = F0 // P
        w, wq = sb("w", [P, 2, KD * F0]), sb("wq", [P, 2, KD * F0], BF16)
        wsum, wscale, winv = sb("wsum", [P, 2]), sb("wscale", [P, 2]), sb("winv", [P, 2])
        b1, b2 = sb("b1", [P, F0]), sb("b2", [P, D])
        xn, xr, xq, xqT = sb("xn", [P, TPB, D]), sb("xr", [P, TPB, D]), sb("xq", [P, TPB, D], BF16), sb("xqT", [P, TPB, D], BF16)
        h, hr, hq = sb("h", [P, TPB, F0]), sb("hr", [P, TPB, F0]), sb("hq", [P, TPB, F0], BF16)
        hqT = sb("hqT", [P, TPB, F0], BF16)
        xa, xinv, xscale = sb("xa", [P, TPB]), sb("xinv", [P, TPB]), sb("xscale", [P, TPB])
        ha, hinv, hscale = sb("ha", [P, TPB]), sb("hinv", [P, TPB]), sb("hscale", [P, TPB])
        xo = sb("xo", [P, TPB, D])
        (w_loaded, chain, sum_ready, total_ps, weights_ready, stats, stats_ready, rstd_ready, xn_ready, xq_ready,
         xqT_ps, xqT_ready, h_ps, h_scaled, gelu_done, hq_ready, hqT_ps, hqT_ready, out_ps, step) = semaphores(
            nc, ctx, "b", "w_loaded chain sum_ready total_ps weights_ready stats stats_ready rstd_ready xn_ready xq_ready "
            "xqT_ps xqT_ready h_ps h_scaled gelu_done hq_ready hqT_ps hqT_ready out_ps step")
        bank = sh.bank
        total_p, xqT_p, h_p = bank[0], bank[0], [[bank[1], bank[2]], [bank[3], bank[4]]]
        hqT_p, out_p = [bank[5], bank[6]], bank[7]
        w1q = wq[:, 0].rearrange("p (c f) -> p c f", c=KD)
        w2q = wq[:, 1].rearrange("p (c f) -> p c f", c=KF)
        STEPS = 11
        block = ctx.enter_context(nc.Block())

        @block.sync
        def _(sp):
            for dst, name in [(w[:, 0], "L0_w1"), (w[:, 1], "L0_w2"), (b1[:], "L0_b1"), (b2[:], "L0_b2")]:
                sp.dma_start(dst, d[name]).then_inc(w_loaded, 16)

        @block.gpsimd
        def _(pool):
            with pool.Fori(0, B) as b:
                layernorm_pool(pool, sh, stats_ready, rstd_ready, b)

        @block.vector
        def _(dve):
            dve.wait_ge(w_loaded, 4 * 16)
            dve.tensor_reduce(wsum[:], w[:], AX.X, ALU.add, apply_absolute_value=True).then_inc(sum_ready, 1)
            dve.wait_ge(total_ps, 1)
            dve.tensor_scalar(wscale[:], total_p[:, 0:2], 1.0 / (D * F0), QEPS, ALU.mult, ALU.max).then_inc(chain, 1)
            dve.wait_ge(chain, 1)
            dve.reciprocal(winv[:], wscale[:]).then_inc(chain, 1)
            dve.wait_ge(chain, 2)
            for k in range(2):
                dve.tensor_scalar(w[:, k], w[:, k], winv[:, k:k + 1], ROUND, ALU.mult, ALU.add).then_inc(chain, 1)
            dve.wait_ge(chain, 4)
            dve.tensor_scalar(w[:], w[:], ROUND, 1.0, ALU.subtract, ALU.min).then_inc(chain, 1)
            dve.wait_ge(chain, 5)
            dve.tensor_scalar(wq[:], w[:], -1.0, None, ALU.max).then_inc(weights_ready, 1)

            with dve.Fori(0, B) as b:
                s0 = b * STEPS

                def quantize(x, absmax, inv, scale, k, rounded, q, ready, s):
                    dve.tensor_reduce(absmax[:], x[:], AX.X, ALU.max, apply_absolute_value=True).then_inc(step, 1)
                    dve.wait_ge(step, s + 1)
                    dve.tensor_scalar(absmax[:], absmax[:], QEPS, None, ALU.max).then_inc(step, 1)
                    dve.wait_ge(step, s + 2)
                    dve.tensor_scalar(scale[:], absmax[:], wscale[:, k:k + 1], 1.0 / QB, ALU.mult, ALU.mult)
                    dve.reciprocal(inv[:], absmax[:]).then_inc(step, 1)
                    dve.wait_ge(step, s + 3)
                    dve.tensor_scalar(inv[:], inv[:], QB, None, ALU.mult).then_inc(step, 1)
                    dve.wait_ge(step, s + 4)
                    for t in range(TPB):
                        ins = dve.tensor_scalar(rounded[:, t], x[:, t], inv[:, t:t + 1], ROUND, ALU.mult, ALU.add)
                    ins.then_inc(step, 1)
                    dve.wait_ge(step, s + 5)
                    for t in range(TPB):
                        ins = dve.tensor_scalar(q[:, t], rounded[:, t], ROUND, QB, ALU.subtract, ALU.min)
                    ins.then_inc(ready, 1)
                    dve.wait_ge(ready, 2 * b + 1)
                    dve.tensor_scalar(q[:], q[:], -QB - 1.0, None, ALU.max).then_inc(ready, 1)

                layernorm_vector(dve, sh, lambda t: x_tile(sh, b * TPB + t), xn, stats, stats_ready, rstd_ready, xn_ready, b)
                dve.wait_ge(xn_ready, b + 1)
                quantize(xn, xa, xinv, xscale, 0, xr, xq, xq_ready, s0)
                dve.wait_ge(xqT_ps, b + 1)
                dve.tensor_copy(xqT[:].rearrange("p t d -> p (t d)"), xqT_p[:].bitcast(BF16)[:, 0:TPB * D]).then_inc(xqT_ready, 1)
                for t in range(TPB):
                    dve.wait_ge(h_ps, b * TPB + t + 1)
                    for n in range(2):
                        ins = dve.scalar_tensor_tensor(h[:, t, n * 512:(n + 1) * 512], h_p[t][n][:], xscale[:, t:t + 1],
                                                       b1[:, n * 512:(n + 1) * 512], ALU.mult, ALU.add)
                    ins.then_inc(h_scaled, 1)
                dve.wait_ge(gelu_done, b * TPB + TPB)
                quantize(h, ha, hinv, hscale, 1, hr, hq, hq_ready, s0 + 5)
                dve.wait_ge(out_ps, b + 1)
                for t in range(TPB):
                    ins = dve.scalar_tensor_tensor(xo[:, t], out_p[:, t * D:(t + 1) * D], hscale[:, t:t + 1], b2[:], ALU.mult, ALU.add)
                ins.then_inc(step, 1)
                dve.wait_ge(step, s0 + STEPS)
                dve.tensor_tensor(x_batch(sh, b), x_batch(sh, b), xo[:].rearrange("p t d -> p (t d)"), ALU.add)

        @block.scalar
        def _(act):
            with act.Fori(0, B) as b:
                for t in range(TPB):
                    act.wait_ge(h_scaled, b * TPB + t + 1)
                    act.activation(h[:, t], h[:, t], ACT.Gelu).then_inc(gelu_done, 1)
                for t in range(TPB):
                    act.wait_ge(hqT_ps, b * TPB + t + 1)
                    act.activation(hqT[:, t], hqT_p[t][:].bitcast(BF16), ACT.Copy).then_inc(hqT_ready, 1)

        @block.tensor
        def _(pe):
            pe.wait_ge(sum_ready, 1)
            pe.matmul(total_p[:, 0:2], sh.ones[:], wsum[:], start=True, stop=True).then_inc(total_ps, 1)
            pe.wait_ge(weights_ready, 1)
            with pe.Fori(0, B) as b:
                pe.wait_ge(xq_ready, 2 * b + 2)
                for t in range(TPB):
                    for c in range(KD):
                        at = (t * KD + c) * P
                        ins = pe.transpose(xqT_p[:].bitcast(BF16)[:, at:at + P], xq[:, t, c * P:(c + 1) * P], sh.ident16[:])
                ins.then_inc(xqT_ps, 1)
                pe.wait_ge(xqT_ready, b + 1)
                for t in range(TPB):
                    for n in range(2):
                        ins = product(pe, h_p[t][n][:], [xqT[:, t, c * P:(c + 1) * P] for c in range(KD)],
                                      [w1q[:, c, n * 512:(n + 1) * 512] for c in range(KD)])
                    ins.then_inc(h_ps, 1)
                pe.wait_ge(hq_ready, 2 * b + 2)
                for t in range(TPB):
                    for c in range(KF):
                        ins = pe.transpose(hqT_p[t][:].bitcast(BF16)[:, c * P:(c + 1) * P], hq[:, t, c * P:(c + 1) * P], sh.ident16[:])
                    ins.then_inc(hqT_ps, 1)
                for t in range(TPB):
                    pe.wait_ge(hqT_ready, b * TPB + t + 1)
                    ins = product(pe, out_p[:, t * D:(t + 1) * D], [hqT[:, t, c * P:(c + 1) * P] for c in range(KF)],
                                  [w2q[:, c] for c in range(KF)])
                ins.then_inc(out_ps, 1)


def stage_l1_attention(nc, sh, d):
    with ExitStack() as ctx:
        def sb(name, shape, dt=F32):
            return ctx.enter_context(nc.sbuf_tensor("c_" + name, shape, dt))

        SK = 2 * S
        KC = SK // P
        HALF = DH1
        HR = H // 2
        MR = HR * DH1 // P
        NU = TPB * HR
        NW = 2 * MR
        w_stage = sb("w_stage", [P, 2, 4, KD, P])
        w_split = sb("w_split", [P, 2, 4, KD, MR * P], F32R)
        wo = sb("wo", [P, NW, D])
        gain, shift, bo = sb("gain", [P, KD]), sb("shift", [P, KD]), sb("bo", [P, D])
        ctxT, ctx_split, x_split = sb("ctxT", [P, KD, S]), sb("ctx_split", [P, 2, KD, S], F32R), sb("x_split", [P, 2, KD, S], F32R)
        x1, xn = sb("x1", [P, GROUP, D]), sb("xn", [P, GROUP, D])
        xnT = sb("xnT", [P, KD, TOK])
        q, k = sb("q", [P, 2, HR, S], F32R), sb("k", [P, HR, SK], F32R)
        v = sb("v", [P, KC, HR * DH1])
        probs, probsT = sb("probs", [P, 2, SK]), sb("probsT", [P, 2, KC, P])
        negmax, sums, rsums = sb("negmax", [P, 2]), sb("sums", [P, TPB, HR]), sb("rsums", [P, TPB, HR])
        att, attT = sb("att", [P, TPB, HR * DH1]), sb("attT", [P, TPB, MR, P])
        xo = sb("xo", [P, TPB, D])
        probsT_ready = semaphores(nc, ctx, "c", "probsT_act probsT_dve")
        w_loaded = semaphores(nc, ctx, "c", "w_loaded0 w_loaded1")
        (s_loaded, w_taken, w_high, w_ready, ctx_loaded, ctx_high, ctx_ready, x_high, x_ready, stats, stats_ready,
         rstd_ready, xn_ready, xnT_ps, xnT_ready, job_ps, job_high, job_ready, q_twice, s_ps, max_ready, exp_ready, probsT_ps,
         head_done, rsums_ready, att_ready, attT_ps, attT_ready, out_ps, out_read,
         x_done) = semaphores(
            nc, ctx, "c", "s_loaded w_taken w_high w_ready ctx_loaded ctx_high ctx_ready x_high x_ready stats "
            "stats_ready rstd_ready xn_ready xnT_ps xnT_ready job_ps job_high job_ready q_twice s_ps max_ready exp_ready "
            "probsT_ps head_done rsums_ready att_ready attT_ps attT_ready out_ps out_read x_done")
        bank = sh.bank
        s_p, probsT_p, o_p, job_p = [bank[0], bank[1]], [bank[2], bank[3]], [bank[4], bank[5]], [bank[6], bank[7]]
        attT_p, out_p = [bank[2], bank[3]], bank[6]
        SMALL = [(gain, "L1_g"), (shift, "L1_b"), (bo, "L1_bo"), (wo, "L1_wo")]
        JOBS = [("k", 0, 2), ("q", 0, 3), ("k", 1, 6), ("q", 1, 7), ("v", (0, 0), 9), ("v", (0, 1), 10),
                ("k", 2, 11), ("q", 2, 12), ("k", 3, 14), ("q", 3, 15), ("v", (1, 0), None), ("v", (1, 1), None)]
        NJ = len(JOBS)
        JOB_AT = {step: j for j, (_, _, step) in enumerate(JOBS) if step is not None}
        Q_JOB = [j for j, (kind, _, _) in enumerate(JOBS) if kind == "q"]

        def v_part(number, r):
            half, pair = number
            return v[:, 2 * pair + r, half * 2 * P:(half + 1) * 2 * P]

        high_rows, low_rows = (slice(0, HALF), slice(HALF, P)), (slice(HALF, P), slice(0, HALF))
        block = ctx.enter_context(nc.Block())

        def rounds(engine, do_round):
            for half in range(2):
                with engine.Fori(0, B - 1) as b:
                    do_round(b + half * B, b, half, False)
                do_round(half * B + B - 1, B - 1, half, True)

        @block.sync
        def _(sp):
            def load_weights(j):
                if j >= 2:
                    sp.wait_ge(w_ready, j - 1)
                sp.dma_start(w_stage[:, j % 2], d["L1_w"][:, j]).then_inc(w_loaded[j % 2], 16)

            def load_context(b):
                sp.dma_start(ctxT[:], d["ctxT"][:, bass.ds(b * KD, KD), :]).then_inc(ctx_loaded, 16)

            for dst, name in SMALL[:3]:
                sp.dma_start(dst[:], d[name]).then_inc(s_loaded, 16)
            load_context(0)
            load_weights(0)
            load_weights(1)
            sp.dma_start(wo[:], d["L1_wo"]).then_inc(s_loaded, 16)
            for j in range(2, MR + 2):
                load_weights(j)
            for half in range(2):
                if half:
                    sp.wait_ge(ctx_ready, B)
                    load_context(0)
                    for j in range(MR + 2, NW):
                        load_weights(j)
                with sp.Fori(1, B) as b:
                    sp.wait_ge(ctx_ready, b + half * B)
                    load_context(b)

        @block.gpsimd
        def _(pool):
            def split_weights(j):
                pool.wait_ge(w_loaded[j % 2], 16 * (j // 2) + 16)
                pool.sem_inc(w_taken, 1)
                high, low = [w_split[:, hl, :, :, j % MR * P:(j % MR + 1) * P].rearrange("p n c s -> p (n c) s") for hl in range(2)]
                w = w_stage[:, j % 2].rearrange("p n c s -> p (n c) s")
                pool.tensor_copy(high, w).then_inc(w_high, 1)
                pool.wait_ge(w_high, j + 1)
                pool.tensor_tensor(low, w, high.bitcast(F32), ALU.subtract).then_inc(w_ready, 1)

            def split_sources(i, b):
                pool.wait_ge(ctx_loaded, i * 16 + 16)
                pool.sem_inc(w_taken, 1)
                pool.tensor_copy(ctx_split[:, 0], ctxT[:]).then_inc(ctx_high, 1)
                pool.tensor_copy(x_split[:, 0], xnT[:, :, bass.ds(b * S, S)]).then_inc(x_high, 1)
                pool.wait_ge(ctx_high, i + 1)
                pool.tensor_tensor(ctx_split[:, 1], ctxT[:], ctx_split[:, 0].bitcast(F32), ALU.subtract).then_inc(ctx_ready, 1)
                pool.wait_ge(x_high, i + 1)
                pool.sem_inc(w_taken, 1)
                pool.tensor_tensor(x_split[:, 1], xnT[:, :, bass.ds(b * S, S)], x_split[:, 0].bitcast(F32), ALU.subtract)\
                    .then_inc(x_ready, 1)

            def double_queries(i, m, first=False):
                pool.wait_ge(x_ready, i + 1)
                pool.wait_ge(job_ready, i * NJ + Q_JOB[m] + 1)
                for par in range(2):
                    if par or m or not first:
                        pool.wait_ge(q_twice, (i * MR + m) * 2 + par)
                    pool.sem_inc(w_taken, 1)
                    pool.tensor_copy(q[low_rows[par], :, 2 * m + par], q[high_rows[par], :, 2 * m + par].bitcast(F32))\
                        .then_inc(q_twice, 1)

            def do_round(i, b, half, end):
                new_weights = end and half == 0
                if end and half:
                    return
                pool.wait_ge(job_ps, i * NJ + NJ)
                pool.wait_ge(q_twice, (i + 1) * MR * 2)
                split_sources(i + 1, 0 if new_weights else b + 1)
                for m in range(MR):
                    if new_weights:
                        if m:
                            pool.wait_ge(q_twice, ((i + 1) * MR + m) * 2)
                        split_weights(MR + m)
                        pool.wait_ge(w_ready, MR + m + 1)
                    double_queries(i + 1, m)

            layernorm_pool(pool, sh, stats_ready, rstd_ready, 0, n=GROUP)
            layernorm_pool(pool, sh, stats_ready, rstd_ready, 1, n=GROUP)
            split_weights(0)
            layernorm_pool(pool, sh, stats_ready, rstd_ready, 2, n=GROUP)
            layernorm_pool(pool, sh, stats_ready, rstd_ready, 3, n=GROUP)
            pool.wait_ge(xnT_ready, 2 * KD)
            split_sources(0, 0)
            for m in range(1, MR):
                split_weights(m)
            pool.wait_ge(w_ready, MR)
            for m in range(MR):
                double_queries(0, m, first=True)
            pool.wait_ge(xnT_ready, NT // GROUP * 2 * KD)
            rounds(pool, do_round)

        @block.vector
        def _(dve):
            def low_job(i, j):
                kind, m, _ = JOBS[j]
                dve.wait_ge(job_high, i * NJ + j + 1)
                ps = job_p[j % 2]
                if kind == "k":
                    for par in range(2):
                        hi = high_rows[par]
                        ins = dve.tensor_tensor(k[low_rows[par], 2 * m + par], ps[hi, :], k[hi, 2 * m + par].bitcast(F32), ALU.subtract)
                elif kind == "q":
                    for par in range(2):
                        hi = high_rows[par]
                        ins = dve.scalar_tensor_tensor(q[hi, 1, 2 * m + par], ps[hi, 0:S], DH1 ** -0.5,
                                                       q[hi, 0, 2 * m + par].bitcast(F32), ALU.mult, ALU.subtract)
                else:
                    ins = dve.tensor_copy(v_part(m, 1), ps[:, 2 * P:4 * P])
                ins.then_inc(job_ready, 1)

            def row_max(i, u, first=False):
                dve.wait_ge(s_ps, i * NU + u + 1)
                if not first:
                    dve.wait_ge(exp_ready, i * NU + u - 1)
                dve.tensor_reduce(negmax[:, u % 2:u % 2 + 1], s_p[u % 2][:], AX.X, ALU.max, negate=True).then_inc(max_ready, 1)

            def do_round(i, b, half, end):
                last = end and half == 1
                for u in range(NU):
                    if u + 2 < NU or not last:
                        row_max(i, u + 2)
                    if u % 2:
                        dve.wait_ge(probsT_ps, i * NU + u + 1)
                        if u >= 2:
                            dve.wait_ge(head_done, i * NU + u - 1)
                        dve.tensor_copy(probsT[:, 1].rearrange("p c s -> p (c s)"), probsT_p[1][:]).then_inc(probsT_ready[1], 1)
                    if u - 1 in JOB_AT and not last:
                        low_job(i + 1, JOB_AT[u - 1])
                if not last:
                    low_job(i + 1, NJ - 3)
                dve.wait_ge(exp_ready, i * NU + NU)
                dve.reciprocal(rsums[:], sums[:]).then_inc(rsums_ready, 1)
                dve.wait_ge(rsums_ready, i + 1)
                dve.wait_ge(head_done, i * NU + NU)
                for t in range(TPB):
                    dve.tensor_tensor(att[:, t].rearrange("p (h e) -> p h e", e=DH1),
                                      o_p[t][:].rearrange("p (h e) -> p h e", e=DH1),
                                      rsums[:, t].unsqueeze(2).to_broadcast([P, HR, DH1]), ALU.mult).then_inc(att_ready, 1)
                if not last:
                    low_job(i + 1, NJ - 2)
                    low_job(i + 1, NJ - 1)
                dve.wait_ge(out_ps, i + 1)
                if half == 0:
                    dve.tensor_tensor(xo[:], tiles(out_p[:]), over_tiles(bo[:]), ALU.add).then_inc(out_read, 1)
                    dve.wait_ge(out_read, i + 1)
                    dve.tensor_tensor(x_batch(sh, b), x_batch(sh, b), xo[:].rearrange("p t d -> p (t d)"), ALU.add).then_inc(x_done, 1)
                else:
                    dve.wait_ge(x_done, i - B + 1)
                    dve.tensor_tensor(x_batch(sh, b), x_batch(sh, b), out_p[:], ALU.add).then_inc(out_read, 1)

            dve.wait_ge(s_loaded, 16 * len(SMALL))
            for g in range(NT // GROUP):
                xg = sh.X[:, g * GROUP * D:(g + 1) * GROUP * D]
                layernorm_vector(dve, sh, lambda t: xg[:, t * D:(t + 1) * D], x1, stats, stats_ready, rstd_ready, xn_ready, g,
                                 per=2, n=GROUP)
                dve.wait_ge(xn_ready, 2 * g + 1)
                if g:
                    dve.wait_ge(xnT_ps, g * 2 * KD)
                layernorm_vector(dve, sh, lambda t: x1[:, t], xn, stats, stats_ready, rstd_ready, xn_ready, g, per=2, k=1, n=GROUP)
            for j in range(NJ):
                low_job(0, j)
            row_max(0, 0, first=True)
            row_max(0, 1, first=True)
            rounds(dve, do_round)
            dve.wait_ge(out_read, 2 * B)

        @block.scalar
        def _(act):
            def high_job(i, j):
                kind, m, _ = JOBS[j]
                act.wait_ge(job_ps, i * NJ + j + 1)
                ps = job_p[j % 2]
                if kind == "k":
                    for par in range(2):
                        hi = high_rows[par]
                        ins = act.activation(k[hi, 2 * m + par], ps[hi, :], ACT.Copy)
                elif kind == "q":
                    for par in range(2):
                        hi = high_rows[par]
                        ins = act.activation(q[hi, 0, 2 * m + par], ps[hi, 0:S], ACT.Copy, scale=DH1 ** -0.5)
                else:
                    ins = act.activation(v_part(m, 0), ps[:, 0:2 * P], ACT.Copy)
                ins.then_inc(job_high, 1)

            def exp(i, u, first=False):
                act.wait_ge(max_ready, i * NU + u + 1)
                if not first:
                    act.wait_ge(probsT_ps, i * NU + u - 1)
                if u == NU:
                    act.wait_ge(rsums_ready, i + 1)
                h = u % NU // TPB
                act.activation(probs[:, u % 2], s_p[u % 2][:], ACT.Exp, bias=negmax[:, u % 2:u % 2 + 1],
                               accum_out=sums[:, u % TPB, h:h + 1]).then_inc(exp_ready, 1)

            def do_round(i, b, half, end):
                last = end and half == 1
                for u in range(NU):
                    if u + 1 < NU:
                        exp(i, u + 1, first=(u == 0))
                    if u % 2 == 0:
                        act.wait_ge(probsT_ps, i * NU + u + 1)
                        if u >= 2:
                            act.wait_ge(head_done, i * NU + u - 1)
                        act.activation(probsT[:, 0].rearrange("p c s -> p (c s)"), probsT_p[0][:], ACT.Copy)\
                           .then_inc(probsT_ready[0], 1)
                    if u - 1 in JOB_AT and not last:
                        high_job(i + 1, JOB_AT[u - 1])
                if not last:
                    high_job(i + 1, NJ - 3)
                    exp(i, NU)
                    high_job(i + 1, NJ - 2)
                    high_job(i + 1, NJ - 1)
                for t in range(TPB):
                    act.wait_ge(attT_ps, i * TPB + t + 1)
                    act.activation(attT[:, t].rearrange("p m s -> p (m s)"), attT_p[t][:], ACT.Copy).then_inc(attT_ready, 1)

            act.wait_ge(s_loaded, 16 * len(SMALL))
            for g in range(NT // GROUP):
                for c in range(KD):
                    for n in range(2):
                        act.wait_ge(xnT_ps, (g * KD + c) * 2 + n + 1)
                        at = (g * 2 + n) * 512
                        act.activation(xnT[:, c, at:at + 512], bank[4 * g + 2 * c + n][:], ACT.Identity, bias=shift[:, c:c + 1],
                                       scale=gain[:, c:c + 1]).then_inc(xnT_ready, 1)
            for j in range(NJ):
                high_job(0, j)
            exp(0, 0, first=True)
            rounds(act, do_round)

        @block.tensor
        def _(pe):
            def job(i, j, first=False):
                kind, m, _ = JOBS[j]
                if j == 0:
                    pe.wait_ge(x_ready, i + 1)
                    pe.wait_ge(ctx_ready, i + 1)
                if j >= 2:
                    pe.wait_ge(job_ready, i * NJ + j - 1)
                elif not first:
                    pe.wait_ge(out_read, i - 1)
                ps = job_p[j % 2]
                w = lambda n: [[w_split[:, hl, n, c, m * P:(m + 1) * P] for hl in range(2)] for c in range(KD)]
                src = lambda s: [[s[:, hl, c] for hl in range(2)] for c in range(KD)]
                if kind == "k":
                    product_split(pe, ps[:, 0:S], w(1), src(x_split))
                    ins = product_split(pe, ps[:, S:SK], w(3), src(ctx_split))
                elif kind == "q":
                    ins = product_split(pe, ps[:, 0:S], w(0), src(x_split))
                else:
                    half, pair = m
                    a, n = ((x_split, 2), (ctx_split, 3))[pair]
                    for r in range(2):
                        ins = product_split(pe, ps[:, r * 2 * P:(r + 1) * 2 * P],
                                            [[a[:, hl, c, r * P:(r + 1) * P] for hl in range(2)] for c in range(KD)],
                                            [[w_split[:, hl, n, c, half * 2 * P:(half + 1) * 2 * P] for hl in range(2)]
                                             for c in range(KD)])
                ins.then_inc(job_ps, 1)

            def scores(i, u, first=False):
                h, t = u % NU // TPB, u % TPB
                if not first:
                    pe.wait_ge(exp_ready, i * NU + u - 1)
                for hl in range(2):
                    ins = pe.matmul(s_p[u % 2][:], q[:, hl, h, t * P:(t + 1) * P], k[:, h], start=(hl == 0), stop=(hl == 1))
                ins.then_inc(s_ps, 1)

            def turn(i, u):
                pe.wait_ge(exp_ready, i * NU + u + 1)
                if u >= 2:
                    pe.wait_ge(probsT_ready[u % 2], i * (NU // 2) + u // 2)
                for c in range(KC):
                    ins = pe.transpose(probsT_p[u % 2][:, c * P:(c + 1) * P], probs[:, u % 2, c * P:(c + 1) * P], sh.ident[:])
                ins.then_inc(probsT_ps, 1)

            def values(i, u):
                h, t = u // TPB, u % TPB
                pe.wait_ge(probsT_ready[u % 2], i * (NU // 2) + u // 2 + 1)
                product(pe, o_p[t][:, h * DH1:(h + 1) * DH1], [probsT[:, u % 2, c] for c in range(KC)],
                        [v[:, c, h * DH1:(h + 1) * DH1] for c in range(KC)]).then_inc(head_done, 1)

            def do_round(i, b, half, end):
                last = end and half == 1
                for u in range(NU):
                    turn(i, u)
                    if u == 1:
                        pe.wait_ge(q_twice, (i + 1) * MR * 2)
                        pe.wait_ge(job_ready, (i + 1) * NJ)
                    if u + 2 < NU or not last:
                        if u + 2 == NU:
                            pe.wait_ge(q_twice, (i + 1) * MR * 2 + 2)
                        scores(i, u + 2)
                    if u >= 1:
                        values(i, u - 1)
                    if u in JOB_AT and not last:
                        j = JOB_AT[u]
                        if end and JOBS[j][0] == "k":
                            pe.wait_ge(w_ready, MR + JOBS[j][1] + 1)
                        job(i + 1, j)
                values(i, NU - 1)
                if not last:
                    job(i + 1, NJ - 2)
                    job(i + 1, NJ - 1)
                for t in range(TPB):
                    pe.wait_ge(att_ready, i * TPB + t + 1)
                    pe.wait_ge(probsT_ready[t], (i + 1) * (NU // 2))
                    for m in range(MR):
                        ins = pe.transpose(attT_p[t][:, m * P:(m + 1) * P], att[:, t, m * P:(m + 1) * P], sh.ident[:])
                    ins.then_inc(attT_ps, 1)
                for t in range(TPB):
                    pe.wait_ge(attT_ready, i * TPB + t + 1)
                    if t == 0 and not last:
                        pe.wait_ge(job_ready, (i + 1) * NJ + NJ - 1)
                    ins = product(pe, out_p[:, t * D:(t + 1) * D], [attT[:, t, m] for m in range(MR)],
                                  [wo[:, half * MR + m] for m in range(MR)])
                ins.then_inc(out_ps, 1)

            pe.wait_ge(s_loaded, 16 * len(SMALL))
            for g in range(NT // GROUP):
                pe.wait_ge(xn_ready, 2 * g + 2)
                for c in range(KD):
                    for n in range(2):
                        for qt in range(4):
                            ins = pe.transpose(bank[4 * g + 2 * c + n][:, qt * P:(qt + 1) * P], xn[:, 4 * n + qt, c * P:(c + 1) * P],
                                               sh.ident[:])
                        ins.then_inc(xnT_ps, 1)
            pe.wait_ge(xnT_ready, NT // GROUP * 2 * KD)
            for j in range(NJ):
                if JOBS[j][0] == "k":
                    pe.wait_ge(w_ready, JOBS[j][1] + 1)
                job(0, j, first=True)
            pe.wait_ge(q_twice, 2)
            scores(0, 0, first=True)
            scores(0, 1, first=True)
            rounds(pe, do_round)


def stage_l1_ffn(nc, sh, d):
    with ExitStack() as ctx:
        def sb(name, shape, dt=F32):
            return ctx.enter_context(nc.sbuf_tensor("d_" + name, shape, dt))

        KF = F1 // P
        FB, HB = F1 // R1, D // R1
        NCH = 16
        FPC = FB // NCH
        gw1, gb1 = sb("gw1", [P, KD, D]), sb("gb1", [P, KD])
        gw2r, gb2r = sb("gw2r", [P, KD, P]), sb("gb2r", [P, 1])
        gw2a, gb2a = sb("gw2a", [P, KD, E1 + 1]), sb("gb2a", [E1 + 1, 1])
        tb1, tb2 = sb("tb1", [E1 + 1, F1]), sb("tb2", [E1 + 1, D])
        w1, w2 = sb("w1", [P, KD, F1]), sb("w2", [P, KF, D])
        pieces = sb("pieces", [P, 4 * 1024])
        tw = [pieces[:, i * 1024:(i + 1) * 1024] for i in range(4)]
        w1b = pieces[:, 0:KD * F1].rearrange("p (c f) -> p c f", c=KD)
        w2b = pieces[:, KD * F1:KD * F1 + KF * D].rearrange("p (c f) -> p c f", c=KF)
        m1, m2 = sb("m1", [P, KD, B, F1]), sb("m2", [P, KF, B, D])
        xnT = sb("xnT", [P, KD, TOK])
        xn, xTb, hrelu = [m1[:, 0, i, :].rearrange("p (t d) -> p t d", t=2)[:, :, 0:D] for i in range(3)]
        hsum, hsums = sb("hsum", [P, KD]), sb("hsums", [P, KD, B])
        gcol, dup, G, gT = sb("gcol", [P, B]), sb("dup", [P, R1]), sb("G", [P, B, R1]), sb("gT", [E1 + 1, B])
        gTb, mb1, mb1b = sb("gTb", [E1 + 1, P]), sb("mb1", [P, KF, B]), sb("mb1b", [P, KF])
        hT = w1[:].rearrange("p c f -> p (c f)").rearrange("p (c s) -> p c s", c=KF)
        (w_loaded, stats, stats_ready, rstd_ready, xn_ready, xnT_ps, xTb_ready, xnT_kept, hg_ps, relu_done, hsum_kept,
         gates_ps, gates_ready, chain, mb1_ps, mb1_ready, tw_used, merged_ps, merged, w1b_ready, w2b_ready, xb_ready,
         h_ps, gelu_done, out_ps, x_done, tick) = semaphores(
            nc, ctx, "d", "w_loaded stats stats_ready rstd_ready xn_ready xnT_ps xTb_ready xnT_kept hg_ps relu_done "
            "hsum_kept gates_ps gates_ready chain mb1_ps mb1_ready tw_used merged_ps merged w1b_ready w2b_ready xb_ready "
            "h_ps gelu_done out_ps x_done tick")
        tw_loaded = semaphores(nc, ctx, "d", "tw_loaded0 tw_loaded1 tw_loaded2 tw_loaded3")
        bank = sh.bank
        WEIGHTS = [(gw1, "L1_gw1"), (gb1, "L1_gb1"), (gw2r, "L1_gw2r"), (gb2r, "L1_gb2r"), (gw2a, "L1_gw2a"),
                   (gb2a, "L1_gb2a"), (tb1, "L1_tb1"), (tb2, "L1_tb2"), (w1, "L1_w1"), (w2, "L1_w2")]
        block = ctx.enter_context(nc.Block())

        @block.sync
        def _(sp):
            for dst, name in WEIGHTS:
                sp.dma_start(dst[:], d[name]).then_inc(w_loaded, 16)
            with sp.Fori(0, NCH // 2) as i:
                for k in range(4):
                    sp.wait_ge(tw_used, 4 * i + k + 1)
                    sp.dma_start(tw[k], d["L1_tw1" if k < 2 else "L1_tw2"][:, bass.ds((2 * i + k % 2) * 1024, 1024)])\
                      .then_inc(tw_loaded[k], 16)

        @block.gpsimd
        def _(pool):
            with pool.Fori(0, B) as b:
                layernorm_pool(pool, sh, stats_ready, rstd_ready, b)

        @block.vector
        def _(dve):
            dve.wait_ge(w_loaded, 16 * len(WEIGHTS))
            with dve.Fori(0, B) as b:
                layernorm_vector(dve, sh, lambda t: x_tile(sh, b * TPB + t), xn, stats, stats_ready, rstd_ready, xn_ready, b)
                dve.wait_ge(xTb_ready, b + 1)
                dve.tensor_scalar(xnT[:, :, bass.ds(b * S, S)], xTb, 1.0, None, ALU.mult).then_inc(xnT_kept, 1)
                dve.wait_ge(relu_done, b + 1)
                dve.tensor_scalar(hsums[:, :, bass.ds(b, 1)], hsum[:].unsqueeze(2), 1.0 / S, None, ALU.mult).then_inc(hsum_kept, 1)
            dve.wait_ge(hsum_kept, B)
            dve.tensor_reduce(dup[:], sh.ident[:].rearrange("p (e r) -> p r e", r=R1), AX.X, ALU.add).then_inc(chain, 1)
            dve.wait_ge(gates_ps, 1)
            dve.tensor_scalar(gcol[:], bank[0][:, 0:B], gb2r[:, 0:1], None, ALU.add).then_inc(chain, 1)
            dve.tensor_scalar(gT[:], bank[1][0:E1 + 1, 0:B], gb2a[:, 0:1], None, ALU.add).then_inc(gates_ready, 1)
            dve.wait_ge(chain, 2)
            dve.tensor_tensor(G[:], gcol[:].unsqueeze(2).to_broadcast([P, B, R1]), dup[:].unsqueeze(1).to_broadcast([P, B, R1]),
                              ALU.mult).then_inc(gates_ready, 1)
            dve.wait_ge(mb1_ps, 1)
            dve.tensor_copy(mb1[:].rearrange("p c b -> p (c b)"), bank[2][:, 0:KF * B]).then_inc(mb1_ready, 1)
            dve.sem_inc(merged, 8)
            with dve.Fori(0, NCH // 2) as i:
                for k in range(4):
                    for n in range(2):
                        j = 2 * k + n
                        ch = 2 * i + k % 2
                        if k < 2:
                            cols = bass.ds(ch * FPC * R1, FPC * R1)
                            dst = m1[:, n, :, cols].rearrange("p b (f r) -> p f b r", r=R1)
                            base = w1[:, n, cols].rearrange("p (f r) -> p f r", r=R1)
                        else:
                            cols = bass.ds(ch * R1, R1)
                            dst = m2[:, 4 * n:4 * n + 4, :, cols]
                            base = w2[:, 4 * n:4 * n + 4, cols]
                        dve.wait_ge(merged_ps, 8 * i + j + 1)
                        dve.tensor_tensor(dst, bank[j][:].rearrange("p (f b r) -> p f b r", f=4, b=B),
                                          base.unsqueeze(2).to_broadcast([P, 4, B, R1]), ALU.add).then_inc(merged, 1)
            dve.wait_ge(merged, 8 + 4 * NCH)
            dve.sem_inc(out_ps, 1)
            with dve.Fori(0, B) as b:
                dve.wait_ge(out_ps, b + 1)
                dve.tensor_copy(gTb[:], gT[:, bass.ds(b, 1)].to_broadcast([E1 + 1, P]))
                dve.tensor_copy(mb1b[:], mb1[:, :, bass.ds(b, 1)].rearrange("p c b -> p (c b)")).then_inc(xb_ready, 1)
                dve.tensor_copy(w2b, m2[:, :, bass.ds(b, 1), :].rearrange("p c b d -> p (c b) d")).then_inc(w2b_ready, 1)
                dve.wait_ge(out_ps, b + 2)
                dve.tensor_tensor(x_batch(sh, b), x_batch(sh, b), bank[4][:], ALU.add).then_inc(x_done, 1)

        @block.scalar
        def _(act):
            act.wait_ge(w_loaded, 16 * len(WEIGHTS))
            with act.Fori(0, B) as b:
                act.wait_ge(xnT_ps, b + 1)
                act.activation(xTb, tiles(bank[0][:], KD), ACT.Copy).then_inc(xTb_ready, 1)
                act.wait_ge(hg_ps, b + 1)
                for m in range(KD):
                    ins = act.activation(hrelu[:, m], bank[1][:, m * S:(m + 1) * S], ACT.Relu, bias=gb1[:, m:m + 1],
                                         accum_out=hsum[:, m:m + 1])
                ins.then_inc(relu_done, 1)
            act.wait_ge(merged, 8 + 4 * NCH)
            act.sem_inc(h_ps, 1)
            with act.Fori(0, B) as b:
                act.wait_ge(h_ps, b * (KF // 2) + 1)
                act.sem_inc(tick, 1)
                act.activation(w1b, m1[:, :, bass.ds(b, 1), :].rearrange("p c b d -> p (c b) d"), ACT.Copy).then_inc(w1b_ready, 1)
                act.wait_ge(xb_ready, b + 1)
                for m in range(KF):
                    act.wait_ge(h_ps, b * (KF // 2) + m // 2 + 2)
                    act.activation(hT[:, m], bank[m // 2][:, m % 2 * S:(m % 2 + 1) * S], ACT.Gelu_apprx_tanh,
                                   bias=mb1b[:, m:m + 1]).then_inc(gelu_done, 1)

        @block.tensor
        def _(pe):
            pe.wait_ge(w_loaded, 16 * len(WEIGHTS))
            with pe.Fori(0, B) as b:
                pe.wait_ge(xn_ready, b + 1)
                transpose_batch(pe, sh, bank[0], xn).then_inc(xnT_ps, 1)
                pe.wait_ge(xTb_ready, b + 1)
                for m in range(KD):
                    ins = product(pe, bank[1][:, m * S:(m + 1) * S], [gw1[:, c, m * P:(m + 1) * P] for c in range(KD)],
                                  [xTb[:, c] for c in range(KD)])
                ins.then_inc(hg_ps, 1)
            pe.wait_ge(hsum_kept, B)
            product(pe, bank[0][:, 0:B], [gw2r[:, c] for c in range(KD)], [hsums[:, c] for c in range(KD)])
            product(pe, bank[1][0:E1 + 1, 0:B], [gw2a[:, c] for c in range(KD)], [hsums[:, c] for c in range(KD)]).then_inc(gates_ps, 1)
            pe.wait_ge(gates_ready, 2)
            for m in range(KF):
                ins = pe.matmul(bank[2][:, m * B:(m + 1) * B], tb1[:, m * P:(m + 1) * P], gT[:], start=True, stop=True)
            ins.then_inc(mb1_ps, 1)
            pe.wait_ge(mb1_ready, 1)
            pe.sem_inc(tw_used, 4)
            with pe.Fori(0, NCH // 2) as i:
                for k in range(4):
                    pe.wait_ge(tw_loaded[k], 16 * i + 16)
                    for n in range(2):
                        j = 2 * k + n
                        pe.wait_ge(merged, 8 * i + j + 1)
                        for f in range(4):
                            at = f * D + n * P if k < 2 else (4 * n + f) * P
                            ins = pe.matmul(bank[j][:, f * P:(f + 1) * P], tw[k][:, at:at + P],
                                            G[:].rearrange("p b r -> p (b r)"), start=True, stop=True)
                        ins.then_inc(merged_ps, 1)
                    pe.wait_ge(merged_ps, 8 * i + 2 * k + 2)
                    pe.sem_inc(tw_used, 1)
            pe.wait_ge(merged, 8 + 4 * NCH)
            with pe.Fori(0, B) as b:
                pe.wait_ge(w1b_ready, b + 1)
                for m in range(KF):
                    ins = product(pe, bank[m // 2][:, m % 2 * S:(m % 2 + 1) * S], [w1b[:, c, m * P:(m + 1) * P] for c in range(KD)],
                                  [xnT[:, c, bass.ds(b * S, S)] for c in range(KD)])
                    if m % 2:
                        ins.then_inc(h_ps, 1)
                pe.wait_ge(w2b_ready, b + 1)
                pe.wait_ge(gelu_done, b * KF + KF)
                for t in range(TPB):
                    ins = product(pe, bank[4][:, t * D:(t + 1) * D],
                                  [gTb[:]] + [hT[:, c, t * P:(t + 1) * P] for c in range(KF)], [tb2[:]] + [w2b[:, c] for c in range(KF)])
                ins.then_inc(out_ps, 1)


def stage_l2_attention(nc, sh, d):
    with ExitStack() as ctx:
        def sb(name, shape, dt=F32):
            return ctx.enter_context(nc.sbuf_tensor("e_" + name, shape, dt))

        wq, wk, wv, wg, wo = [sb(n, [P, KD, D]) for n in ("wq", "wk", "wv", "wg", "wo")]
        bq, bk, bg, bgn = [sb(n, [P, KD]) for n in ("bq", "bk", "bg", "bgn")]
        bv, bo = sb("bv", [P, D]), sb("bo", [P, D])
        ctxT = sb("ctxT", [P, KD, S])
        xn, v, probs, xo = [sb(n, [P, TPB, D]) for n in ("xn", "v", "probs", "xo")]
        xnT, qT, kT, gate, probsT, att = [sb(n, [P, KD, S]) for n in ("xnT", "qT", "kT", "gate", "probsT", "att")]
        negmax, sums, rsums = sb("negmax", [P, TPB]), sb("sums", [P, TPB]), sb("rsums", [P, TPB])
        (w_loaded, ctx_loaded, ctx_used, stats, stats_ready, rstd_ready, xn_ready, xnT_ps, xnT_ready, k_ps, v_ps, q_ps,
         g_ps, k_ready, v_ready, q_ready, gate_exp, step, gate_ready, s_ps, max_ready, exp_ready, probs_ready, probsT_ps,
         probsT_ready, att_ps, att_ready, out_ps, out_read, bias_ready) = semaphores(
            nc, ctx, "e", "w_loaded ctx_loaded ctx_used stats stats_ready rstd_ready xn_ready xnT_ps xnT_ready k_ps v_ps "
            "q_ps g_ps k_ready v_ready q_ready gate_exp step gate_ready s_ps max_ready exp_ready probs_ready probsT_ps "
            "probsT_ready att_ps att_ready out_ps out_read bias_ready")
        xnT_p, k_p, v_p, q_p, g_p, s_p, probsT_p, att_p = sh.bank
        out_p = xnT_p
        WEIGHTS = [(wq, "L2_wq"), (wk, "L2_wk"), (wv, "L2_wv"), (wg, "L2_wg"), (wo, "L2_wo"), (bq, "L2_bq"),
                   (bk, "L2_bk"), (bg, "L2_bg"), (bv, "L2_bv"), (bo, "L2_bo")]
        block = ctx.enter_context(nc.Block())

        @block.sync
        def _(sp):
            for dst, name in WEIGHTS:
                sp.dma_start(dst[:], d[name]).then_inc(w_loaded, 16)
            with sp.Fori(0, B) as b:
                sp.wait_ge(ctx_used, b + 1)
                sp.dma_start(ctxT[:], d["ctxT"][:, bass.ds(b * KD, KD), :]).then_inc(ctx_loaded, 16)

        @block.gpsimd
        def _(pool):
            with pool.Fori(0, B) as b:
                layernorm_pool(pool, sh, stats_ready, rstd_ready, b)

        @block.vector
        def _(dve):
            dve.wait_ge(w_loaded, 16 * len(WEIGHTS))
            dve.tensor_scalar(bgn[:], bg[:], -1.0, None, ALU.mult).then_inc(bias_ready, 1)
            with dve.Fori(0, B) as b:
                layernorm_vector(dve, sh, lambda t: x_tile(sh, b * TPB + t), xn, stats, stats_ready, rstd_ready, xn_ready, b)
                dve.wait_ge(v_ps, b + 1)
                dve.tensor_tensor(v[:], tiles(v_p[:]), over_tiles(bv[:]), ALU.add).then_inc(v_ready, 1)
                dve.wait_ge(s_ps, b + 1)
                dve.tensor_reduce(negmax[:], tiles(s_p[:]), AX.X, ALU.max, negate=True).then_inc(max_ready, 1)
                dve.wait_ge(gate_exp, b + 1)
                dve.tensor_scalar(gate[:], gate[:], 1.0, None, ALU.add).then_inc(step, 1)
                dve.wait_ge(step, 2 * b + 1)
                dve.reciprocal(gate[:], gate[:]).then_inc(gate_ready, 1)
                dve.wait_ge(exp_ready, b * TPB + TPB)
                dve.reciprocal(rsums[:], sums[:]).then_inc(step, 1)
                dve.wait_ge(step, 2 * b + 2)
                for t in range(TPB):
                    dve.tensor_scalar(probs[:, t], probs[:, t], rsums[:, t:t + 1], None, ALU.mult).then_inc(probs_ready, 1)
                dve.wait_ge(att_ps, b + 1)
                dve.wait_ge(gate_ready, b + 1)
                dve.tensor_tensor(att[:], tiles(att_p[:], KD), gate[:], ALU.mult).then_inc(att_ready, 1)
                dve.wait_ge(out_ps, b + 1)
                dve.tensor_tensor(xo[:], tiles(out_p[:]), over_tiles(bo[:]), ALU.add).then_inc(out_read, 1)
                dve.wait_ge(out_read, b + 1)
                dve.tensor_tensor(x_batch(sh, b), x_batch(sh, b), xo[:].rearrange("p t d -> p (t d)"), ALU.add)

        @block.scalar
        def _(act):
            act.wait_ge(bias_ready, 1)
            with act.Fori(0, B) as b:
                act.wait_ge(k_ps, b + 1)
                for m in range(KD):
                    ins = act.activation(kT[:, m], k_p[:, m * S:(m + 1) * S], ACT.Identity, bias=bk[:, m:m + 1])
                ins.then_inc(k_ready, 1)
                act.wait_ge(xnT_ps, b + 1)
                act.activation(xnT[:].rearrange("p c s -> p (c s)"), xnT_p[:], ACT.Copy).then_inc(xnT_ready, 1)
                act.wait_ge(q_ps, b + 1)
                for m in range(KD):
                    ins = act.activation(qT[:, m], q_p[:, m * S:(m + 1) * S], ACT.Identity, bias=bq[:, m:m + 1])
                ins.then_inc(q_ready, 1)
                act.wait_ge(g_ps, b + 1)
                for m in range(KD):
                    ins = act.activation(gate[:, m], g_p[:, m * S:(m + 1) * S], ACT.Exp, bias=bgn[:, m:m + 1], scale=-1.0)
                ins.then_inc(gate_exp, 1)
                act.wait_ge(max_ready, b + 1)
                for t in range(TPB):
                    act.activation(probs[:, t], s_p[:, t * S:(t + 1) * S], ACT.Exp, bias=negmax[:, t:t + 1],
                                   accum_out=sums[:, t:t + 1]).then_inc(exp_ready, 1)
                act.wait_ge(probsT_ps, b + 1)
                act.activation(probsT[:].rearrange("p c s -> p (c s)"), probsT_p[:], ACT.Copy).then_inc(probsT_ready, 1)

        @block.tensor
        def _(pe):
            pe.sem_inc(ctx_used, 1)
            pe.wait_ge(w_loaded, 16 * len(WEIGHTS))

            def turned(out, w, src):
                for m in range(KD):
                    ins = product(pe, out[:, m * S:(m + 1) * S], [w[:, c, m * P:(m + 1) * P] for c in range(KD)],
                                  [src[:, c] for c in range(KD)])
                return ins

            with pe.Fori(0, B) as b:
                pe.wait_ge(ctx_loaded, b * 16 + 16)
                pe.wait_ge(xn_ready, b + 1)
                transpose_batch(pe, sh, xnT_p, xn).then_inc(xnT_ps, 1)
                turned(k_p, wk, ctxT).then_inc(k_ps, 1)
                for t in range(TPB):
                    ins = product(pe, v_p[:, t * D:(t + 1) * D], [ctxT[:, c, t * P:(t + 1) * P] for c in range(KD)],
                                  [wv[:, c] for c in range(KD)])
                ins.then_inc(v_ps, 1)
                pe.wait_ge(v_ps, b + 1)
                pe.sem_inc(ctx_used, 1)
                pe.wait_ge(xnT_ready, b + 1)
                turned(q_p, wq, xnT).then_inc(q_ps, 1)
                turned(g_p, wg, xnT).then_inc(g_ps, 1)
                pe.wait_ge(k_ready, b + 1)
                pe.wait_ge(q_ready, b + 1)
                for t in range(TPB):
                    ins = product(pe, s_p[:, t * S:(t + 1) * S], [qT[:, c, t * P:(t + 1) * P] for c in range(KD)],
                                  [kT[:, c] for c in range(KD)])
                ins.then_inc(s_ps, 1)
                pe.wait_ge(probs_ready, b * TPB + TPB)
                transpose_batch(pe, sh, probsT_p, probs).then_inc(probsT_ps, 1)
                pe.wait_ge(v_ready, b + 1)
                pe.wait_ge(probsT_ready, b + 1)
                turned(att_p, v, probsT).then_inc(att_ps, 1)
                pe.wait_ge(att_ready, b + 1)
                for t in range(TPB):
                    ins = product(pe, out_p[:, t * D:(t + 1) * D], [att[:, c, t * P:(t + 1) * P] for c in range(KD)],
                                  [wo[:, c] for c in range(KD)])
                ins.then_inc(out_ps, 1)


def stage_l3_attention(nc, sh, d):
    with ExitStack() as ctx:
        def sb(name, shape, dt=F32):
            return ctx.enter_context(nc.sbuf_tensor("g_" + name, shape, dt))

        wl = sb("wl", [P, 4 * KD, D])
        wcq, wc, wqv = sb("wcq", [P, KD]), sb("wc", [P, KD]), sb("wqv", [P, KD])
        b3, bsum, bl = sb("b3", [P, 3]), sb("bsum", [P, 1]), sb("bl", [P, D])
        ctxT, cx = sb("ctxT", [P, KD, S]), sb("cx", [P, TPB, D])
        xn, probs, xo = [sb(n, [P, TPB, D]) for n in ("xn", "probs", "xo")]
        xnT, lq, probsT, c2qT, cc, cq = [sb(n, [P, KD, S]) for n in ("xnT", "lq", "probsT", "c2qT", "cc", "cq")]
        negmax, sums, rsums, smax = [sb(n, [P, TPB]) for n in ("negmax", "sums", "rsums", "smax")]
        row, rmax, rsum, bcol, q2c = sb("row", [1, S]), sb("rmax", [1, 1]), sb("rsum", [1, 1]), sb("bcol", [P, TPB]), sb("q2c", [P, KD])
        (w_loaded, ctx_loaded, ctx_used, stats, stats_ready, rstd_ready, xn_ready, xnT_ps, xnT_ready, lq_ready, s_ps,
         max_ready, exp_ready, sums_ready, probs_ready, probsT_ps, probsT_ready, c2q_ps, c2q_ready, cc_ready, smax_ready,
         row_ps, rmax_ready, row_exp, rsum_ready, row_ready, bcol_ps, bcol_ready, q2c_ps, q2c_ready, cq_ready, out_ps,
         out_read, bias_ready) = semaphores(
            nc, ctx, "g", "w_loaded ctx_loaded ctx_used stats stats_ready rstd_ready xn_ready xnT_ps xnT_ready lq_ready "
            "s_ps max_ready exp_ready sums_ready probs_ready probsT_ps probsT_ready c2q_ps c2q_ready cc_ready smax_ready "
            "row_ps rmax_ready row_exp rsum_ready row_ready bcol_ps bcol_ready q2c_ps q2c_ready cq_ready out_ps out_read "
            "bias_ready")
        xnT_p, s_p, r_p, probsT_p, c2q_p, row_p, col_p, out_p = sh.bank

        def c2q2(p):
            return p[:, 4:4 + KD]

        WEIGHTS = [(wl, "L3_wl"), (wcq, "L3_wcq"), (wc, "L3_wc"), (wqv, "L3_wqv"), (b3, "L3_b3"), (bl, "L3_bl")]
        block = ctx.enter_context(nc.Block())

        @block.sync
        def _(sp):
            for dst, name in WEIGHTS:
                sp.dma_start(dst[:], d[name]).then_inc(w_loaded, 16)
            with sp.Fori(0, B) as b:
                sp.wait_ge(ctx_used, b + 1)
                sp.dma_start(ctxT[:], d["ctxT"][:, bass.ds(b * KD, KD), :]).then_inc(ctx_loaded, 16)
                sp.dma_start(cx[:], d["ctx"][:, bass.ds(b * TPB, TPB), :]).then_inc(ctx_loaded, 16)

        @block.gpsimd
        def _(pool):
            with pool.Fori(0, B) as b:
                layernorm_pool(pool, sh, stats_ready, rstd_ready, b)

        @block.vector
        def _(dve):
            dve.wait_ge(w_loaded, 16 * len(WEIGHTS))
            dve.tensor_reduce(bsum[:], b3[:], AX.X, ALU.add).then_inc(bias_ready, 1)
            dve.wait_ge(bias_ready, 1)
            with dve.Fori(0, B) as b:
                layernorm_vector(dve, sh, lambda t: x_tile(sh, b * TPB + t), xn, stats, stats_ready, rstd_ready, xn_ready, b)
                dve.wait_ge(xnT_ready, b + 1)
                for c in range(KD):
                    ins = dve.tensor_scalar(lq[:, c], xnT[:, c], wcq[:, c:c + 1], wqv[:, c:c + 1], ALU.mult, ALU.add)
                ins.then_inc(lq_ready, 1)
                dve.wait_ge(s_ps, b + 1)
                dve.tensor_reduce(negmax[:], tiles(s_p[:]), AX.X, ALU.max, negate=True).then_inc(max_ready, 1)
                dve.wait_ge(max_ready, b + 1)
                dve.scalar_tensor_tensor(smax[:], r_p[:, 0:TPB], bsum[:, 0:1], negmax[:], ALU.add, ALU.subtract).then_inc(smax_ready, 1)
                dve.wait_ge(exp_ready, b + 1)
                dve.reciprocal(rsums[:], sums[:]).then_inc(sums_ready, 1)
                dve.wait_ge(sums_ready, b + 1)
                for t in range(TPB):
                    ins = dve.tensor_scalar(probs[:, t], probs[:, t], rsums[:, t:t + 1], None, ALU.mult)
                ins.then_inc(probs_ready, 1)
                dve.wait_ge(row_ps, b + 1)
                dve.tensor_reduce(rmax[:], row_p[0:1, 0:S], AX.X, ALU.max, negate=True).then_inc(rmax_ready, 1)
                dve.wait_ge(row_exp, b + 1)
                dve.reciprocal(rsum[:], rsum[:]).then_inc(rsum_ready, 1)
                dve.wait_ge(rsum_ready, b + 1)
                dve.tensor_scalar(row[:], row[:], rsum[0:1, 0:1], None, ALU.mult).then_inc(row_ready, 1)
                dve.wait_ge(bcol_ps, b + 1)
                dve.tensor_scalar(bcol[:], col_p[:, 0:TPB], 1.0, None, ALU.mult).then_inc(bcol_ready, 1)
                dve.wait_ge(c2q_ready, b + 1)
                dve.tensor_tensor(cc[:], xnT[:], c2qT[:], ALU.mult).then_inc(cc_ready, 1)
                dve.wait_ge(q2c_ps, b + 1)
                dve.tensor_scalar(q2c[:], c2q2(col_p), 1.0, None, ALU.mult).then_inc(q2c_ready, 1)
                dve.wait_ge(q2c_ready, b + 1)
                for c in range(KD):
                    ins = dve.tensor_scalar(cq[:, c], xnT[:, c], q2c[:, c:c + 1], None, ALU.mult)
                ins.then_inc(cq_ready, 1)
                dve.wait_ge(out_ps, b + 1)
                dve.tensor_tensor(xo[:], tiles(out_p[:]), over_tiles(bl[:]), ALU.add).then_inc(out_read, 1)
                dve.wait_ge(out_read, b + 1)
                dve.tensor_tensor(x_batch(sh, b), x_batch(sh, b), xo[:].rearrange("p t d -> p (t d)"), ALU.add)

        @block.scalar
        def _(act):
            with act.Fori(0, B) as b:
                act.wait_ge(xnT_ps, b + 1)
                act.activation(xnT[:].rearrange("p c s -> p (c s)"), xnT_p[:], ACT.Copy).then_inc(xnT_ready, 1)
                act.wait_ge(max_ready, b + 1)
                for t in range(TPB):
                    ins = act.activation(probs[:, t], s_p[:, t * S:(t + 1) * S], ACT.Exp, bias=negmax[:, t:t + 1],
                                         accum_out=sums[:, t:t + 1])
                ins.then_inc(exp_ready, 1)
                act.wait_ge(rmax_ready, b + 1)
                act.activation(row[:], row_p[0:1, 0:S], ACT.Exp, bias=rmax[0:1, 0:1], accum_out=rsum[:]).then_inc(row_exp, 1)
                act.wait_ge(probsT_ps, b + 1)
                act.activation(probsT[:].rearrange("p c s -> p (c s)"), probsT_p[:], ACT.Copy).then_inc(probsT_ready, 1)
                act.wait_ge(c2q_ps, b + 1)
                act.activation(c2qT[:].rearrange("p c s -> p (c s)"), c2q_p[:], ACT.Copy).then_inc(c2q_ready, 1)

        @block.tensor
        def _(pe):
            pe.sem_inc(ctx_used, 1)
            pe.wait_ge(w_loaded, 16 * len(WEIGHTS))
            with pe.Fori(0, B) as b:
                pe.wait_ge(xn_ready, b + 1)
                transpose_batch(pe, sh, xnT_p, xn).then_inc(xnT_ps, 1)
                pe.wait_ge(xnT_ready, b + 1)
                for t in range(TPB):
                    product(pe, r_p[:, t:t + 1], [xnT[:, c, t * P:(t + 1) * P] for c in range(KD)], [wc[:, c:c + 1] for c in range(KD)])
                pe.wait_ge(ctx_loaded, b * 32 + 32)
                pe.wait_ge(lq_ready, b + 1)
                for t in range(TPB):
                    ins = product(pe, s_p[:, t * S:(t + 1) * S], [lq[:, c, t * P:(t + 1) * P] for c in range(KD)],
                                  [ctxT[:, c] for c in range(KD)])
                ins.then_inc(s_ps, 1)
                pe.wait_ge(smax_ready, b + 1)
                for t in range(TPB):
                    ins = pe.matmul(row_p[0:1, t * P:(t + 1) * P], smax[:, t:t + 1], sh.ident[:], start=True, stop=True)
                ins.then_inc(row_ps, 1)
                pe.wait_ge(probs_ready, b + 1)
                transpose_batch(pe, sh, probsT_p, probs).then_inc(probsT_ps, 1)
                pe.wait_ge(row_ready, b + 1)
                for t in range(TPB):
                    ins = pe.matmul(col_p[:, t:t + 1], row[0:1, t * P:(t + 1) * P], sh.ones[0:1, 0:1], start=True, stop=True)
                ins.then_inc(bcol_ps, 1)
                pe.wait_ge(probsT_ready, b + 1)
                for m in range(KD):
                    ins = product(pe, c2q_p[:, m * S:(m + 1) * S], [cx[:, c, m * P:(m + 1) * P] for c in range(TPB)],
                                  [probsT[:, c] for c in range(TPB)])
                ins.then_inc(c2q_ps, 1)
                pe.wait_ge(c2q_ps, b + 1)
                pe.sem_inc(ctx_used, 1)
                pe.wait_ge(bcol_ready, b + 1)
                for m in range(KD):
                    ins = product(pe, c2q2(col_p)[:, m:m + 1], [xn[:, t, m * P:(m + 1) * P] for t in range(TPB)],
                                  [bcol[:, t:t + 1] for t in range(TPB)])
                ins.then_inc(q2c_ps, 1)
                pe.wait_ge(cc_ready, b + 1)
                pe.wait_ge(cq_ready, b + 1)
                for t in range(TPB):
                    tok = slice(t * P, (t + 1) * P)
                    ins = product(pe, out_p[:, t * D:(t + 1) * D],
                                  [src[:, c, tok] for src in (xnT, c2qT, cc, cq) for c in range(KD)], [wl[:, k] for k in range(4 * KD)])
                ins.then_inc(out_ps, 1)


def stage_l2_ffn(nc, sh, d):
    experts(nc, sh, d, "f", "L2", I2, gated=True)


def stage_l3_ffn(nc, sh, d):
    experts(nc, sh, d, "h", "L3", F3, gated=False)


def experts(nc, sh, d, tag, layer, width, gated):
    with ExitStack() as ctx:
        def sb(name, shape, dt=F32):
            return ctx.enter_context(nc.sbuf_tensor(f"{tag}_{name}", shape, dt))

        NC = -(-width // P)
        size = [min(P, width - c * P) for c in range(NC)]
        NIN = 2 if gated else 1
        WIN, WCOLS = NIN * KD * width, NIN * KD * width + NC * D
        BLK, NB = 512, TOK // 512
        packed = [gated and c == NC - 1 for c in range(NC)]
        w_stage = sb("w_stage", [P, WCOLS + (0 if gated else NC)])
        w_split = sb("w_split", [P, 2, 2, WCOLS], F32R)
        bias = sb("bias", [P, 2, NC])

        def w_in(k, kd, c, m):
            at = kd * NIN * width + (NIN * c + m) * P
            return [w_split[:, k, hl, at:at + P] for hl in range(2)]

        def w_out(k, c):
            return [w_split[:, k, hl, WIN + c * D:WIN + (c + 1) * D] for hl in range(2)]

        wr, small = sb("wr", [P, KD, NE]), sb("small", [P, NE])
        if not gated:
            nw, b2, wtsT = sb("nw", [P, KD]), sb("b2", [NE, D]), sb("wtsT", [NE, TOK])
            square, ms, rms = sb("square", [P, GROUP, D]), sb("ms", [P, GROUP]), sb("rms", [P, GROUP])
        iota_i, iota = sb("iota_i", [P, NE], I32), sb("iota", [P, NE])
        work = sb("work", [P, 4, BLK])
        xn, h, act_out = work[:].rearrange("p a (b d) -> p (a b) d", d=D), work[:, 0:2], work[:, 2:4]
        xnT = sb("xnT", [P, 2, KD, TOK], F32R)
        wr_split = sb("wr_split", [P, 2, KD, NE], F32R)
        hT = sb("hT", [P, 2, 2 * NC - (1 if gated else 0), BLK], F32R)
        logits, top, topi, topf = sb("logits", [P, NT, NE]), sb("top", [P, NT, 8]), sb("topi", [P, NT, 8], U32), sb("topf", [P, NT, 8])
        dl, rw1, rw2 = sb("dl", [P, NT]), sb("rw1", [P, NT]), sb("rw2", [P, NT])
        wt1, wt2, wts, wcol = sb("wt1", [P, NT, NE]), sb("wt2", [P, NT, NE]), sb("wts", [P, NT, NE]), sb("wcol", [P, 2, NT])
        (s_loaded, stats, stats_ready, rstd_ready, xn_ready, ms_ready, rms_ready, t_ready, xnT_ps, xnT_high, xnT_kept, logits_ps,
         iota_ready, step, top_ready, exp_ready, wts_ready, wcol_ready, act_ready, h_made, h_high, h_done, in_ps, down_ps,
         acc_done, wtsT_ps, wtsT_ready, bias_ps, w_loaded, w_taken, w_high, w_ready, wr_high, wr_ready) = semaphores(
            nc, ctx, tag, "s_loaded stats stats_ready rstd_ready xn_ready ms_ready rms_ready t_ready xnT_ps xnT_high xnT_kept "
            "logits_ps iota_ready step top_ready exp_ready wts_ready wcol_ready act_ready h_made h_high h_done in_ps down_ps "
            "acc_done wtsT_ps wtsT_ready bias_ps w_loaded w_taken w_high w_ready wr_high wr_ready")
        bank = sh.bank
        in_p = [[bank[0], bank[2]], [bank[1], bank[3]]]
        down_p = [bank[4], bank[5], bank[6], bank[7]]
        SMALL = [(wr, layer + "_wr"), (small, layer + "_small")] + ([] if gated else [(nw, layer + "_nw"), (b2, layer + "_b2")])
        n_step_bias = 9
        STEPS = 2 * NB
        block = ctx.enter_context(nc.Block())

        @block.sync
        def _(sp):
            for dst, name in SMALL:
                sp.dma_start(dst[:], d[name]).then_inc(s_loaded, 16)
            sp.dma_start(w_stage[:], d[layer + "_w"][:, 0]).then_inc(w_loaded, 16)
            with sp.Fori(0, NE - 1) as e:
                sp.wait_ge(w_ready, e + 1)
                sp.dma_start(w_stage[:], d[layer + "_w"][:, bass.ds(e + 1, 1), :].rearrange("p e w -> p (e w)")).then_inc(w_loaded, 16)

        @block.gpsimd
        def _(pool):
            pool.iota(iota_i[:], [[1, NE]], base=0, channel_multiplier=0).then_inc(iota_ready, 1)
            for g in range(NT // GROUP):
                layernorm_pool(pool, sh, stats_ready, rstd_ready, g, n=GROUP)
                if not gated:
                    pool.wait_ge(ms_ready, g + 1)
                    pool.tensor_tensor(rms[:], ms[:], sh.minus_half[:], ALU.pow).then_inc(rms_ready, 1)

            def split(e, k):
                pool.wait_ge(w_loaded, 16 * e + 16)
                pool.sem_inc(w_taken, 1)
                if not gated:
                    pool.tensor_copy(bias[:, k], w_stage[:, WCOLS:WCOLS + NC])
                pool.tensor_copy(w_split[:, k, 0], w_stage[:, 0:WCOLS]).then_inc(w_high, 1)
                pool.wait_ge(w_high, e + 1)
                pool.tensor_tensor(w_split[:, k, 1], w_stage[:, 0:WCOLS], w_split[:, k, 0].bitcast(F32), ALU.subtract).then_inc(w_ready, 1)

            split(0, 0)
            split(1, 1)
            with pool.Fori(1, NE // 2) as i:
                for k in range(2):
                    pool.wait_ge(down_ps, 2 * (STEPS * (i - 1) + (k + 1) * NB))
                    split(2 * i + k, k)

        @block.vector
        def _(dve):
            dve.wait_ge(s_loaded, 16 * len(SMALL))
            dve.tensor_copy(wr_split[:, 0], wr[:]).then_inc(wr_high, 1)
            dve.wait_ge(wr_high, 1)
            dve.tensor_tensor(wr_split[:, 1], wr[:], wr_split[:, 0].bitcast(F32), ALU.subtract).then_inc(wr_ready, 1)
            for g in range(NT // GROUP):
                xg = sh.X[:, g * GROUP * D:(g + 1) * GROUP * D]
                if g:
                    dve.wait_ge(xnT_ps, g * 2 * KD)
                layernorm_vector(dve, sh, lambda t: xg[:, t * D:(t + 1) * D], xn, stats, stats_ready, rstd_ready, xn_ready, g,
                                 n=GROUP)
                if not gated:
                    dve.wait_ge(xn_ready, g + 1)
                    dve.tensor_tensor(xg, xg, xn.rearrange("p t d -> p (t d)"), ALU.add)
                    dve.wait_ge(t_ready, 2 * g + 1)
                    dve.tensor_scalar(ms[:], ms[:], 1.0 / D, RMS_EPS, ALU.mult, ALU.add).then_inc(ms_ready, 1)
                    dve.wait_ge(rms_ready, g + 1)
                    for t in range(GROUP):
                        ins = dve.tensor_scalar(xn[:, t], xn[:, t], rms[:, t:t + 1], None, ALU.mult)
                    ins.then_inc(t_ready, 1)
                for c in range(KD):
                    for n in range(2):
                        dve.wait_ge(xnT_high, (g * KD + c) * 2 + n + 1)
                        at = (g * 2 + n) * 512
                        dve.scalar_tensor_tensor(xnT[:, 1, c, at:at + 512], bank[2 * c + n][:], 1.0 if gated else nw[:, c:c + 1],
                                                 xnT[:, 0, c, at:at + 512].bitcast(F32), ALU.mult, ALU.subtract)\
                           .then_inc(xnT_kept, 1)
            n_step = [0]

            def link(ins):
                n_step[0] += 1
                ins.then_inc(step, 1)
                dve.wait_ge(step, n_step[0])

            dve.wait_ge(iota_ready, 1)
            dve.tensor_copy(iota[:], iota_i[:])
            dve.wait_ge(logits_ps, 1)
            link(dve.tensor_tensor(logits[:], bank[1][:, 0:NT * NE].rearrange("p (t e) -> p t e", e=NE),
                                   small[:].unsqueeze(1).to_broadcast([P, NT, NE]), ALU.add))
            for t in range(NT):
                ins = dve.max(top[:, t], logits[:, t])
            link(ins)
            for t in range(NT):
                ins = dve.max_index(topi[:, t], top[:, t], logits[:, t])
            link(ins)
            dve.tensor_copy(topf[:], topi[:])
            dve.tensor_tensor(dl[:], top[:, :, 1], top[:, :, 0], ALU.subtract).then_inc(top_ready, 1)
            dve.wait_ge(exp_ready, 1)
            link(dve.tensor_scalar(rw1[:], rw2[:], 1.0, None, ALU.add))
            link(dve.reciprocal(rw1[:], rw1[:]))
            link(dve.tensor_tensor(rw2[:], rw2[:], rw1[:], ALU.mult))
            over_e = lambda ap: ap.to_broadcast([P, NT, NE])
            iota_t = iota[:].unsqueeze(1).to_broadcast([P, NT, NE])
            dve.tensor_tensor(wt1[:], iota_t, over_e(topf[:, :, 0:1]), ALU.is_equal)
            link(dve.tensor_tensor(wt2[:], iota_t, over_e(topf[:, :, 1:2]), ALU.is_equal))
            dve.tensor_tensor(wt1[:], wt1[:], over_e(rw1[:].unsqueeze(2)), ALU.mult)
            link(dve.tensor_tensor(wt2[:], wt2[:], over_e(rw2[:].unsqueeze(2)), ALU.mult))
            link(dve.tensor_tensor(wts[:], wt1[:], wt2[:], ALU.add))
            if gated:
                link(dve.memset(wts[:, :, NE - 1:NE], 1.0))
            dve.tensor_scalar(wt1[:], wts[:], 1.0, None, ALU.mult).then_inc(wts_ready, 1)
            if not gated:
                for n in range(NT // 4):
                    dve.wait_ge(wtsT_ps, n + 1)
                    dve.tensor_copy(wtsT[:, n * 512:(n + 1) * 512], bank[4 + n][0:NE, :]).then_inc(wtsT_ready, 1)
                for n in range(NT // 2):
                    dve.wait_ge(bias_ps, n + 1)
                    link(dve.tensor_tensor(sh.X[:, n * 512:(n + 1) * 512], sh.X[:, n * 512:(n + 1) * 512], bank[n % 4][:], ALU.add))

            dve.wait_ge(wts_ready, 1)
            dve.sem_inc(acc_done, 4)
            dve.sem_inc(h_done, 2)
            if gated:
                dve.sem_inc(h_made, 2)
            with dve.Fori(0, NE // 2) as i:
                def accumulate(s, half):
                    a = 2 * s + half
                    dve.wait_ge(down_ps, 2 * STEPS * i + a + 1)
                    dve.wait_ge(acc_done, 2 * STEPS * i + a + 4)
                    for q in range(2):
                        tile = s % NB * 4 + 2 * half + q
                        xt = sh.X[:, tile * D:(tile + 1) * D]
                        ins = dve.scalar_tensor_tensor(xt, down_p[a % 4][:, q * D:(q + 1) * D], wcol[:, s // NB, tile:tile + 1],
                                                       xt, ALU.mult, ALU.add)
                    ins.then_inc(acc_done, 1)

                for s in range(STEPS):
                    if s % NB == 0:
                        dve.tensor_copy(wcol[:, s // NB], wts[:, :, bass.ds(2 * i + s // NB, 1)].rearrange("p t e -> p (t e)"))\
                           .then_inc(wcol_ready, 1)
                        dve.wait_ge(wcol_ready, 2 * i + s // NB + 1)
                    for c in range(NC):
                        j = s * NC + c
                        rows = slice(64, P) if packed[c] else slice(0, P)
                        if gated:
                            dve.wait_ge(act_ready, STEPS * NC * i + j + 1)
                            dve.wait_ge(h_done, STEPS * NC * i + j + 1)
                            if c == 0 and s >= 2:
                                dve.wait_ge(down_ps, 2 * STEPS * i + 2 * (s - 1))
                            dve.tensor_tensor(h[rows, c % 2], in_p[c % 2][0 if packed[c] else 1][rows, :], act_out[rows, c % 2],
                                              ALU.mult).then_inc(h_made, 1)
                        if s >= 1 and c in (2, 3):
                            accumulate(s - 1, c - 2)
                        dve.wait_ge(h_high, STEPS * NC * i + j + 1)
                        dve.tensor_tensor(hT[0:64, s % 2, 2 * c] if packed[c] else hT[:, s % 2, 2 * c + 1], h[rows, c % 2],
                                          hT[rows, s % 2, 2 * c].bitcast(F32), ALU.subtract).then_inc(h_done, 1)
                accumulate(STEPS - 1, 0)
                accumulate(STEPS - 1, 1)
            dve.wait_ge(acc_done, 4 + NE * NB * 2)

        @block.scalar
        def _(act):
            act.wait_ge(s_loaded, 16 * len(SMALL))
            for g in range(NT // GROUP):
                if not gated:
                    act.wait_ge(xn_ready, g + 1)
                    for t in range(GROUP):
                        ins = act.activation(square[:, t], xn[:, t], ACT.Square, accum_out=ms[:, t:t + 1])
                    ins.then_inc(t_ready, 1)
                for c in range(KD):
                    for n in range(2):
                        act.wait_ge(xnT_ps, (g * KD + c) * 2 + n + 1)
                        at = (g * 2 + n) * 512
                        act.activation(xnT[:, 0, c, at:at + 512], bank[2 * c + n][:], ACT.Copy,
                                       scale=1.0 if gated else nw[:, c:c + 1]).then_inc(xnT_high, 1)
            act.wait_ge(top_ready, 1)
            act.activation(rw2[:], dl[:], ACT.Exp).then_inc(exp_ready, 1)
            if not gated:
                act.sem_inc(h_made, 2)
            with act.Fori(0, NE // 2) as i:
                for s in range(STEPS):
                    for c in range(NC):
                        j = s * NC + c
                        act.wait_ge(in_ps, STEPS * NC * i + j + 1)
                        rows = slice(64, P) if packed[c] else slice(0, P)
                        if gated:
                            act.wait_ge(h_made, STEPS * NC * i + j + 1)
                            act.activation(act_out[rows, c % 2], in_p[c % 2][0][0:64 if packed[c] else P, :], ACT.Silu)\
                               .then_inc(act_ready, 1)
                        else:
                            act.wait_ge(h_done, STEPS * NC * i + j + 1)
                            if c == 0 and s >= 2:
                                act.wait_ge(down_ps, 2 * STEPS * i + 2 * (s - 1))
                            act.activation(h[:, c % 2], in_p[c % 2][0][:], ACT.Gelu, bias=bias[:, s // NB, c:c + 1])\
                               .then_inc(h_made, 1)
                        act.wait_ge(h_made, STEPS * NC * i + j + 3)
                        act.activation(hT[rows, s % 2, 2 * c], h[rows, c % 2], ACT.Copy).then_inc(h_high, 1)

        @block.tensor
        def _(pe):
            pe.wait_ge(s_loaded, 16 * len(SMALL))
            for g in range(NT // GROUP):
                pe.wait_ge(xn_ready if gated else t_ready, g + 1 if gated else 2 * g + 2)
                for c in range(KD):
                    for n in range(2):
                        if g:
                            pe.wait_ge(xnT_kept, ((g - 1) * KD + c) * 2 + n + 1)
                        for q in range(4):
                            ins = pe.transpose(bank[2 * c + n][:, q * P:(q + 1) * P], xn[:, 4 * n + q, c * P:(c + 1) * P], sh.ident[:])
                        ins.then_inc(xnT_ps, 1)
            pe.wait_ge(wr_ready, 1)
            pe.wait_ge(xnT_kept, NT // GROUP * 2 * KD)
            for t in range(NT):
                ins = product_full(pe, bank[1][:, t * NE:(t + 1) * NE],
                                   [[xnT[:, hl, c, t * P:(t + 1) * P] for hl in range(2)] for c in range(KD)],
                                   [[wr_split[:, hl, c] for hl in range(2)] for c in range(KD)])
            ins.then_inc(logits_ps, 1)
            pe.wait_ge(wts_ready, 1)
            if not gated:
                for n in range(NT // 4):
                    for q in range(4):
                        ins = pe.transpose(bank[4 + n][0:NE, q * P:(q + 1) * P], wts[:, 4 * n + q], sh.ident[:])
                    ins.then_inc(wtsT_ps, 1)
                pe.wait_ge(wtsT_ready, NT // 4)
                for n in range(NT // 2):
                    if n >= 4:
                        pe.wait_ge(step, n_step_bias + n - 3)
                    for q in range(2):
                        t = 2 * n + q
                        ins = pe.matmul(bank[n % 4][:, q * D:(q + 1) * D], wtsT[:, t * P:(t + 1) * P], b2[:], start=True, stop=True)
                    ins.then_inc(bias_ps, 1)
                pe.wait_ge(step, n_step_bias + NT // 2)
            with pe.Fori(0, NE // 2) as i:
                def down(s):
                    pe.wait_ge(h_done, STEPS * NC * i + (s + 1) * NC + 2)
                    for half in range(2):
                        a = 2 * s + half
                        pe.wait_ge(acc_done, 2 * STEPS * i + a + 1)
                        for q in range(2):
                            tok = slice((2 * half + q) * P, (2 * half + q + 1) * P)
                            out = down_p[a % 4][:, q * D:(q + 1) * D]
                            for c in range(NC):
                                w = w_out(s // NB, c)
                                if packed[c]:
                                    for hl in range(2):
                                        ins = pe.matmul(out, hT[:, s % 2, 2 * c, tok], w[hl], start=False, stop=(hl == 1))
                                else:
                                    high, low = hT[:, s % 2, 2 * c, tok], hT[:, s % 2, 2 * c + 1, tok]
                                    pe.matmul(out, high, w[0], start=(c == 0), stop=False)
                                    pe.matmul(out, high, w[1], start=False, stop=False)
                                    ins = pe.matmul(out, low, w[0], start=False, stop=(c == NC - 1))
                        ins.then_inc(down_ps, 1)

                for s in range(STEPS):
                    if s % NB == 0:
                        pe.wait_ge(w_ready, 2 * i + s // NB + 1)
                    for c in range(NC):
                        j = s * NC + c
                        pe.wait_ge(h_made, STEPS * NC * i + j + 1)
                        for m in range(1 if packed[c] else NIN):
                            tok = slice(s % NB * BLK, (s % NB + 1) * BLK)
                            ins = product_split(pe, in_p[c % 2][m][:], [w_in(s // NB, k, c, m) for k in range(KD)],
                                                [[xnT[:, hl, k, tok] for hl in range(2)] for k in range(KD)])
                        ins.then_inc(in_ps, 1)
                        if c == 1 and s >= 1:
                            down(s - 1)
                down(STEPS - 1)

STAGES = [stage_l0_attention, stage_l0_ffn, stage_l1_attention, stage_l1_ffn,
          stage_l2_attention, stage_l2_ffn, stage_l3_attention, stage_l3_ffn]


def program(nc, d, out, n_stages=99):
    with ExitStack() as ctx:
        def sb(name, shape, dt=F32):
            return ctx.enter_context(nc.sbuf_tensor(name, shape, dt))

        sh = Shared()
        sh.X = sb("X", [P, NT * D])
        sh.ident, sh.ident16 = sb("ident", [P, P]), sb("ident16", [P, P], BF16)
        sh.ones, sh.minus_half = sb("ones", [P, P]), sb("minus_half", [P, GROUP])
        sh.bn6, sh.mv = sb("bn6", [P, GROUP, 6]), sb("mv", [P, GROUP, 2])
        sh.var, sh.rstd = sb("var", [P, GROUP]), sb("rstd", [P, GROUP])
        sh.bank = [ctx.enter_context(nc.psum_tensor(f"bank{i}", [P, 512], F32)) for i in range(8)]
        stage_start(nc, sh, d)
        for stage in STAGES[:n_stages]:
            stage(nc, sh, d)
        stored = ctx.enter_context(nc.semaphore("stored"))
        block = ctx.enter_context(nc.Block())

        @block.sync
        def _(sp):
            sp.dma_start(out, tiles(sh.X[:], NT)).then_inc(stored, 16)
            sp.wait_ge(stored, 16)


def laid_out(inputs):
    import numpy as np

    g = {k: np.asarray(v) for k, v in inputs.items()}

    def rows(w, n=None):
        k, n = w.shape
        return np.ascontiguousarray(w.reshape(k // P, P, n).transpose(1, 0, 2))

    def column(v):
        return np.ascontiguousarray(v.reshape(-1, P).T)

    def everywhere(v):
        return np.ascontiguousarray(np.broadcast_to(v.reshape(1, -1), (P, v.size)))

    def tokens(a):
        return rows(a.reshape(TOK, -1))

    def heads(w):
        w = w.reshape(w.shape[:-1] + (H, 1, DK0))
        return np.broadcast_to(w, w.shape[:-2] + (2, DK0)).reshape(w.shape[:-3] + (H * PAD0,))

    a = {}
    a["x"] = tokens(g["x"])
    a["ctx"] = tokens(g["ctx_1024"])
    a["ctxT"] = np.ascontiguousarray(g["ctx_1024"].reshape(B, S, KD, P).transpose(3, 0, 2, 1).reshape(P, B * KD, S))
    a["mask"] = tokens(g["mask_BxSxS2_ik1"])
    p = "L0_xattn_"
    a["L0_wq"], a["L0_wk"] = rows(heads(g[p + "Wq"])), rows(heads(g[p + "Wk"]))
    a["L0_bq"], a["L0_bk"] = column(heads(g[p + "bq"])), column(heads(g[p + "bk"]))
    a["L0_wv"], a["L0_wo"] = rows(g[p + "Wv"]), rows(g[p + "Wo"])
    a["L0_bv"], a["L0_bo"] = everywhere(g[p + "bv"]), everywhere(g[p + "bo"])
    a["L0_low_rows"] = np.where(np.arange(P) % PAD0 < DK0, 0, -1).astype(np.float32).reshape(P, 1)
    p = "L0_ffn_"
    a["L0_w1"], a["L0_w2"] = rows(g[p + "W1"].T).reshape(P, -1), rows(g[p + "W2"].T).reshape(P, -1)
    a["L0_b1"], a["L0_b2"] = everywhere(g[p + "b1"]), everywhere(g[p + "b2"])
    p = "L1_xattn_"
    ws = (g[p + "Wq"], g[p + "Wkv"][:, :INNER1], g[p + "Wkv"][:, INNER1:], g[p + "Wm"])
    a["L1_w"] = np.stack([rows(w).reshape(P, KD, M1, P).transpose(0, 2, 1, 3) for w in ws], axis=2)
    a["L1_wo"], a["L1_bo"] = rows(g[p + "Wo"]), everywhere(g[p + "bo"])
    a["L1_g"], a["L1_b"] = column(g[p + "ln_g"]), column(g[p + "ln_b"])
    p = "L1_ffn_"
    a["L1_gw1"], a["L1_gb1"] = rows(g[p + "gate_w1"].T), column(g[p + "gate_b1"])
    gw2T = g[p + "gate_w2"].T
    a["L1_gw2r"] = rows(np.repeat(gw2T, R1, axis=1))
    a["L1_gb2r"] = np.repeat(g[p + "gate_b2"], R1).reshape(P, 1)
    a["L1_gw2a"] = rows(np.concatenate([gw2T, np.zeros((D, 1), gw2T.dtype)], axis=1))
    a["L1_gb2a"] = np.concatenate([g[p + "gate_b2"], np.ones(1, gw2T.dtype)]).reshape(E1 + 1, 1)
    a["L1_tb1"] = np.concatenate([g[p + "Tb1"], g[p + "b1"][None]])
    a["L1_tb2"] = np.concatenate([g[p + "Tb2"], g[p + "b2"][None]])
    a["L1_w1"], a["L1_w2"] = rows(g[p + "W1"].T), rows(g[p + "W2"].T)
    blocks = lambda w: np.ascontiguousarray(w.reshape(E1, -1, R1, w.shape[2]).transpose(0, 2, 1, 3)).reshape(P, -1)
    a["L1_tw1"], a["L1_tw2"] = blocks(g[p + "TW1"]), blocks(g[p + "TW2"])
    p = "L2_xattn_"
    for n in ("q", "k", "v", "g", "o"):
        a["L2_w" + n] = rows(g[p + "W" + n])
        a["L2_b" + n] = everywhere(g[p + "b" + n]) if n in "vo" else column(g[p + "b" + n])
    p = "L2_ffn_"
    wr = np.concatenate([g[p + "wr"].T, np.zeros((D, NE - E2), np.float32)], axis=1)
    a["L2_wr"] = rows(wr)
    a["L2_small"] = everywhere(np.concatenate([g[p + "rb"], np.full(NE - E2, NEVER, np.float32)]))

    def expert(w_in, w_out, tail=()):
        width = w_out.shape[1]
        whole = width // P * P
        cols = [w[c:c + P] for c in range(0, whole, P) for w in w_in] + [w[whole:] for w in w_in]
        out = np.concatenate([w_out.T[:whole], w_out.T[whole:], w_out.T[whole:]])
        return np.concatenate([rows(np.concatenate(cols).T).reshape(P, -1), rows(out).reshape(P, -1), *tail], axis=1)

    a["L2_w"] = np.stack([expert([g[p + "rg"][e], g[p + "ru"][e]], g[p + "rd"][e]) for e in range(E2)]
                         + [expert([g[p + "sg"], g[p + "su"]], g[p + "sd"])], axis=1)
    p = "L3_xattn_"
    a["L3_wl"], a["L3_bl"] = rows(g[p + "W_l"].T), everywhere(g[p + "b_l"])
    a["L3_wcq"], a["L3_wc"], a["L3_wqv"] = column(g[p + "w_cq"]), column(g[p + "w_c"]), column(g[p + "w_q"])
    a["L3_b3"] = everywhere(np.stack([g[p + "b_c"], g[p + "b_q"], g[p + "b_cq"]]))
    p = "L3_ffn_"
    a["L3_nw"], a["L3_wr"] = column(g[p + "norm_weight"]), rows(g[p + "gate_w"].T)
    a["L3_small"], a["L3_b2"] = np.zeros((P, NE), np.float32), g[p + "b2"]
    a["L3_w"] = np.stack([expert([g[p + "w1"][e]], g[p + "w2"][e], [column(g[p + "b1"][e])]) for e in range(E3)], axis=1)
    return {k: np.ascontiguousarray(v) for k, v in a.items()}


def kernel(**inputs):
    import numpy as np
    import concourse.bacc as bacc
    from concourse.bass_utils import run_bass_kernel_spmd

    nc = bacc.Bacc("TRN2", target_bir_lowering=False, num_devices=1)
    arrays = laid_out(inputs)
    d = {name: nc.dram_tensor("in_" + name, a.shape, mybir.dt.from_np(a.dtype), kind="ExternalInput").ap()
         for name, a in arrays.items()}
    out = nc.dram_tensor("out_x", (P, NT, D), F32, kind="ExternalOutput").ap()
    program(nc, d, out)
    r = run_bass_kernel_spmd(nc, [{"in_" + name: a for name, a in arrays.items()}], core_ids=[0])
    return np.ascontiguousarray(r.results[0]["out_x"].transpose(1, 0, 2)).reshape(B, S, D)
```

```python
from contextlib import ExitStack

import concourse.bass as bass
from concourse import mybir

F32 = mybir.dt.float32
F32R = mybir.dt.float32r
BF16 = mybir.dt.bfloat16
I32 = mybir.dt.int32
U32 = mybir.dt.uint32
ALU = mybir.AluOpType
ACT = mybir.ActivationFunctionType
AX = mybir.AxisListType

P = 128
B, S, D = 8, 256, 256
TOK = B * S
NT = TOK // P
TPB = S // P
GROUP = NT // 2
KD = D // P
H = 16
DK0, PAD0 = D // H, 32
M0 = H * PAD0 // P
DH1, INNER1 = 64, H * 64
M1 = INNER1 // P
F0, F1 = 1024, 1024
E1, R1 = 8, 16
I2, E2 = 704, 7
F3, E3 = 512, 8
NE = 8
LN_EPS = 1e-5
RMS_EPS = 1e-6
QB = 127.0
QEPS = 1e-5
ROUND = 1.5 * 2.0 ** 23
MASKED = -(2.0 ** 30)
NEVER = -3.0e38


class Shared:
    pass


def semaphores(nc, ctx, stage, names):
    names = names.split()
    free = sorted(nc.free_semaphores)
    first = next(n for n in free if all(n + i in free for i in range(len(names))))
    sems = [nc.alloc_semaphore(f"{stage}_{n}", first + i) for i, n in enumerate(names)]

    def end():
        nc.all_engine_barrier(sems_to_clear=range(first, first + len(sems)))
        for s in sems:
            nc.release_semaphore(s)

    ctx.callback(end)
    return sems


def x_tile(sh, t):
    return sh.X[:, bass.ds(t * D, D)]


def x_batch(sh, b):
    return sh.X[:, bass.ds(b * TPB * D, TPB * D)]


def tiles(ap, n=TPB):
    return ap.rearrange("p (t d) -> p t d", t=n)


def over_tiles(ap, n=TPB):
    return ap.unsqueeze(1).to_broadcast([P, n, ap.shape[1]])


def layernorm_vector(dve, sh, src, dst, stats, stats_ready, rstd_ready, normed, b, eps=LN_EPS, per=1, k=0, n=TPB):
    layernorm_statistics(dve, sh, src, stats, stats_ready, b, eps, per, k, n)
    layernorm_apply(dve, sh, src, dst, rstd_ready, normed, b, per, k, n)


def layernorm_statistics(dve, sh, src, stats, stats_ready, b, eps=LN_EPS, per=1, k=0, n=TPB):
    for t in range(n):
        ins = dve.bn_stats(sh.bn6[:, t, :], src(t))
    ins.then_inc(stats, 1)
    dve.wait_ge(stats, b * (3 * per) + 3 * k + 1)
    dve.sem_inc(stats, 1)
    for t in range(n):
        ins = dve.bn_aggr(sh.mv[:, t, :], sh.bn6[:, t, :])
    ins.then_inc(stats, 1)
    dve.wait_ge(stats, b * (3 * per) + 3 * k + 3)
    dve.tensor_scalar(sh.var[:, 0:n], sh.mv[:, 0:n, 1], eps, None, ALU.add).then_inc(stats_ready, 1)


def layernorm_apply(dve, sh, src, dst, rstd_ready, normed, b, per=1, k=0, n=TPB):
    dve.wait_ge(rstd_ready, b * per + k + 1)
    for t in range(n):
        ins = dve.tensor_scalar(dst[:, t, :], src(t), sh.mv[:, t, 0:1], sh.rstd[:, t:t + 1], ALU.subtract, ALU.mult)
    ins.then_inc(normed, 1)


def layernorm_pool(pool, sh, stats_ready, rstd_ready, k, n=TPB):
    pool.wait_ge(stats_ready, k + 1)
    pool.tensor_tensor(sh.rstd[:, 0:n], sh.var[:, 0:n], sh.minus_half[:, 0:n], ALU.pow).then_inc(rstd_ready, 1)


def transpose_batch(pe, sh, out, src, n_rows=TPB, n_cols=KD):
    for c in range(n_cols):
        for t in range(n_rows):
            ins = pe.transpose(out[:, (c * n_rows + t) * P:(c * n_rows + t + 1) * P], src[:, t, c * P:(c + 1) * P], sh.ident[:])
    return ins


def product(pe, out, lhsT, rhs):
    n = len(lhsT)
    for k in range(n):
        ins = pe.matmul(out, lhsT[k], rhs[k], start=(k == 0), stop=(k == n - 1))
    return ins


def product_split(pe, out, lhsT, rhs):
    n = len(lhsT)
    for k in range(n):
        pe.matmul(out, lhsT[k][0], rhs[k][0], start=(k == 0), stop=False)
        pe.matmul(out, lhsT[k][0], rhs[k][1], start=False, stop=False)
        ins = pe.matmul(out, lhsT[k][1], rhs[k][0], start=False, stop=(k == n - 1))
    return ins


def stage_start(nc, sh, d):
    with ExitStack() as ctx:
        zeroed, made = semaphores(nc, ctx, "st", "zeroed made")
        block = ctx.enter_context(nc.Block())

        @block.gpsimd
        def _(pool):
            pool.memset(sh.ident[:], 0.0).then_inc(zeroed, 1)
            pool.wait_ge(zeroed, 1)
            pool.affine_select(out=sh.ident[:], in_=sh.ident[:], compare_op=ALU.not_equal, fill=1.0, base=0,
                               pattern=[[-1, P]], channel_multiplier=1).then_inc(made, 1)
            pool.memset(sh.minus_half[:], -0.5).then_inc(made, 1)
            pool.memset(sh.ones[:], 1.0).then_inc(made, 1)
            pool.wait_ge(made, 3)
            pool.tensor_copy(sh.ident16[:], sh.ident[:]).then_inc(made, 1)
            pool.wait_ge(made, 4)


def stage_l0_attention(nc, sh, d):
    with ExitStack() as ctx:
        def sb(name, shape, dt=F32):
            return ctx.enter_context(nc.sbuf_tensor("a_" + name, shape, dt))

        wq, wk, wv, wo = sb("wq", [P, KD, H * PAD0]), sb("wk", [P, KD, H * PAD0]), sb("wv", [P, KD, H * PAD0]), sb("wo", [P, M0, D])
        wq_split, wk_split = sb("wq_split", [P, 2, KD, H * PAD0], F32R), sb("wk_split", [P, 2, KD, H * PAD0], F32R)
        wv_split = sb("wv_split", [P, 2, KD, H * PAD0], F32R)
        bq, bqs, bk = sb("bq", [P, M0]), sb("bqs", [P, M0]), sb("bk", [P, M0])
        bv, bo, low_rows = sb("bv", [P, H * PAD0]), sb("bo", [P, D]), sb("low_rows", [P, 1])
        ctxT, ctx_split = sb("ctxT", [P, KD, S]), sb("ctx_split", [P, 2, KD, S], F32R)
        mask = sb("mask", [P, TPB, S], I32)
        lowered = sb("lowered", [P, TPB * S])
        xn = sb("xn", [P, TPB, D])
        xnT = sb("xnT", [P, 2, KD, S], F32R)
        q_full, q_high = sb("q_full", [P, 2, S]), sb("q_high", [P, 2, S], F32R)
        qT, kT = sb("qT", [P, M0, S], F32R), sb("kT", [P, 2, M0, S], F32R)
        v = sb("v", [P, TPB, H * PAD0])
        sm, probs, probsT = sb("sm", [P, 4, TPB, S]), sb("probs", [P, 4, TPB, S]), sb("probsT", [P, 2, TPB, S])
        negmax, sums, rsums = sb("negmax", [P, 4, TPB]), sb("sums", [P, 4, TPB]), sb("rsums", [P, 4, TPB])
        attT = sb("attT", [P, M0, S])
        xo = sb("xo", [P, TPB, D])
        (w_loaded, w_high, w_low, ctx_loaded, mask_loaded, ctx_high, ctx_ready, mask_used, stats, stats_ready, rstd_ready,
         xn_ready, xnT_ps, xnT_high, xnT_ready, kq_ps, kq_high, kq_ready, v_ps, v_ready, s_ps, s_masked, max_ready, exp_ready,
         probsT_ps, probsT_ready, head_done, rsums_ready, probs_ready, attT_ready, out_ps, out_read, x_done,
         bias_ready, ctx_taken, first_x_loaded, x_loaded) = semaphores(
            nc, ctx, "a", "w_loaded w_high w_low ctx_loaded mask_loaded ctx_high ctx_ready mask_used stats stats_ready "
            "rstd_ready xn_ready xnT_ps xnT_high xnT_ready kq_ps kq_high kq_ready v_ps v_ready s_ps s_masked max_ready "
            "exp_ready probsT_ps probsT_ready head_done rsums_ready probs_ready attT_ready out_ps out_read x_done "
            "bias_ready ctx_taken first_x_loaded x_loaded")
        bank = sh.bank
        s_p, probsT_p, o_p = [bank[0], bank[1]], [bank[2], bank[3]], [bank[4], bank[5]]
        xnT_p, kq_p, v_p, out_p = bank[6], [bank[7], bank[6]], [bank[7], bank[6]], bank[7]
        WEIGHTS = [(wq, "L0_wq"), (wk, "L0_wk"), (wv, "L0_wv"), (wo, "L0_wo"), (bq, "L0_bq"), (bk, "L0_bk"),
                   (bv, "L0_bv"), (bo, "L0_bo"), (low_rows, "L0_low_rows")]
        SPLITS = [(wq, wq_split), (wk, wk_split), (wv, wv_split)]
        T_AT, KQ_AT = 2, {4: 0, 7: 1, 10: 2, 14: 3}
        block = ctx.enter_context(nc.Block())

        @block.sync
        def _(sp):
            x = tiles(sh.X[:], NT)
            sp.dma_start(x[:, 0:TPB], d["x"][:, 0:TPB]).then_inc(first_x_loaded, 16)
            sp.dma_start(ctxT[:], d["ctxT"][:, 0:KD, :]).then_inc(ctx_loaded, 16)
            for dst, name in WEIGHTS:
                sp.dma_start(dst[:], d[name]).then_inc(w_loaded, 16)
            sp.dma_start(mask[:], d["mask"][:, 0:TPB, :]).then_inc(mask_loaded, 16)
            sp.dma_start(x[:, TPB:NT], d["x"][:, TPB:NT]).then_inc(x_loaded, 16)
            with sp.Fori(1, B) as b:
                sp.wait_ge(ctx_ready, b)
                sp.dma_start(ctxT[:], d["ctxT"][:, bass.ds(b * KD, KD), :]).then_inc(ctx_loaded, 16)
                sp.wait_ge(mask_used, b)
                sp.dma_start(mask[:], d["mask"][:, bass.ds(b * TPB, TPB), :]).then_inc(mask_loaded, 16)

        @block.gpsimd
        def _(pool):
            def split_context(b):
                pool.wait_ge(ctx_loaded, b * 16 + 16)
                pool.sem_inc(ctx_taken, 1)
                pool.tensor_copy(ctx_split[:, 0], ctxT[:]).then_inc(ctx_high, 1)
                pool.wait_ge(ctx_high, b + 1)
                pool.tensor_tensor(ctx_split[:, 1], ctxT[:], ctx_split[:, 0].bitcast(F32), ALU.subtract).then_inc(ctx_ready, 1)

            def normalize(b, h):
                pool.wait_ge(rsums_ready, b * H + h + 1)
                pool.tensor_tensor(probs[:, h % 4], probs[:, h % 4], rsums[:, h % 4].unsqueeze(2).to_broadcast([P, TPB, S]),
                                   ALU.mult).then_inc(probs_ready, 1)

            def batch(b, last):
                for h in range(H):
                    if h + 1 < H or not last:
                        normalize(b, h + 1)
                    if not last and h == T_AT - 2:
                        layernorm_pool(pool, sh, stats_ready, rstd_ready, b + 1)
                        pool.wait_ge(v_ps, (b + 1) * TPB)
                        split_context(b + 1)

            layernorm_pool(pool, sh, stats_ready, rstd_ready, 0)
            split_context(0)
            normalize(0, 0)
            with pool.Fori(0, B - 1) as b:
                batch(b, last=False)
            batch(B - 1, last=True)

        @block.vector
        def _(dve):
            def norm(b):
                layernorm_vector(dve, sh, lambda t: x_tile(sh, b * TPB + t), xn, stats, stats_ready, rstd_ready, xn_ready, b)

            def low_xnT(b):
                dve.wait_ge(xnT_high, b + 1)
                dve.tensor_tensor(xnT[:, 1].rearrange("p c s -> p (c s)"), xnT_p[:],
                                  xnT[:, 0].rearrange("p c s -> p (c s)").bitcast(F32), ALU.subtract).then_inc(xnT_ready, 1)

            def low_kq(b, m):
                dve.wait_ge(kq_high, b * M0 + m + 1)
                dve.scalar_tensor_tensor(kT[:, 1, m], kq_p[m % 2][:, 0:S], bk[:, m:m + 1], kT[:, 0, m].bitcast(F32),
                                         ALU.add, ALU.subtract)
                dve.scalar_tensor_tensor(qT[:, m], q_high[:, m % 2].bitcast(F32), low_rows[:], q_full[:, m % 2],
                                         ALU.mult, ALU.add).then_inc(kq_ready, 1)

            def keep_v(b, t):
                dve.wait_ge(v_ps, b * TPB + t + 1)
                dve.tensor_tensor(v[:, t], v_p[t][:], bv[:], ALU.add).then_inc(v_ready, 1)

            def lower(b):
                dve.wait_ge(mask_loaded, b * 16 + 16)
                dve.tensor_scalar(tiles(lowered[:]), mask[:], 0.0, MASKED, ALU.is_equal, ALU.mult).then_inc(mask_used, 1)
                dve.wait_ge(mask_used, b + 1)

            def row_max(b, h, first=False):
                dve.wait_ge(s_ps, b * H + h + 1)
                if not first:
                    dve.wait_ge(exp_ready, b * H + h - 3)
                dve.tensor_tensor(sm[:, h % 4].rearrange("p t s -> p (t s)"), s_p[h % 2][:], lowered[:], ALU.add)\
                   .then_inc(s_masked, 1)
                dve.wait_ge(s_masked, b * H + h + 1)
                dve.tensor_reduce(negmax[:, h % 4], sm[:, h % 4], AX.X, ALU.max, negate=True).then_inc(max_ready, 1)

            def invert_sums(b, h):
                dve.wait_ge(exp_ready, b * H + h + 1)
                dve.reciprocal(rsums[:, h % 4], sums[:, h % 4]).then_inc(rsums_ready, 1)

            def batch(b, last):
                for h in range(H):
                    if h + 1 < H or not last:
                        invert_sums(b, h + 1)
                    if h + 3 == H and not last:
                        lower(b + 1)
                    if h + 3 < H or not last:
                        row_max(b, h + 3)
                    if last:
                        continue
                    if h == T_AT - 2:
                        norm(b + 1)
                    if h == T_AT + 1:
                        low_xnT(b + 1)
                    if h - 1 in KQ_AT:
                        low_kq(b + 1, KQ_AT[h - 1])
                if not last:
                    for t in range(TPB):
                        keep_v(b + 1, t)
                dve.wait_ge(out_ps, b + 1)
                dve.tensor_tensor(xo[:], tiles(out_p[:]), over_tiles(bo[:]), ALU.add).then_inc(out_read, 1)
                dve.wait_ge(out_read, b + 1)
                dve.tensor_tensor(x_batch(sh, b), x_batch(sh, b), xo[:].rearrange("p t d -> p (t d)"), ALU.add).then_inc(x_done, 1)

            dve.wait_ge(first_x_loaded, 16)
            norm(0)
            dve.wait_ge(w_loaded, 16 * len(WEIGHTS))
            dve.tensor_scalar(bqs[:], bq[:], DK0 ** -0.5, None, ALU.mult).then_inc(bias_ready, 1)
            low_xnT(0)
            for n, (w, w_split) in enumerate(SPLITS):
                dve.wait_ge(w_high, n + 1)
                dve.tensor_tensor(w_split[:, 1], w[:], w_split[:, 0].bitcast(F32), ALU.subtract).then_inc(w_low, 1)
            for m in range(M0):
                low_kq(0, m)
            for t in range(TPB):
                keep_v(0, t)
            lower(0)
            for h in range(3):
                row_max(0, h, first=True)
            invert_sums(0, 0)
            dve.wait_ge(x_loaded, 16)
            with dve.Fori(0, B - 1) as b:
                batch(b, last=False)
            batch(B - 1, last=True)
            dve.wait_ge(x_done, B)

        @block.scalar
        def _(act):
            def high_xnT(b):
                act.wait_ge(xnT_ps, b + 1)
                act.activation(xnT[:, 0].rearrange("p c s -> p (c s)"), xnT_p[:], ACT.Copy).then_inc(xnT_high, 1)

            def high_kq(b, m):
                act.wait_ge(kq_ps, b * M0 + m + 1)
                act.activation(kT[:, 0, m], kq_p[m % 2][:, 0:S], ACT.Identity, bias=bk[:, m:m + 1])
                act.activation(q_full[:, m % 2], kq_p[m % 2][:, S:2 * S], ACT.Identity, bias=bqs[:, m:m + 1], scale=DK0 ** -0.5)
                act.activation(q_high[:, m % 2], kq_p[m % 2][:, S:2 * S], ACT.Identity, bias=bqs[:, m:m + 1],
                               scale=DK0 ** -0.5).then_inc(kq_high, 1)

            def exp(b, h, first=False):
                act.wait_ge(max_ready, b * H + h + 1)
                if not first:
                    act.wait_ge(probsT_ps, b * H + h - 3)
                for t in range(TPB):
                    ins = act.activation(probs[:, h % 4, t], sm[:, h % 4, t], ACT.Exp, bias=negmax[:, h % 4, t:t + 1],
                                         accum_out=sums[:, h % 4, t:t + 1])
                ins.then_inc(exp_ready, 1)

            def keep_attT(b, half):
                act.wait_ge(head_done, b * H + (half + 1) * H // 2)
                act.activation(attT[:, 2 * half:2 * half + 2].rearrange("p c s -> p (c s)"), o_p[half][:], ACT.Copy)\
                   .then_inc(attT_ready, 1)

            def batch(b, last):
                for h in range(H):
                    if h + 2 < H or not last:
                        exp(b, h + 2, first=(h < 2))
                    act.wait_ge(probsT_ps, b * H + h + 1)
                    if h >= 2:
                        act.wait_ge(head_done, b * H + h - 1)
                    act.activation(probsT[:, h % 2].rearrange("p c s -> p (c s)"), probsT_p[h % 2][:], ACT.Copy)\
                       .then_inc(probsT_ready, 1)
                    if h == H // 2 + 1:
                        keep_attT(b, 0)
                    if last:
                        continue
                    if h == T_AT + 1:
                        high_xnT(b + 1)
                    if h - 1 in KQ_AT:
                        high_kq(b + 1, KQ_AT[h - 1])
                keep_attT(b, 1)

            act.wait_ge(w_loaded, 16 * len(WEIGHTS))
            for w, w_split in SPLITS:
                act.activation(w_split[:, 0], w[:], ACT.Copy).then_inc(w_high, 1)
            act.wait_ge(bias_ready, 1)
            high_xnT(0)
            for m in range(M0):
                if m >= 2:
                    act.wait_ge(kq_ready, m - 1)
                high_kq(0, m)
            exp(0, 0, first=True)
            exp(0, 1, first=True)
            with act.Fori(0, B - 1) as b:
                batch(b, last=False)
            batch(B - 1, last=True)

        @block.tensor
        def _(pe):
            def turn_x(b):
                pe.wait_ge(xn_ready, b + 1)
                transpose_batch(pe, sh, xnT_p, xn).then_inc(xnT_ps, 1)

            def project_kq(b, m):
                for w, src, col in ((wk_split, ctx_split, 0), (wq_split, xnT, S)):
                    ins = product_split(pe, kq_p[m % 2][:, col:col + S],
                                        [[w[:, hl, c, m * P:(m + 1) * P] for hl in range(2)] for c in range(KD)],
                                        [[src[:, hl, c] for hl in range(2)] for c in range(KD)])
                ins.then_inc(kq_ps, 1)

            def project_v(b, t):
                product_split(pe, v_p[t][:], [[ctx_split[:, hl, c, t * P:(t + 1) * P] for hl in range(2)] for c in range(KD)],
                              [[wv_split[:, hl, c] for hl in range(2)] for c in range(KD)]).then_inc(v_ps, 1)

            def scores(b, h, first=False):
                r, m = h % 4 * PAD0, h % H // 4
                if not first:
                    pe.wait_ge(s_masked, b * H + h - 1)
                for t in range(TPB):
                    for hl in range(2):
                        ins = pe.matmul(s_p[h % 2][:, t * S:(t + 1) * S], qT[r:r + PAD0, m, t * P:(t + 1) * P],
                                        kT[r:r + PAD0, hl, m], start=(hl == 0), stop=(hl == 1))
                ins.then_inc(s_ps, 1)

            def turn(b, h):
                pe.wait_ge(probs_ready, b * H + h + 1)
                if h >= 2:
                    pe.wait_ge(probsT_ready, b * H + h - 1)
                transpose_batch(pe, sh, probsT_p[h % 2], probs[:, h % 4]).then_inc(probsT_ps, 1)

            def values(b, h):
                pe.wait_ge(probsT_ready, b * H + h + 1)
                r, col = h % 4 * PAD0, h // 4 % 2 * S
                product(pe, o_p[h // 8][r:r + PAD0, col:col + S], [v[:, c, h * PAD0:(h + 1) * PAD0] for c in range(TPB)],
                        [probsT[:, h % 2, c] for c in range(TPB)]).then_inc(head_done, 1)

            def batch(b, last):
                for h in range(H):
                    if h + 3 < H or not last:
                        if h + 3 == H:
                            pe.wait_ge(kq_ready, (b + 1) * M0 + 1)
                        scores(b, h + 3)
                    turn(b, h)
                    if h == 1:
                        pe.wait_ge(v_ready, (b + 1) * TPB)
                    if h >= 1:
                        values(b, h - 1)
                    if last:
                        continue
                    if h == T_AT:
                        turn_x(b + 1)
                    if h in KQ_AT:
                        if KQ_AT[h] == 0:
                            pe.wait_ge(xnT_ready, b + 2)
                            pe.wait_ge(ctx_ready, b + 2)
                            pe.wait_ge(out_read, b)
                        if KQ_AT[h] >= 2:
                            pe.wait_ge(kq_ready, (b + 1) * M0 + KQ_AT[h] - 1)
                        project_kq(b + 1, KQ_AT[h])
                values(b, H - 1)
                if not last:
                    for t in range(TPB):
                        pe.wait_ge(kq_ready, (b + 1) * M0 + 3 + t)
                        project_v(b + 1, t)
                    pe.wait_ge(v_ready, (b + 1) * TPB + 1)
                pe.wait_ge(attT_ready, (b + 1) * 2)
                for t in range(TPB):
                    ins = product(pe, out_p[:, t * D:(t + 1) * D], [attT[:, m, t * P:(t + 1) * P] for m in range(M0)],
                                  [wo[:, m] for m in range(M0)])
                ins.then_inc(out_ps, 1)

            turn_x(0)
            pe.wait_ge(w_loaded, 16 * len(WEIGHTS))
            pe.wait_ge(w_low, len(SPLITS))
            pe.wait_ge(xnT_ready, 1)
            pe.wait_ge(ctx_ready, 1)
            for m in range(M0):
                if m >= 2:
                    pe.wait_ge(kq_ready, m - 1)
                project_kq(0, m)
            for t in range(TPB):
                pe.wait_ge(kq_ready, 3 + t)
                project_v(0, t)
            scores(0, 0, first=True)
            scores(0, 1, first=True)
            scores(0, 2)
            with pe.Fori(0, B - 1) as b:
                batch(b, last=False)
            batch(B - 1, last=True)


def stage_l0_ffn(nc, sh, d):
    with ExitStack() as ctx:
        def sb(name, shape, dt=F32):
            return ctx.enter_context(nc.sbuf_tensor("b_" + name, shape, dt))

        KF = F0 // P
        w, wq = sb("w", [P, 2, KD * F0]), sb("wq", [P, 2, KD * F0], BF16)
        wsum, wscale, winv = sb("wsum", [P, 2]), sb("wscale", [P, 2]), sb("winv", [P, 2])
        b1, b2, unround = sb("b1", [P, F0]), sb("b2", [P, D]), sb("unround", [P, 1])
        xn, xr, xq, xqT = sb("xn", [P, TPB, D]), sb("xr", [P, TPB, D]), sb("xq", [P, TPB, D], BF16), sb("xqT", [P, TPB, D], BF16)
        h, hr, hq = sb("h", [P, TPB, F0]), sb("hr", [P, TPB, F0]), sb("hq", [P, TPB, F0], BF16)
        hqT = sb("hqT", [P, TPB, F0], BF16)
        xa, xinv, xscale = sb("xa", [P, TPB]), sb("xinv", [P, TPB]), sb("xscale", [P, TPB])
        ha, hinv, hscale = sb("ha", [P, TPB]), sb("hinv", [P, TPB]), sb("hscale", [P, TPB])
        xo = sb("xo", [P, TPB, D])
        (w_loaded, chain, sum_ready, total_ps, weights_ready, stats, stats_ready, rstd_ready, xn_ready, x_chain, xr_ready,
         xq_ready, xqT_ps, xqT_ready, h_ps, h_scaled, gelu_done, h_chain, hr_ready, hq_ready, hqT_ps, hqT_ready, out_ps,
         out_read, x_done) = semaphores(
            nc, ctx, "b", "w_loaded chain sum_ready total_ps weights_ready stats stats_ready rstd_ready xn_ready x_chain "
            "xr_ready xq_ready xqT_ps xqT_ready h_ps h_scaled gelu_done h_chain hr_ready hq_ready hqT_ps hqT_ready out_ps "
            "out_read x_done")
        bank = sh.bank
        total_p, xqT_p, h_p = bank[0], bank[0], [[bank[1], bank[2]], [bank[3], bank[4]]]
        hqT_p, out_p = [bank[5], bank[6]], bank[7]
        w1q = wq[:, 0].rearrange("p (c f) -> p c f", c=KD)
        w2q = wq[:, 1].rearrange("p (c f) -> p c f", c=KF)
        block = ctx.enter_context(nc.Block())

        @block.sync
        def _(sp):
            for dst, name in [(w[:, 0], "L0_w1"), (w[:, 1], "L0_w2"), (b1[:], "L0_b1"), (b2[:], "L0_b2")]:
                sp.dma_start(dst, d[name]).then_inc(w_loaded, 16)

        @block.gpsimd
        def _(pool):
            with pool.Fori(0, B) as b:
                layernorm_pool(pool, sh, stats_ready, rstd_ready, b)

        @block.vector
        def _(dve):
            def quantize(b, x, absmax, inv, scale, k, rounded, steps, ready):
                dve.tensor_reduce(absmax[:], x[:], AX.X, ALU.max, apply_absolute_value=True).then_inc(steps, 1)
                dve.wait_ge(steps, b * 5 + 1)
                dve.tensor_scalar(absmax[:], absmax[:], QEPS, None, ALU.max).then_inc(steps, 1)
                dve.wait_ge(steps, b * 5 + 2)
                dve.tensor_scalar(scale[:], absmax[:], wscale[:, k:k + 1], 1.0 / QB, ALU.mult, ALU.mult)
                dve.reciprocal(inv[:], absmax[:]).then_inc(steps, 1)
                dve.wait_ge(steps, b * 5 + 3)
                dve.tensor_scalar(inv[:], inv[:], QB, None, ALU.mult).then_inc(steps, 1)
                dve.wait_ge(steps, b * 5 + 4)
                for t in range(TPB):
                    ins = dve.tensor_scalar(rounded[:, t], x[:, t], inv[:, t:t + 1], QB, ALU.mult, ALU.min)
                ins.then_inc(steps, 1)
                dve.wait_ge(steps, b * 5 + 5)
                dve.tensor_scalar(rounded[:], rounded[:], -QB - 1.0, ROUND, ALU.max, ALU.add).then_inc(ready, 1)

            def quantize_x(b):
                layernorm_vector(dve, sh, lambda t: x_tile(sh, b * TPB + t), xn, stats, stats_ready, rstd_ready, xn_ready, b)
                dve.wait_ge(xn_ready, b + 1)
                quantize(b, xn, xa, xinv, xscale, 0, xr, x_chain, xr_ready)

            def keep_xqT(b):
                dve.wait_ge(xqT_ps, b + 1)
                dve.tensor_copy(xqT[:].rearrange("p t d -> p (t d)"), xqT_p[:].bitcast(BF16)[:, 0:TPB * D]).then_inc(xqT_ready, 1)

            def scale_hidden(b):
                for t in range(TPB):
                    dve.wait_ge(h_ps, b * TPB + t + 1)
                    for n in range(2):
                        ins = dve.scalar_tensor_tensor(h[:, t, n * 512:(n + 1) * 512], h_p[t][n][:], xscale[:, t:t + 1],
                                                       b1[:, n * 512:(n + 1) * 512], ALU.mult, ALU.add)
                    ins.then_inc(h_scaled, 1)

            def batch(b, ahead):
                dve.wait_ge(gelu_done, b * TPB + TPB)
                quantize(b, h, ha, hinv, hscale, 1, hr, h_chain, hr_ready)
                if ahead >= 1:
                    dve.wait_ge(hr_ready, b + 1)
                    scale_hidden(b + 1)
                if ahead >= 2:
                    quantize_x(b + 2)
                dve.wait_ge(out_ps, b + 1)
                for t in range(TPB):
                    ins = dve.scalar_tensor_tensor(xo[:, t], out_p[:, t * D:(t + 1) * D], hscale[:, t:t + 1], b2[:], ALU.mult, ALU.add)
                ins.then_inc(out_read, 1)
                dve.wait_ge(out_read, b + 1)
                dve.tensor_tensor(x_batch(sh, b), x_batch(sh, b), xo[:].rearrange("p t d -> p (t d)"), ALU.add).then_inc(x_done, 1)
                if ahead >= 2:
                    keep_xqT(b + 2)

            dve.memset(unround[:], -ROUND).then_inc(chain, 1)
            dve.wait_ge(w_loaded, 4 * 16)
            dve.tensor_reduce(wsum[:], w[:], AX.X, ALU.add, apply_absolute_value=True).then_inc(sum_ready, 1)
            dve.wait_ge(total_ps, 1)
            dve.tensor_scalar(wscale[:], total_p[:, 0:2], 1.0 / (D * F0), QEPS, ALU.mult, ALU.max).then_inc(chain, 1)
            dve.wait_ge(chain, 2)
            dve.reciprocal(winv[:], wscale[:]).then_inc(chain, 1)
            dve.wait_ge(chain, 3)
            for k in range(2):
                dve.tensor_scalar(w[:, k], w[:, k], winv[:, k:k + 1], ROUND, ALU.mult, ALU.add).then_inc(chain, 1)
            dve.wait_ge(chain, 5)
            dve.tensor_scalar(w[:], w[:], ROUND, 1.0, ALU.subtract, ALU.min).then_inc(chain, 1)
            dve.wait_ge(chain, 6)
            dve.tensor_scalar(wq[:], w[:], -1.0, None, ALU.max).then_inc(weights_ready, 1)
            quantize_x(0)
            keep_xqT(0)
            scale_hidden(0)
            quantize_x(1)
            keep_xqT(1)
            with dve.Fori(0, B - 2) as b:
                batch(b, ahead=2)
            batch(B - 2, ahead=1)
            batch(B - 1, ahead=0)
            dve.wait_ge(x_done, B)

        @block.scalar
        def _(act):
            def integers(b, rounded, q, rounded_ready, ready):
                act.wait_ge(rounded_ready, b + 1)
                act.activation(q[:], rounded[:], ACT.Identity, bias=unround[:, 0:1]).then_inc(ready, 1)

            def gelu(b):
                for t in range(TPB):
                    act.wait_ge(h_scaled, b * TPB + t + 1)
                    act.activation(h[:, t], h[:, t], ACT.Gelu).then_inc(gelu_done, 1)

            def batch(b, ahead):
                integers(b, hr, hq, hr_ready, hq_ready)
                for t in range(TPB):
                    act.wait_ge(hqT_ps, b * TPB + t + 1)
                    act.activation(hqT[:, t], hqT_p[t][:].bitcast(BF16), ACT.Copy).then_inc(hqT_ready, 1)
                if ahead >= 1:
                    gelu(b + 1)
                if ahead >= 2:
                    integers(b + 2, xr, xq, xr_ready, xq_ready)

            act.wait_ge(chain, 1)
            integers(0, xr, xq, xr_ready, xq_ready)
            gelu(0)
            integers(1, xr, xq, xr_ready, xq_ready)
            with act.Fori(0, B - 2) as b:
                batch(b, ahead=2)
            batch(B - 2, ahead=1)
            batch(B - 1, ahead=0)

        @block.tensor
        def _(pe):
            def take_in(b):
                pe.wait_ge(xq_ready, b + 1)
                for t in range(TPB):
                    for c in range(KD):
                        at = (t * KD + c) * P
                        ins = pe.transpose(xqT_p[:].bitcast(BF16)[:, at:at + P], xq[:, t, c * P:(c + 1) * P], sh.ident16[:])
                ins.then_inc(xqT_ps, 1)
                pe.wait_ge(xqT_ready, b + 1)
                pe.wait_ge(h_scaled, b * TPB)
                for t in range(TPB):
                    for n in range(2):
                        ins = product(pe, h_p[t][n][:], [xqT[:, t, c * P:(c + 1) * P] for c in range(KD)],
                                      [w1q[:, c, n * 512:(n + 1) * 512] for c in range(KD)])
                    ins.then_inc(h_ps, 1)

            def batch(b, ahead):
                pe.wait_ge(hq_ready, b + 1)
                for t in range(TPB):
                    for c in range(KF):
                        ins = pe.transpose(hqT_p[t][:].bitcast(BF16)[:, c * P:(c + 1) * P], hq[:, t, c * P:(c + 1) * P], sh.ident16[:])
                    ins.then_inc(hqT_ps, 1)
                pe.wait_ge(out_read, b)
                for t in range(TPB):
                    pe.wait_ge(hqT_ready, b * TPB + t + 1)
                    ins = product(pe, out_p[:, t * D:(t + 1) * D], [hqT[:, t, c * P:(c + 1) * P] for c in range(KF)],
                                  [w2q[:, c] for c in range(KF)])
                ins.then_inc(out_ps, 1)
                if ahead >= 2:
                    take_in(b + 2)

            pe.wait_ge(sum_ready, 1)
            pe.matmul(total_p[:, 0:2], sh.ones[:], wsum[:], start=True, stop=True).then_inc(total_ps, 1)
            pe.wait_ge(weights_ready, 1)
            take_in(0)
            take_in(1)
            with pe.Fori(0, B - 2) as b:
                batch(b, ahead=2)
            batch(B - 2, ahead=1)
            batch(B - 1, ahead=0)


def stage_l1_attention(nc, sh, d):
    with ExitStack() as ctx:
        def sb(name, shape, dt=F32):
            return ctx.enter_context(nc.sbuf_tensor("c_" + name, shape, dt))

        SK = 2 * S
        KC = SK // P
        HALF = DH1
        HR = H // 2
        MR = HR * DH1 // P
        NU = TPB * HR
        NW = 2 * MR
        w_stage = sb("w_stage", [P, 2, 4, KD, P])
        w_split = sb("w_split", [P, 2, 4, KD, MR * P], F32R)
        wo = sb("wo", [P, NW, D])
        gain, shift, bo = sb("gain", [P, KD]), sb("shift", [P, KD]), sb("bo", [P, D])
        ctxT, ctx_split, x_split = sb("ctxT", [P, KD, S]), sb("ctx_split", [P, 2, KD, S], F32R), sb("x_split", [P, 2, KD, S], F32R)
        x1, xn = sb("x1", [P, GROUP, D]), sb("xn", [P, GROUP, D])
        xnT = sb("xnT", [P, KD, TOK])
        q, k = sb("q", [P, 2, HR, S], F32R), sb("k", [P, HR, SK], F32R)
        v = sb("v", [P, KC, HR * DH1])
        probs, probsT = sb("probs", [P, 2, SK]), sb("probsT", [P, 2, KC, P])
        negmax, sums, rsums = sb("negmax", [P, 2]), sb("sums", [P, TPB, HR]), sb("rsums", [P, TPB, HR])
        att, attT = sb("att", [P, TPB, HR * DH1]), sb("attT", [P, TPB, MR, P])
        xo = sb("xo", [P, TPB, D])
        probsT_ready = semaphores(nc, ctx, "c", "probsT_act probsT_dve")
        w_loaded = semaphores(nc, ctx, "c", "w_loaded0 w_loaded1")
        (s_loaded, w_taken, h_taken, w_high, w_ready, ctx_loaded, ctx_high, ctx_ready, x_high, x_ready, stats, stats_ready,
         rstd_ready, xn_ready, xnT_ps, xnT_ready, job_ps, job_high, job_ready, q_twice, s_ps, max_ready, exp_ready, probsT_ps,
         head_done, rsums_ready, att_ready, attT_ps, attT_ready, out_ps, out_read,
         x_done) = semaphores(
            nc, ctx, "c", "s_loaded w_taken h_taken w_high w_ready ctx_loaded ctx_high ctx_ready x_high x_ready stats "
            "stats_ready rstd_ready xn_ready xnT_ps xnT_ready job_ps job_high job_ready q_twice s_ps max_ready exp_ready "
            "probsT_ps head_done rsums_ready att_ready attT_ps attT_ready out_ps out_read x_done")
        bank = sh.bank
        s_p, probsT_p, o_p, job_p = [bank[0], bank[1]], [bank[2], bank[3]], [bank[4], bank[5]], [bank[6], bank[7]]
        attT_p, out_p = [bank[2], bank[3]], bank[6]
        SMALL = [(gain, "L1_g"), (shift, "L1_b"), (bo, "L1_bo"), (wo, "L1_wo")]
        JOBS = [("k", 0, 3), ("q", 0, 4), ("k", 1, 6), ("q", 1, 7), ("v", (0, 0), 9), ("v", (0, 1), 10),
                ("k", 2, 11), ("q", 2, 12), ("k", 3, 14), ("q", 3, 15), ("v", (1, 0), None), ("v", (1, 1), None)]
        NJ = len(JOBS)
        JOB_AT = {step: j for j, (_, _, step) in enumerate(JOBS) if step is not None}
        SPLIT_AT = {1: 0, 4: 1, 9: 2, 12: 3}
        TURN_AT = 4
        Q_JOB = [j for j, (kind, _, _) in enumerate(JOBS) if kind == "q"]

        def v_part(number, r):
            half, pair = number
            return v[:, 2 * pair + r, half * 2 * P:(half + 1) * 2 * P]

        high_rows, low_rows = (slice(0, HALF), slice(HALF, P)), (slice(HALF, P), slice(0, HALF))
        block = ctx.enter_context(nc.Block())

        def rounds(engine, do_round):
            for half in range(2):
                with engine.Fori(0, B - 1) as b:
                    do_round(b + half * B, b, half, False)
                do_round(half * B + B - 1, B - 1, half, True)

        @block.sync
        def _(sp):
            def load_weights(j):
                if j >= 2:
                    sp.wait_ge(w_ready, j - 1)
                sp.dma_start(w_stage[:, j % 2], d["L1_w"][:, j]).then_inc(w_loaded[j % 2], 16)

            def load_context(b):
                sp.dma_start(ctxT[:], d["ctxT"][:, bass.ds(b * KD, KD), :]).then_inc(ctx_loaded, 16)

            for dst, name in SMALL[:3]:
                sp.dma_start(dst[:], d[name]).then_inc(s_loaded, 16)
            load_context(0)
            load_weights(0)
            load_weights(1)
            sp.dma_start(wo[:], d["L1_wo"]).then_inc(s_loaded, 16)
            for j in range(2, MR + 2):
                load_weights(j)
            for half in range(2):
                if half:
                    sp.wait_ge(ctx_ready, B)
                    load_context(0)
                    for j in range(MR + 2, NW):
                        load_weights(j)
                with sp.Fori(1, B) as b:
                    sp.wait_ge(ctx_ready, b + half * B)
                    load_context(b)

        @block.gpsimd
        def _(pool):
            def low_weights(j):
                high, low = [w_split[:, hl, :, :, j % MR * P:(j % MR + 1) * P].rearrange("p n c s -> p (n c) s") for hl in range(2)]
                pool.wait_ge(w_high, j + 1)
                pool.tensor_tensor(low, w_stage[:, j % 2].rearrange("p n c s -> p (n c) s"), high.bitcast(F32), ALU.subtract)\
                    .then_inc(w_ready, 1)

            def low_context(i):
                pool.wait_ge(ctx_high, i + 1)
                pool.tensor_tensor(ctx_split[:, 1], ctxT[:], ctx_split[:, 0].bitcast(F32), ALU.subtract).then_inc(ctx_ready, 1)

            def low_tokens(i, b):
                pool.wait_ge(x_high, i + 1)
                pool.sem_inc(w_taken, 1)
                pool.tensor_tensor(x_split[:, 1], xnT[:, :, bass.ds(b * S, S)], x_split[:, 0].bitcast(F32), ALU.subtract)\
                    .then_inc(x_ready, 1)

            def double_queries(i, m, first=False):
                pool.wait_ge(x_ready, i + 1)
                pool.wait_ge(job_ready, i * NJ + Q_JOB[m] + 1)
                for par in range(2):
                    if par or m or not first:
                        pool.wait_ge(q_twice, (i * MR + m) * 2 + par)
                    pool.sem_inc(w_taken, 1)
                    pool.tensor_copy(q[low_rows[par], :, 2 * m + par], q[high_rows[par], :, 2 * m + par].bitcast(F32))\
                        .then_inc(q_twice, 1)

            def do_round(i, b, half, end):
                new_weights = end and half == 0
                if end and half:
                    return
                pool.wait_ge(q_twice, (i + 1) * MR * 2)
                low_context(i + 1)
                low_tokens(i + 1, 0 if new_weights else b + 1)
                for m in range(MR):
                    if new_weights:
                        if m:
                            pool.wait_ge(q_twice, ((i + 1) * MR + m) * 2)
                        low_weights(MR + m)
                        pool.wait_ge(w_ready, MR + m + 1)
                    double_queries(i + 1, m)

            layernorm_pool(pool, sh, stats_ready, rstd_ready, 0, n=GROUP)
            low_weights(0)
            low_context(0)
            layernorm_pool(pool, sh, stats_ready, rstd_ready, 1, n=GROUP)
            low_weights(1)
            layernorm_pool(pool, sh, stats_ready, rstd_ready, 2, n=GROUP)
            low_tokens(0, 0)
            layernorm_pool(pool, sh, stats_ready, rstd_ready, 3, n=GROUP)
            for m in range(2, MR):
                low_weights(m)
            pool.wait_ge(w_ready, MR)
            for m in range(MR):
                double_queries(0, m, first=True)
            rounds(pool, do_round)

        @block.vector
        def _(dve):
            def low_job(i, j):
                kind, m, _ = JOBS[j]
                dve.wait_ge(job_high, i * NJ + j + 1)
                ps = job_p[j % 2]
                if kind == "k":
                    for par in range(2):
                        hi = high_rows[par]
                        ins = dve.tensor_tensor(k[low_rows[par], 2 * m + par], ps[hi, :], k[hi, 2 * m + par].bitcast(F32), ALU.subtract)
                elif kind == "q":
                    for par in range(2):
                        hi = high_rows[par]
                        ins = dve.scalar_tensor_tensor(q[hi, 1, 2 * m + par], ps[hi, 0:S], DH1 ** -0.5,
                                                       q[hi, 0, 2 * m + par].bitcast(F32), ALU.mult, ALU.subtract)
                else:
                    ins = dve.tensor_copy(v_part(m, 1), ps[:, 2 * P:4 * P])
                ins.then_inc(job_ready, 1)

            def row_max(i, u, first=False):
                dve.wait_ge(s_ps, i * NU + u + 1)
                if not first:
                    dve.wait_ge(exp_ready, i * NU + u - 1)
                dve.tensor_reduce(negmax[:, u % 2:u % 2 + 1], s_p[u % 2][:], AX.X, ALU.max, negate=True).then_inc(max_ready, 1)

            def do_round(i, b, half, end):
                last = end and half == 1
                for u in range(NU):
                    if u + 2 < NU or not last:
                        row_max(i, u + 2)
                    if u % 2:
                        dve.wait_ge(probsT_ps, i * NU + u + 1)
                        if u >= 2:
                            dve.wait_ge(head_done, i * NU + u - 1)
                        dve.tensor_copy(probsT[:, 1].rearrange("p c s -> p (c s)"), probsT_p[1][:]).then_inc(probsT_ready[1], 1)
                    if u - 1 in JOB_AT and not last:
                        low_job(i + 1, JOB_AT[u - 1])
                if not last:
                    low_job(i + 1, NJ - 3)
                dve.wait_ge(exp_ready, i * NU + NU)
                dve.reciprocal(rsums[:], sums[:]).then_inc(rsums_ready, 1)
                dve.wait_ge(rsums_ready, i + 1)
                dve.wait_ge(head_done, i * NU + NU)
                for t in range(TPB):
                    dve.tensor_tensor(att[:, t].rearrange("p (h e) -> p h e", e=DH1),
                                      o_p[t][:].rearrange("p (h e) -> p h e", e=DH1),
                                      rsums[:, t].unsqueeze(2).to_broadcast([P, HR, DH1]), ALU.mult).then_inc(att_ready, 1)
                if not last:
                    low_job(i + 1, NJ - 2)
                    low_job(i + 1, NJ - 1)
                dve.wait_ge(out_ps, i + 1)
                if half == 0:
                    dve.tensor_tensor(xo[:], tiles(out_p[:]), over_tiles(bo[:]), ALU.add).then_inc(out_read, 1)
                    dve.wait_ge(out_read, i + 1)
                    dve.tensor_tensor(x_batch(sh, b), x_batch(sh, b), xo[:].rearrange("p t d -> p (t d)"), ALU.add).then_inc(x_done, 1)
                else:
                    dve.wait_ge(x_done, i - B + 1)
                    dve.tensor_tensor(x_batch(sh, b), x_batch(sh, b), out_p[:], ALU.add).then_inc(out_read, 1)

            def first_norm(g):
                layernorm_vector(dve, sh, lambda t: x_tile(sh, g * GROUP + t), x1, stats, stats_ready, rstd_ready, xn_ready, g,
                                 per=2, n=GROUP)
                dve.wait_ge(xn_ready, 2 * g + 1)
                layernorm_statistics(dve, sh, lambda t: x1[:, t], stats, stats_ready, g, per=2, k=1, n=GROUP)

            def second_norm(g):
                layernorm_apply(dve, sh, lambda t: x1[:, t], xn, rstd_ready, xn_ready, g, per=2, k=1, n=GROUP)

            first_norm(0)
            second_norm(0)
            first_norm(1)
            dve.wait_ge(xnT_ps, 2 * KD)
            dve.wait_ge(s_loaded, 16 * len(SMALL))
            for j in range(NJ):
                if j == 2:
                    second_norm(1)
                low_job(0, j)
            row_max(0, 0, first=True)
            row_max(0, 1, first=True)
            rounds(dve, do_round)
            dve.wait_ge(out_read, 2 * B)

        @block.scalar
        def _(act):
            def high_job(i, j):
                kind, m, _ = JOBS[j]
                act.wait_ge(job_ps, i * NJ + j + 1)
                ps = job_p[j % 2]
                if kind == "k":
                    for par in range(2):
                        hi = high_rows[par]
                        ins = act.activation(k[hi, 2 * m + par], ps[hi, :], ACT.Copy)
                elif kind == "q":
                    for par in range(2):
                        hi = high_rows[par]
                        ins = act.activation(q[hi, 0, 2 * m + par], ps[hi, 0:S], ACT.Copy, scale=DH1 ** -0.5)
                else:
                    ins = act.activation(v_part(m, 0), ps[:, 0:2 * P], ACT.Copy)
                ins.then_inc(job_high, 1)

            def high_weights(j):
                act.wait_ge(w_loaded[j % 2], 16 * (j // 2) + 16)
                act.activation(w_split[:, 0, :, :, j % MR * P:(j % MR + 1) * P].rearrange("p n c s -> p (n c) s"),
                               w_stage[:, j % 2].rearrange("p n c s -> p (n c) s"), ACT.Copy).then_inc(w_high, 1)

            def high_context(i):
                act.wait_ge(ctx_loaded, i * 16 + 16)
                act.sem_inc(h_taken, 1)
                act.activation(ctx_split[:, 0], ctxT[:], ACT.Copy).then_inc(ctx_high, 1)

            def high_tokens(b):
                act.activation(x_split[:, 0], xnT[:, :, bass.ds(b * S, S)], ACT.Copy).then_inc(x_high, 1)

            def exp(i, u, first=False):
                act.wait_ge(max_ready, i * NU + u + 1)
                if not first:
                    act.wait_ge(probsT_ps, i * NU + u - 1)
                if u == NU:
                    act.wait_ge(rsums_ready, i + 1)
                h = u % NU // TPB
                act.activation(probs[:, u % 2], s_p[u % 2][:], ACT.Exp, bias=negmax[:, u % 2:u % 2 + 1],
                               accum_out=sums[:, u % TPB, h:h + 1]).then_inc(exp_ready, 1)

            def do_round(i, b, half, end):
                last = end and half == 1
                for u in range(NU):
                    if u + 1 < NU:
                        exp(i, u + 1, first=(u == 0))
                    if u == 0 and not last:
                        act.wait_ge(job_ps, i * NJ + NJ)
                        high_context(i + 1)
                        high_tokens(0 if end else b + 1)
                    if u % 2 == 0:
                        act.wait_ge(probsT_ps, i * NU + u + 1)
                        if u >= 2:
                            act.wait_ge(head_done, i * NU + u - 1)
                        act.activation(probsT[:, 0].rearrange("p c s -> p (c s)"), probsT_p[0][:], ACT.Copy)\
                           .then_inc(probsT_ready[0], 1)
                    if u - 1 in JOB_AT and not last:
                        high_job(i + 1, JOB_AT[u - 1])
                    if end and not last and u in SPLIT_AT:
                        high_weights(MR + SPLIT_AT[u])
                if not last:
                    high_job(i + 1, NJ - 3)
                    exp(i, NU)
                    high_job(i + 1, NJ - 2)
                    high_job(i + 1, NJ - 1)
                for t in range(TPB):
                    act.wait_ge(attT_ps, i * TPB + t + 1)
                    act.activation(attT[:, t].rearrange("p m s -> p (m s)"), attT_p[t][:], ACT.Copy).then_inc(attT_ready, 1)

            def keep_xnT(g):
                for c in range(KD):
                    for n in range(2):
                        act.wait_ge(xnT_ps, (g * KD + c) * 2 + n + 1)
                        at = (g * 2 + n) * 512
                        act.activation(xnT[:, c, at:at + 512], bank[2 * c + n][:], ACT.Identity, bias=shift[:, c:c + 1],
                                       scale=gain[:, c:c + 1]).then_inc(xnT_ready, 1)

            high_weights(0)
            high_context(0)
            high_weights(1)
            act.wait_ge(s_loaded, 16 * len(SMALL))
            keep_xnT(0)
            act.wait_ge(xnT_ready, 2 * KD)
            high_tokens(0)
            for m in range(2, MR):
                high_weights(m)
            for j in range(NJ):
                if j == TURN_AT:
                    keep_xnT(1)
                high_job(0, j)
            exp(0, 0, first=True)
            rounds(act, do_round)

        @block.tensor
        def _(pe):
            def job(i, j, first=False):
                kind, m, _ = JOBS[j]
                if j == 0:
                    pe.wait_ge(x_ready, i + 1)
                    pe.wait_ge(ctx_ready, i + 1)
                if j >= 2:
                    pe.wait_ge(job_ready, i * NJ + j - 1)
                elif not first:
                    pe.wait_ge(out_read, i - 1)
                ps = job_p[j % 2]
                w = lambda n: [[w_split[:, hl, n, c, m * P:(m + 1) * P] for hl in range(2)] for c in range(KD)]
                src = lambda s: [[s[:, hl, c] for hl in range(2)] for c in range(KD)]
                if kind == "k":
                    product_split(pe, ps[:, 0:S], w(1), src(x_split))
                    ins = product_split(pe, ps[:, S:SK], w(3), src(ctx_split))
                elif kind == "q":
                    ins = product_split(pe, ps[:, 0:S], w(0), src(x_split))
                else:
                    half, pair = m
                    a, n = ((x_split, 2), (ctx_split, 3))[pair]
                    for r in range(2):
                        ins = product_split(pe, ps[:, r * 2 * P:(r + 1) * 2 * P],
                                            [[a[:, hl, c, r * P:(r + 1) * P] for hl in range(2)] for c in range(KD)],
                                            [[w_split[:, hl, n, c, half * 2 * P:(half + 1) * 2 * P] for hl in range(2)]
                                             for c in range(KD)])
                ins.then_inc(job_ps, 1)

            def scores(i, u, first=False):
                h, t = u % NU // TPB, u % TPB
                if not first:
                    pe.wait_ge(exp_ready, i * NU + u - 1)
                for hl in range(2):
                    ins = pe.matmul(s_p[u % 2][:], q[:, hl, h, t * P:(t + 1) * P], k[:, h], start=(hl == 0), stop=(hl == 1))
                ins.then_inc(s_ps, 1)

            def turn(i, u):
                pe.wait_ge(exp_ready, i * NU + u + 1)
                if u >= 2:
                    pe.wait_ge(probsT_ready[u % 2], i * (NU // 2) + u // 2)
                for c in range(KC):
                    ins = pe.transpose(probsT_p[u % 2][:, c * P:(c + 1) * P], probs[:, u % 2, c * P:(c + 1) * P], sh.ident[:])
                ins.then_inc(probsT_ps, 1)

            def values(i, u):
                h, t = u // TPB, u % TPB
                pe.wait_ge(probsT_ready[u % 2], i * (NU // 2) + u // 2 + 1)
                product(pe, o_p[t][:, h * DH1:(h + 1) * DH1], [probsT[:, u % 2, c] for c in range(KC)],
                        [v[:, c, h * DH1:(h + 1) * DH1] for c in range(KC)]).then_inc(head_done, 1)

            def do_round(i, b, half, end):
                last = end and half == 1
                for u in range(NU):
                    turn(i, u)
                    if u == 1:
                        pe.wait_ge(q_twice, (i + 1) * MR * 2)
                        pe.wait_ge(job_ready, (i + 1) * NJ)
                    if u + 2 < NU or not last:
                        if u + 2 == NU:
                            pe.wait_ge(q_twice, (i + 1) * MR * 2 + 2)
                        scores(i, u + 2)
                    if u >= 1:
                        values(i, u - 1)
                    if u in JOB_AT and not last:
                        j = JOB_AT[u]
                        if end and JOBS[j][0] == "k":
                            pe.wait_ge(w_ready, MR + JOBS[j][1] + 1)
                        job(i + 1, j)
                values(i, NU - 1)
                if not last:
                    job(i + 1, NJ - 2)
                    job(i + 1, NJ - 1)
                for t in range(TPB):
                    pe.wait_ge(att_ready, i * TPB + t + 1)
                    pe.wait_ge(probsT_ready[t], (i + 1) * (NU // 2))
                    for m in range(MR):
                        ins = pe.transpose(attT_p[t][:, m * P:(m + 1) * P], att[:, t, m * P:(m + 1) * P], sh.ident[:])
                    ins.then_inc(attT_ps, 1)
                for t in range(TPB):
                    pe.wait_ge(attT_ready, i * TPB + t + 1)
                    if t == 0 and not last:
                        pe.wait_ge(job_ready, (i + 1) * NJ + NJ - 1)
                    ins = product(pe, out_p[:, t * D:(t + 1) * D], [attT[:, t, m] for m in range(MR)],
                                  [wo[:, half * MR + m] for m in range(MR)])
                ins.then_inc(out_ps, 1)

            def turn_tokens(g):
                pe.wait_ge(xn_ready, 2 * g + 2)
                for c in range(KD):
                    for n in range(2):
                        if g:
                            pe.wait_ge(xnT_ready, ((g - 1) * KD + c) * 2 + n + 1)
                        for qt in range(4):
                            ins = pe.transpose(bank[2 * c + n][:, qt * P:(qt + 1) * P], xn[:, 4 * n + qt, c * P:(c + 1) * P],
                                               sh.ident[:])
                        ins.then_inc(xnT_ps, 1)

            turn_tokens(0)
            for j in range(NJ):
                if j == TURN_AT:
                    turn_tokens(1)
                if JOBS[j][0] == "k":
                    pe.wait_ge(w_ready, JOBS[j][1] + 1)
                elif JOBS[j][0] == "v":
                    pe.wait_ge(w_ready, 2 * JOBS[j][1][0] + 2)
                job(0, j, first=True)
            pe.wait_ge(xnT_ready, NT // GROUP * 2 * KD)
            pe.wait_ge(s_loaded, 16 * len(SMALL))
            pe.wait_ge(q_twice, 2)
            scores(0, 0, first=True)
            scores(0, 1, first=True)
            rounds(pe, do_round)


def stage_l1_ffn(nc, sh, d):
    with ExitStack() as ctx:
        def sb(name, shape, dt=F32):
            return ctx.enter_context(nc.sbuf_tensor("d_" + name, shape, dt))

        KF = F1 // P
        FB, HB = F1 // R1, D // R1
        NCH = 16
        FPC = FB // NCH
        gw1, gb1 = sb("gw1", [P, KD, D]), sb("gb1", [P, KD])
        gw2r, gb2r = sb("gw2r", [P, KD, P]), sb("gb2r", [P, 1])
        gw2a, gb2a = sb("gw2a", [P, KD, E1 + 1]), sb("gb2a", [E1 + 1, 1])
        tb1, tb2 = sb("tb1", [E1 + 1, F1]), sb("tb2", [E1 + 1, D])
        w1, w2 = sb("w1", [P, KD, F1]), sb("w2", [P, KF, D])
        pieces = sb("pieces", [P, 4 * 1024])
        tw = [pieces[:, i * 1024:(i + 1) * 1024] for i in range(4)]
        w1b = pieces[:, 0:KD * F1].rearrange("p (c f) -> p c f", c=KD)
        w2b = pieces[:, KD * F1:KD * F1 + KF * D].rearrange("p (c f) -> p c f", c=KF)
        m1, m2 = sb("m1", [P, KD, B, F1]), sb("m2", [P, KF, B, D])
        xnT = sb("xnT", [P, KD, TOK])
        NG = NT // GROUP
        xn = m1[:, 0, 0:2].rearrange("p a (b d) -> p (a b) d", d=D)
        hrelu = m1[:, 0, 4:8].rearrange("p a (b s) -> p (a b) s", s=S)
        hsum, hsums = sb("hsum", [P, KD, B]), sb("hsums", [P, KD, B])
        gcol, dup, G, gT = sb("gcol", [P, B]), sb("dup", [P, R1]), sb("G", [P, B, R1]), sb("gT", [E1 + 1, B])
        gTb, mb1, mb1b = sb("gTb", [E1 + 1, P]), sb("mb1", [P, KF, B]), sb("mb1b", [P, KF])
        hT = w1[:].rearrange("p c f -> p (c f)").rearrange("p (c s) -> p c s", c=KF)
        (w_loaded, stats, stats_ready, rstd_ready, xn_ready, xnT_ps, xnT_act, xnT_dve, hg_ps, relu_done, hsum_kept,
         gates_ps, gates_ready, chain, mb1_ps, mb1_ready, merged_ps, merged, w1b_ready, w2b_ready, xb_ready,
         h_ps, gelu_done, out_ps, x_done, tick) = semaphores(
            nc, ctx, "d", "w_loaded stats stats_ready rstd_ready xn_ready xnT_ps xnT_act xnT_dve hg_ps relu_done "
            "hsum_kept gates_ps gates_ready chain mb1_ps mb1_ready merged_ps merged w1b_ready w2b_ready xb_ready "
            "h_ps gelu_done out_ps x_done tick")
        tw_loaded = semaphores(nc, ctx, "d", "tw_loaded0 tw_loaded1 tw_loaded2 tw_loaded3")
        bank = sh.bank
        WEIGHTS = [(gw1, "L1_gw1"), (gb1, "L1_gb1"), (gw2r, "L1_gw2r"), (gb2r, "L1_gb2r"), (gw2a, "L1_gw2a"),
                   (gb2a, "L1_gb2a"), (tb1, "L1_tb1"), (tb2, "L1_tb2"), (w1, "L1_w1"), (w2, "L1_w2")]
        block = ctx.enter_context(nc.Block())

        @block.sync
        def _(sp):
            for dst, name in WEIGHTS:
                sp.dma_start(dst[:], d[name]).then_inc(w_loaded, 16)

            def load_piece(i, k):
                sp.dma_start(tw[k], d["L1_tw1" if k < 2 else "L1_tw2"][:, bass.ds((2 * i + k % 2) * 1024, 1024)])\
                  .then_inc(tw_loaded[k], 16)

            for k in range(4):
                load_piece(0, k)
            with sp.Fori(1, NCH // 2) as i:
                for k in range(4):
                    sp.wait_ge(merged_ps, 8 * (i - 1) + 2 * k + 2)
                    load_piece(i, k)

        @block.gpsimd
        def _(pool):
            for g in range(NG):
                layernorm_pool(pool, sh, stats_ready, rstd_ready, g, n=GROUP)

        @block.vector
        def _(dve):
            def statistics(g):
                layernorm_statistics(dve, sh, lambda t: x_tile(sh, g * GROUP + t), stats, stats_ready, g, n=GROUP)

            statistics(0)
            for g in range(NG):
                if g:
                    dve.wait_ge(xnT_ps, g * 2 * KD)
                layernorm_apply(dve, sh, lambda t: x_tile(sh, g * GROUP + t), xn, rstd_ready, xn_ready, g, n=GROUP)
                if g + 1 < NG:
                    statistics(g + 1)
                for c in range(KD):
                    dve.wait_ge(xnT_ps, (g * KD + c) * 2 + 2)
                    at = (g * 2 + 1) * 512
                    dve.tensor_copy(xnT[:, c, at:at + 512], bank[2 * c + 1][:]).then_inc(xnT_dve, 1)
            dve.wait_ge(w_loaded, 16 * len(WEIGHTS))
            dve.wait_ge(relu_done, NG * 2 * KD)
            dve.tensor_scalar(hsums[:], hsum[:], 1.0 / S, None, ALU.mult).then_inc(hsum_kept, 1)
            dve.wait_ge(hsum_kept, 1)
            dve.tensor_reduce(dup[:], sh.ident[:].rearrange("p (e r) -> p r e", r=R1), AX.X, ALU.add).then_inc(chain, 1)
            dve.wait_ge(gates_ps, 1)
            dve.tensor_scalar(gcol[:], bank[0][:, 0:B], gb2r[:, 0:1], None, ALU.add).then_inc(chain, 1)
            dve.tensor_scalar(gT[:], bank[1][0:E1 + 1, 0:B], gb2a[:, 0:1], None, ALU.add).then_inc(gates_ready, 1)
            dve.wait_ge(chain, 2)
            dve.tensor_tensor(G[:], gcol[:].unsqueeze(2).to_broadcast([P, B, R1]), dup[:].unsqueeze(1).to_broadcast([P, B, R1]),
                              ALU.mult).then_inc(gates_ready, 1)
            dve.wait_ge(mb1_ps, 1)
            dve.tensor_copy(mb1[:].rearrange("p c b -> p (c b)"), bank[2][:, 0:KF * B]).then_inc(mb1_ready, 1)
            dve.sem_inc(merged, 8)
            with dve.Fori(0, NCH // 2) as i:
                for k in range(4):
                    for n in range(2):
                        j = 2 * k + n
                        ch = 2 * i + k % 2
                        if k < 2:
                            cols = bass.ds(ch * FPC * R1, FPC * R1)
                            dst = m1[:, n, :, cols].rearrange("p b (f r) -> p f b r", r=R1)
                            base = w1[:, n, cols].rearrange("p (f r) -> p f r", r=R1)
                        else:
                            cols = bass.ds(ch * R1, R1)
                            dst = m2[:, 4 * n:4 * n + 4, :, cols]
                            base = w2[:, 4 * n:4 * n + 4, cols]
                        dve.wait_ge(merged_ps, 8 * i + j + 1)
                        dve.tensor_tensor(dst, bank[j][:].rearrange("p (f b r) -> p f b r", f=4, b=B),
                                          base.unsqueeze(2).to_broadcast([P, 4, B, R1]), ALU.add).then_inc(merged, 1)
            dve.wait_ge(merged, 8 + 4 * NCH)
            dve.sem_inc(out_ps, 1)
            with dve.Fori(0, B) as b:
                dve.wait_ge(out_ps, b + 1)
                dve.tensor_copy(gTb[:], gT[:, bass.ds(b, 1)].to_broadcast([E1 + 1, P]))
                dve.tensor_copy(mb1b[:], mb1[:, :, bass.ds(b, 1)].rearrange("p c b -> p (c b)")).then_inc(xb_ready, 1)
                dve.tensor_copy(w2b, m2[:, :, bass.ds(b, 1), :].rearrange("p c b d -> p (c b) d")).then_inc(w2b_ready, 1)
                dve.wait_ge(out_ps, b + 2)
                dve.tensor_tensor(x_batch(sh, b), x_batch(sh, b), bank[4][:], ALU.add).then_inc(x_done, 1)

        @block.scalar
        def _(act):
            for g in range(NG):
                for c in range(KD):
                    act.wait_ge(xnT_ps, (g * KD + c) * 2 + 1)
                    at = g * 2 * 512
                    act.activation(xnT[:, c, at:at + 512], bank[2 * c][:], ACT.Copy).then_inc(xnT_act, 1)
                if g == 0:
                    act.wait_ge(w_loaded, 16 * len(WEIGHTS))
                for n in range(2):
                    for m in range(KD):
                        act.wait_ge(hg_ps, (g * 2 + n) * KD + m + 1)
                        for q in range(2):
                            b = (g * 2 + n) * 2 + q
                            ins = act.activation(hrelu[:, b * KD + m], bank[4 + n * KD + m][:, q * S:(q + 1) * S], ACT.Relu,
                                                 bias=gb1[:, m:m + 1], accum_out=hsum[:, m, b:b + 1])
                        ins.then_inc(relu_done, 1)
            act.wait_ge(merged, 8 + 4 * NCH)
            act.sem_inc(h_ps, 1)
            with act.Fori(0, B) as b:
                act.wait_ge(h_ps, b * (KF // 2) + 1)
                act.sem_inc(tick, 1)
                act.activation(w1b, m1[:, :, bass.ds(b, 1), :].rearrange("p c b d -> p (c b) d"), ACT.Copy).then_inc(w1b_ready, 1)
                act.wait_ge(xb_ready, b + 1)
                for m in range(KF):
                    act.wait_ge(h_ps, b * (KF // 2) + m // 2 + 2)
                    act.activation(hT[:, m], bank[m // 2][:, m % 2 * S:(m % 2 + 1) * S], ACT.Gelu_apprx_tanh,
                                   bias=mb1b[:, m:m + 1]).then_inc(gelu_done, 1)

        @block.tensor
        def _(pe):
            for g in range(NG):
                pe.wait_ge(xn_ready, g + 1)
                for c in range(KD):
                    for n in range(2):
                        if g:
                            pe.wait_ge((xnT_act, xnT_dve)[n], (g - 1) * KD + c + 1)
                        for q in range(4):
                            ins = pe.transpose(bank[2 * c + n][:, q * P:(q + 1) * P], xn[:, 4 * n + q, c * P:(c + 1) * P], sh.ident[:])
                        ins.then_inc(xnT_ps, 1)
                if g == 0:
                    pe.wait_ge(w_loaded, 16 * len(WEIGHTS))
                for n in range(2):
                    pe.wait_ge((xnT_act, xnT_dve)[n], (g + 1) * KD)
                    for m in range(KD):
                        if g:
                            pe.wait_ge(relu_done, ((g - 1) * 2 + n) * KD + m + 1)
                        at = (g * 2 + n) * 512
                        product(pe, bank[4 + n * KD + m][:], [gw1[:, c, m * P:(m + 1) * P] for c in range(KD)],
                                [xnT[:, c, at:at + 512] for c in range(KD)]).then_inc(hg_ps, 1)
            pe.wait_ge(hsum_kept, 1)
            product(pe, bank[0][:, 0:B], [gw2r[:, c] for c in range(KD)], [hsums[:, c] for c in range(KD)])
            product(pe, bank[1][0:E1 + 1, 0:B], [gw2a[:, c] for c in range(KD)], [hsums[:, c] for c in range(KD)]).then_inc(gates_ps, 1)
            pe.wait_ge(gates_ready, 2)
            for m in range(KF):
                ins = pe.matmul(bank[2][:, m * B:(m + 1) * B], tb1[:, m * P:(m + 1) * P], gT[:], start=True, stop=True)
            ins.then_inc(mb1_ps, 1)
            pe.wait_ge(mb1_ready, 1)
            with pe.Fori(0, NCH // 2) as i:
                for k in range(4):
                    pe.wait_ge(tw_loaded[k], 16 * i + 16)
                    for n in range(2):
                        j = 2 * k + n
                        pe.wait_ge(merged, 8 * i + j + 1)
                        for f in range(4):
                            at = f * D + n * P if k < 2 else (4 * n + f) * P
                            ins = pe.matmul(bank[j][:, f * P:(f + 1) * P], tw[k][:, at:at + P],
                                            G[:].rearrange("p b r -> p (b r)"), start=True, stop=True)
                        ins.then_inc(merged_ps, 1)
            pe.wait_ge(merged, 8 + 4 * NCH)
            with pe.Fori(0, B) as b:
                pe.wait_ge(w1b_ready, b + 1)
                for m in range(KF):
                    ins = product(pe, bank[m // 2][:, m % 2 * S:(m % 2 + 1) * S], [w1b[:, c, m * P:(m + 1) * P] for c in range(KD)],
                                  [xnT[:, c, bass.ds(b * S, S)] for c in range(KD)])
                    if m % 2:
                        ins.then_inc(h_ps, 1)
                pe.wait_ge(w2b_ready, b + 1)
                for t in range(TPB):
                    out = bank[4][:, t * D:(t + 1) * D]
                    pe.matmul(out, gTb[:], tb2[:], start=True, stop=False)
                    for c in range(KF):
                        if t == 0:
                            pe.wait_ge(gelu_done, b * KF + c + 1)
                        ins = pe.matmul(out, hT[:, c, t * P:(t + 1) * P], w2b[:, c], start=False, stop=(c == KF - 1))
                ins.then_inc(out_ps, 1)


def stage_l2_attention(nc, sh, d):
    with ExitStack() as ctx:
        def sb(name, shape, dt=F32):
            return ctx.enter_context(nc.sbuf_tensor("e_" + name, shape, dt))

        wq, wk, wv, wg, wo = [sb(n, [P, KD, D]) for n in ("wq", "wk", "wv", "wg", "wo")]
        bq, bk, bg, bgn = [sb(n, [P, KD]) for n in ("bq", "bk", "bg", "bgn")]
        bv, bo = sb("bv", [P, D]), sb("bo", [P, D])
        xn = sb("xn", [P, 2 * TPB, D])
        v, probs, xo = [sb(n, [P, 2, TPB, D]) for n in ("v", "probs", "xo")]
        ctxT, xnT, qT, kT, gate, probsT, att = [sb(n, [P, 2, KD, S]) for n in ("ctxT", "xnT", "qT", "kT", "gate", "probsT", "att")]
        negmax, sums, rsums = sb("negmax", [P, 2, TPB]), sb("sums", [P, 2, TPB]), sb("rsums", [P, 2, TPB])
        w_loaded, bias_ready, stats, stats_ready, rstd_ready, xn_ready = semaphores(
            nc, ctx, "e", "w_loaded bias_ready stats stats_ready rstd_ready xn_ready")
        (ctx_loaded, ctx_used, xnT_ps, xnT_ready, k_ps, v_ps, q_ps, g_ps, k_ready, v_ready, q_ready, gate_exp, gate_step,
         gate_ready, s_ps, max_ready, exp_ready, sums_ready, probs_ready, probsT_ps, probsT_ready, att_ps, att_ready, out_ps,
         out_read) = zip(*[semaphores(
             nc, ctx, f"e{a}", "ctx_loaded ctx_used xnT_ps xnT_ready k_ps v_ps q_ps g_ps k_ready v_ready q_ready gate_exp "
             "gate_step gate_ready s_ps max_ready exp_ready sums_ready probs_ready probsT_ps probsT_ready att_ps att_ready "
             "out_ps out_read") for a in range(2)])
        xnT_p, k_p, v_p, q_p = [(sh.bank[n], sh.bank[4 + n]) for n in range(4)]
        g_p, s_p, probsT_p, att_p, out_p = xnT_p, k_p, v_p, q_p, xnT_p
        WEIGHTS = [(wq, "L2_wq"), (wk, "L2_wk"), (wv, "L2_wv"), (wg, "L2_wg"), (wo, "L2_wo"), (bq, "L2_bq"),
                   (bk, "L2_bk"), (bg, "L2_bg"), (bv, "L2_bv"), (bo, "L2_bo")]
        block = ctx.enter_context(nc.Block())

        @block.sync
        def _(sp):
            for dst, name in WEIGHTS:
                sp.dma_start(dst[:], d[name]).then_inc(w_loaded, 16)
            with sp.Fori(0, B // 2) as i:
                for a in range(2):
                    sp.wait_ge(ctx_used[a], i + 1)
                    sp.dma_start(ctxT[:, a], d["ctxT"][:, bass.ds((2 * i + a) * KD, KD), :]).then_inc(ctx_loaded[a], 16)

        @block.gpsimd
        def _(pool):
            with pool.Fori(0, B // 2) as i:
                layernorm_pool(pool, sh, stats_ready, rstd_ready, i, n=2 * TPB)

        @block.vector
        def _(dve):
            def norm(i):
                layernorm_vector(dve, sh, lambda t: x_tile(sh, i * 2 * TPB + t), xn, stats, stats_ready, rstd_ready, xn_ready, i,
                                 n=2 * TPB)

            def keep_v(i):
                for a in range(2):
                    dve.wait_ge(v_ps[a], i + 1)
                    dve.tensor_tensor(v[:, a], tiles(v_p[a][:]), over_tiles(bv[:]), ALU.add).then_inc(v_ready[a], 1)

            def do_pair(i, last):
                if not last:
                    for a in range(2):
                        dve.wait_ge(xnT_ps[a], i + 1)
                    norm(i + 1)
                for a in range(2):
                    dve.wait_ge(s_ps[a], i + 1)
                    dve.tensor_reduce(negmax[:, a], tiles(s_p[a][:]), AX.X, ALU.max, negate=True).then_inc(max_ready[a], 1)
                    dve.wait_ge(gate_exp[a], i + 1)
                    dve.tensor_scalar(gate[:, a], gate[:, a], 1.0, None, ALU.add).then_inc(gate_step[a], 1)
                for a in range(2):
                    dve.wait_ge(exp_ready[a], i * TPB + TPB)
                    dve.reciprocal(rsums[:, a], sums[:, a]).then_inc(sums_ready[a], 1)
                    dve.wait_ge(sums_ready[a], i + 1)
                    for t in range(TPB):
                        dve.tensor_scalar(probs[:, a, t], probs[:, a, t], rsums[:, a, t:t + 1], None, ALU.mult).then_inc(probs_ready[a], 1)
                for a in range(2):
                    dve.wait_ge(gate_step[a], i + 1)
                    dve.reciprocal(gate[:, a], gate[:, a]).then_inc(gate_ready[a], 1)
                for a in range(2):
                    dve.wait_ge(att_ps[a], i + 1)
                    dve.wait_ge(gate_ready[a], i + 1)
                    dve.tensor_tensor(att[:, a], tiles(att_p[a][:], KD), gate[:, a], ALU.mult).then_inc(att_ready[a], 1)
                if not last:
                    keep_v(i + 1)
                for a in range(2):
                    dve.wait_ge(out_ps[a], i + 1)
                    dve.tensor_tensor(xo[:, a], tiles(out_p[a][:]), over_tiles(bo[:]), ALU.add).then_inc(out_read[a], 1)
                    dve.wait_ge(out_read[a], i + 1)
                    xb = x_batch(sh, 2 * i + a)
                    dve.tensor_tensor(xb, xb, xo[:, a].rearrange("p t d -> p (t d)"), ALU.add)

            norm(0)
            dve.wait_ge(w_loaded, 16 * len(WEIGHTS))
            dve.tensor_scalar(bgn[:], bg[:], -1.0, None, ALU.mult).then_inc(bias_ready, 1)
            keep_v(0)
            with dve.Fori(0, B // 2 - 1) as i:
                do_pair(i, last=False)
            do_pair(B // 2 - 1, last=True)

        @block.scalar
        def _(act):
            act.wait_ge(bias_ready, 1)

            def keep_k(i):
                for a in range(2):
                    act.wait_ge(k_ps[a], i + 1)
                    for m in range(KD):
                        ins = act.activation(kT[:, a, m], k_p[a][:, m * S:(m + 1) * S], ACT.Identity, bias=bk[:, m:m + 1])
                    ins.then_inc(k_ready[a], 1)

            def do_pair(i, last):
                for a in range(2):
                    act.wait_ge(xnT_ps[a], i + 1)
                    act.activation(xnT[:, a].rearrange("p c s -> p (c s)"), xnT_p[a][:], ACT.Copy).then_inc(xnT_ready[a], 1)
                for a in range(2):
                    act.wait_ge(q_ps[a], i + 1)
                    for m in range(KD):
                        ins = act.activation(qT[:, a, m], q_p[a][:, m * S:(m + 1) * S], ACT.Identity, bias=bq[:, m:m + 1])
                    ins.then_inc(q_ready[a], 1)
                    act.wait_ge(g_ps[a], i + 1)
                    for m in range(KD):
                        ins = act.activation(gate[:, a, m], g_p[a][:, m * S:(m + 1) * S], ACT.Exp, bias=bgn[:, m:m + 1], scale=-1.0)
                    ins.then_inc(gate_exp[a], 1)
                for a in range(2):
                    act.wait_ge(max_ready[a], i + 1)
                    for t in range(TPB):
                        act.activation(probs[:, a, t], s_p[a][:, t * S:(t + 1) * S], ACT.Exp, bias=negmax[:, a, t:t + 1],
                                       accum_out=sums[:, a, t:t + 1]).then_inc(exp_ready[a], 1)
                for a in range(2):
                    act.wait_ge(probsT_ps[a], i + 1)
                    act.activation(probsT[:, a].rearrange("p c s -> p (c s)"), probsT_p[a][:], ACT.Copy).then_inc(probsT_ready[a], 1)
                if not last:
                    keep_k(i + 1)

            keep_k(0)
            with act.Fori(0, B // 2 - 1) as i:
                do_pair(i, last=False)
            do_pair(B // 2 - 1, last=True)

        @block.tensor
        def _(pe):
            for a in range(2):
                pe.sem_inc(ctx_used[a], 1)
            pe.wait_ge(w_loaded, 16 * len(WEIGHTS))

            def turned(out, w, src):
                for m in range(KD):
                    ins = product(pe, out[:, m * S:(m + 1) * S], [w[:, c, m * P:(m + 1) * P] for c in range(KD)],
                                  [src[:, c] for c in range(KD)])
                return ins

            def project_k(i):
                for a in range(2):
                    pe.wait_ge(ctx_loaded[a], i * 16 + 16)
                    turned(k_p[a], wk, ctxT[:, a]).then_inc(k_ps[a], 1)

            def project_v(i):
                for a in range(2):
                    for t in range(TPB):
                        ins = product(pe, v_p[a][:, t * D:(t + 1) * D], [ctxT[:, a, c, t * P:(t + 1) * P] for c in range(KD)],
                                      [wv[:, c] for c in range(KD)])
                    ins.then_inc(v_ps[a], 1)

            def do_pair(i, last):
                pe.wait_ge(xn_ready, i + 1)
                for a in range(2):
                    pe.wait_ge(out_read[a], i)
                    transpose_batch(pe, sh, xnT_p[a], xn[:, a * TPB:(a + 1) * TPB]).then_inc(xnT_ps[a], 1)
                for a in range(2):
                    pe.wait_ge(v_ps[a], i + 1)
                    pe.sem_inc(ctx_used[a], 1)
                    pe.wait_ge(xnT_ready[a], i + 1)
                    turned(q_p[a], wq, xnT[:, a]).then_inc(q_ps[a], 1)
                    turned(g_p[a], wg, xnT[:, a]).then_inc(g_ps[a], 1)
                for a in range(2):
                    pe.wait_ge(k_ready[a], i + 1)
                    pe.wait_ge(q_ready[a], i + 1)
                    for t in range(TPB):
                        ins = product(pe, s_p[a][:, t * S:(t + 1) * S], [qT[:, a, c, t * P:(t + 1) * P] for c in range(KD)],
                                      [kT[:, a, c] for c in range(KD)])
                    ins.then_inc(s_ps[a], 1)
                for a in range(2):
                    pe.wait_ge(probs_ready[a], i * TPB + TPB)
                    pe.wait_ge(v_ready[a], i + 1)
                    transpose_batch(pe, sh, probsT_p[a], probs[:, a]).then_inc(probsT_ps[a], 1)
                if not last:
                    project_k(i + 1)
                for a in range(2):
                    pe.wait_ge(probsT_ready[a], i + 1)
                    turned(att_p[a], v[:, a], probsT[:, a]).then_inc(att_ps[a], 1)
                if not last:
                    project_v(i + 1)
                for a in range(2):
                    pe.wait_ge(att_ready[a], i + 1)
                    for t in range(TPB):
                        ins = product(pe, out_p[a][:, t * D:(t + 1) * D], [att[:, a, c, t * P:(t + 1) * P] for c in range(KD)],
                                      [wo[:, c] for c in range(KD)])
                    ins.then_inc(out_ps[a], 1)

            project_k(0)
            project_v(0)
            with pe.Fori(0, B // 2 - 1) as i:
                do_pair(i, last=False)
            do_pair(B // 2 - 1, last=True)


def stage_l3_attention(nc, sh, d):
    with ExitStack() as ctx:
        def sb(name, shape, dt=F32):
            return ctx.enter_context(nc.sbuf_tensor("g_" + name, shape, dt))

        wl = sb("wl", [P, 4 * KD, D])
        wcq, wc, wqv = sb("wcq", [P, KD]), sb("wc", [P, KD]), sb("wqv", [P, KD])
        b3, bsum, bl = sb("b3", [P, 3]), sb("bsum", [P, 1]), sb("bl", [P, D])
        xn = sb("xn", [P, 2 * TPB, D])
        cx, probs, xo = [sb(n, [P, 2, TPB, D]) for n in ("cx", "probs", "xo")]
        ctxT, xnT, lq, probsT, c2qT, cc, cq = [sb(n, [P, 2, KD, S]) for n in ("ctxT", "xnT", "lq", "probsT", "c2qT", "cc", "cq")]
        negmax, sums, rsums, smax, bcol = [sb(n, [P, 2, TPB]) for n in ("negmax", "sums", "rsums", "smax", "bcol")]
        row, rmax, rsum, q2c = sb("row", [1, 2, S]), sb("rmax", [1, 2, 1]), sb("rsum", [1, 2, 1]), sb("q2c", [P, 2, KD])
        w_loaded, bias_ready, stats, stats_ready, rstd_ready, xn_ready = semaphores(
            nc, ctx, "g", "w_loaded bias_ready stats stats_ready rstd_ready xn_ready")
        (ctx_loaded, ctx_used, xnT_ps, xnT_ready, lq_ready, s_ps, max_ready, exp_ready, sums_ready, probs_ready, probsT_ps,
         probsT_ready, c2q_ps, c2q_ready, cc_ready, smax_ready, row_ps, rmax_ready, row_exp, rsum_ready, row_ready, bcol_ps,
         bcol_ready, q2c_ps, q2c_ready, cq_ready, out_ps, out_read) = zip(*[semaphores(
             nc, ctx, f"g{a}", "ctx_loaded ctx_used xnT_ps xnT_ready lq_ready s_ps max_ready exp_ready sums_ready probs_ready "
             "probsT_ps probsT_ready c2q_ps c2q_ready cc_ready smax_ready row_ps rmax_ready row_exp rsum_ready row_ready "
             "bcol_ps bcol_ready q2c_ps q2c_ready cq_ready out_ps out_read") for a in range(2)])
        xnT_p, s_p, probsT_p, small_p = [(sh.bank[n], sh.bank[4 + n]) for n in range(4)]
        c2q_p = xnT_p
        out_p = [(s_p[a][:, 0:D], probsT_p[a][:, 0:D]) for a in range(2)]
        r_p, row_p = [p[:, 0:TPB] for p in small_p], [p[0:1, S:2 * S] for p in small_p]
        col_p, q2c_p = [p[:, 8:8 + TPB] for p in small_p], [p[:, 16:16 + KD] for p in small_p]
        WEIGHTS = [(wl, "L3_wl"), (wcq, "L3_wcq"), (wc, "L3_wc"), (wqv, "L3_wqv"), (b3, "L3_b3"), (bl, "L3_bl")]
        block = ctx.enter_context(nc.Block())

        @block.sync
        def _(sp):
            for dst, name in WEIGHTS:
                sp.dma_start(dst[:], d[name]).then_inc(w_loaded, 16)
            with sp.Fori(0, B // 2) as i:
                for a in range(2):
                    sp.wait_ge(ctx_used[a], i + 1)
                    sp.dma_start(ctxT[:, a], d["ctxT"][:, bass.ds((2 * i + a) * KD, KD), :]).then_inc(ctx_loaded[a], 16)
                    sp.dma_start(cx[:, a], d["ctx"][:, bass.ds((2 * i + a) * TPB, TPB), :]).then_inc(ctx_loaded[a], 16)

        @block.gpsimd
        def _(pool):
            with pool.Fori(0, B // 2) as i:
                layernorm_pool(pool, sh, stats_ready, rstd_ready, i, n=2 * TPB)

        @block.vector
        def _(dve):
            def statistics(i):
                layernorm_statistics(dve, sh, lambda t: x_tile(sh, i * 2 * TPB + t), stats, stats_ready, i, n=2 * TPB)

            def normalize(i):
                layernorm_apply(dve, sh, lambda t: x_tile(sh, i * 2 * TPB + t), xn, rstd_ready, xn_ready, i, n=2 * TPB)

            def do_pair(i, last):
                for a in range(2):
                    dve.wait_ge(xnT_ready[a], i + 1)
                    for c in range(KD):
                        ins = dve.tensor_scalar(lq[:, a, c], xnT[:, a, c], wcq[:, c:c + 1], wqv[:, c:c + 1], ALU.mult, ALU.add)
                    ins.then_inc(lq_ready[a], 1)
                if not last:
                    statistics(i + 1)
                for a in range(2):
                    dve.wait_ge(s_ps[a], i + 1)
                    dve.tensor_reduce(negmax[:, a], tiles(s_p[a][:]), AX.X, ALU.max, negate=True).then_inc(max_ready[a], 1)
                    dve.wait_ge(max_ready[a], i + 1)
                    dve.scalar_tensor_tensor(smax[:, a], r_p[a], bsum[:, 0:1], negmax[:, a], ALU.add, ALU.subtract)\
                       .then_inc(smax_ready[a], 1)
                for a in range(2):
                    dve.wait_ge(row_ps[a], i + 1)
                    dve.tensor_reduce(rmax[:, a], row_p[a], AX.X, ALU.max, negate=True).then_inc(rmax_ready[a], 1)
                    dve.wait_ge(exp_ready[a], i + 1)
                    dve.reciprocal(rsums[:, a], sums[:, a]).then_inc(sums_ready[a], 1)
                    dve.wait_ge(sums_ready[a], i + 1)
                    for t in range(TPB):
                        ins = dve.tensor_scalar(probs[:, a, t], probs[:, a, t], rsums[:, a, t:t + 1], None, ALU.mult)
                    ins.then_inc(probs_ready[a], 1)
                for a in range(2):
                    dve.wait_ge(row_exp[a], i + 1)
                    dve.reciprocal(rsum[:, a], rsum[:, a]).then_inc(rsum_ready[a], 1)
                    dve.wait_ge(rsum_ready[a], i + 1)
                    dve.tensor_scalar(row[:, a], row[:, a], rsum[0:1, a, 0:1], None, ALU.mult).then_inc(row_ready[a], 1)
                for a in range(2):
                    dve.wait_ge(bcol_ps[a], i + 1)
                    dve.tensor_scalar(bcol[:, a], col_p[a], 1.0, None, ALU.mult).then_inc(bcol_ready[a], 1)
                for a in range(2):
                    dve.wait_ge(q2c_ps[a], i + 1)
                    dve.tensor_scalar(q2c[:, a], q2c_p[a], 1.0, None, ALU.mult).then_inc(q2c_ready[a], 1)
                    dve.wait_ge(q2c_ready[a], i + 1)
                    for c in range(KD):
                        ins = dve.tensor_scalar(cq[:, a, c], xnT[:, a, c], q2c[:, a, c:c + 1], None, ALU.mult)
                    ins.then_inc(cq_ready[a], 1)
                    dve.wait_ge(c2q_ready[a], i + 1)
                    dve.tensor_tensor(cc[:, a], xnT[:, a], c2qT[:, a], ALU.mult).then_inc(cc_ready[a], 1)
                if not last:
                    normalize(i + 1)
                for a in range(2):
                    dve.wait_ge(out_ps[a], i + 1)
                    for t in range(TPB):
                        ins = dve.tensor_tensor(xo[:, a, t], out_p[a][t], bl[:], ALU.add)
                    ins.then_inc(out_read[a], 1)
                    dve.wait_ge(out_read[a], i + 1)
                    xb = x_batch(sh, 2 * i + a)
                    dve.tensor_tensor(xb, xb, xo[:, a].rearrange("p t d -> p (t d)"), ALU.add)

            statistics(0)
            normalize(0)
            dve.wait_ge(w_loaded, 16 * len(WEIGHTS))
            dve.tensor_reduce(bsum[:], b3[:], AX.X, ALU.add).then_inc(bias_ready, 1)
            dve.wait_ge(bias_ready, 1)
            with dve.Fori(0, B // 2 - 1) as i:
                do_pair(i, last=False)
            do_pair(B // 2 - 1, last=True)

        @block.scalar
        def _(act):
            with act.Fori(0, B // 2) as i:
                for a in range(2):
                    act.wait_ge(xnT_ps[a], i + 1)
                    act.activation(xnT[:, a].rearrange("p c s -> p (c s)"), xnT_p[a][:], ACT.Copy).then_inc(xnT_ready[a], 1)
                for a in range(2):
                    act.wait_ge(max_ready[a], i + 1)
                    for t in range(TPB):
                        ins = act.activation(probs[:, a, t], s_p[a][:, t * S:(t + 1) * S], ACT.Exp, bias=negmax[:, a, t:t + 1],
                                             accum_out=sums[:, a, t:t + 1])
                    ins.then_inc(exp_ready[a], 1)
                for a in range(2):
                    act.wait_ge(rmax_ready[a], i + 1)
                    act.activation(row[:, a], row_p[a], ACT.Exp, bias=rmax[0:1, a, 0:1], accum_out=rsum[:, a]).then_inc(row_exp[a], 1)
                for a in range(2):
                    act.wait_ge(probsT_ps[a], i + 1)
                    act.activation(probsT[:, a].rearrange("p c s -> p (c s)"), probsT_p[a][:], ACT.Copy).then_inc(probsT_ready[a], 1)
                for a in range(2):
                    act.wait_ge(c2q_ps[a], i + 1)
                    act.activation(c2qT[:, a].rearrange("p c s -> p (c s)"), c2q_p[a][:], ACT.Copy).then_inc(c2q_ready[a], 1)

        @block.tensor
        def _(pe):
            for a in range(2):
                pe.sem_inc(ctx_used[a], 1)
            pe.wait_ge(w_loaded, 16 * len(WEIGHTS))

            def add_to_out(src, n, batches=(0, 1)):
                for a in batches:
                    for t in range(TPB):
                        for c in range(KD):
                            k = n * KD + c
                            ins = pe.matmul(out_p[a][t], src[:, a, c, t * P:(t + 1) * P], wl[:, k],
                                            start=(k == 0), stop=(k == 4 * KD - 1))
                return ins

            with pe.Fori(0, B // 2) as i:
                pe.wait_ge(xn_ready, i + 1)
                for a in range(2):
                    transpose_batch(pe, sh, xnT_p[a], xn[:, a * TPB:(a + 1) * TPB]).then_inc(xnT_ps[a], 1)
                for a in range(2):
                    pe.wait_ge(xnT_ready[a], i + 1)
                    for t in range(TPB):
                        product(pe, r_p[a][:, t:t + 1], [xnT[:, a, c, t * P:(t + 1) * P] for c in range(KD)],
                                [wc[:, c:c + 1] for c in range(KD)])
                for a in range(2):
                    pe.wait_ge(ctx_loaded[a], i * 32 + 32)
                    pe.wait_ge(lq_ready[a], i + 1)
                    pe.wait_ge(out_read[a], i)
                    for t in range(TPB):
                        ins = product(pe, s_p[a][:, t * S:(t + 1) * S], [lq[:, a, c, t * P:(t + 1) * P] for c in range(KD)],
                                      [ctxT[:, a, c] for c in range(KD)])
                    ins.then_inc(s_ps[a], 1)
                for a in range(2):
                    pe.wait_ge(smax_ready[a], i + 1)
                    for t in range(TPB):
                        ins = pe.matmul(row_p[a][:, t * P:(t + 1) * P], smax[:, a, t:t + 1], sh.ident[:], start=True, stop=True)
                    ins.then_inc(row_ps[a], 1)
                for a in range(2):
                    pe.wait_ge(probs_ready[a], i + 1)
                    transpose_batch(pe, sh, probsT_p[a], probs[:, a]).then_inc(probsT_ps[a], 1)
                for a in range(2):
                    pe.wait_ge(row_ready[a], i + 1)
                    for t in range(TPB):
                        ins = pe.matmul(col_p[a][:, t:t + 1], row[0:1, a, t * P:(t + 1) * P], sh.ones[0:1, 0:1], start=True, stop=True)
                    ins.then_inc(bcol_ps[a], 1)
                for a in range(2):
                    pe.wait_ge(probsT_ready[a], i + 1)
                    for m in range(KD):
                        ins = product(pe, c2q_p[a][:, m * S:(m + 1) * S], [cx[:, a, c, m * P:(m + 1) * P] for c in range(TPB)],
                                      [probsT[:, a, c] for c in range(TPB)])
                    ins.then_inc(c2q_ps[a], 1)
                add_to_out(xnT, 0)
                for a in range(2):
                    pe.wait_ge(bcol_ready[a], i + 1)
                    for m in range(KD):
                        ins = product(pe, q2c_p[a][:, m:m + 1], [xn[:, a * TPB + t, m * P:(m + 1) * P] for t in range(TPB)],
                                      [bcol[:, a, t:t + 1] for t in range(TPB)])
                    ins.then_inc(q2c_ps[a], 1)
                    pe.wait_ge(c2q_ps[a], i + 1)
                    pe.sem_inc(ctx_used[a], 1)
                for a in range(2):
                    pe.wait_ge(c2q_ready[a], i + 1)
                add_to_out(c2qT, 1)
                for a in range(2):
                    pe.wait_ge(cc_ready[a], i + 1)
                    add_to_out(cc, 2, [a])
                    pe.wait_ge(cq_ready[a], i + 1)
                    add_to_out(cq, 3, [a]).then_inc(out_ps[a], 1)


def stage_l2_ffn(nc, sh, d):
    experts(nc, sh, d, "f", "L2", I2, gated=True)


def stage_l3_ffn(nc, sh, d):
    experts(nc, sh, d, "h", "L3", F3, gated=False)


def experts(nc, sh, d, tag, layer, width, gated):
    with ExitStack() as ctx:
        def sb(name, shape, dt=F32):
            return ctx.enter_context(nc.sbuf_tensor(f"{tag}_{name}", shape, dt))

        NC = -(-width // P)
        size = [min(P, width - c * P) for c in range(NC)]
        NIN = 2 if gated else 1
        WIN, WCOLS = NIN * KD * width, NIN * KD * width + NC * D
        BLK, NB = 512, TOK // 512
        packed = [gated and c == NC - 1 for c in range(NC)]
        w_stage = sb("w_stage", [P, WCOLS + (0 if gated else NC)])
        w_split = sb("w_split", [P, 2, 2, WCOLS], F32R)
        bias = sb("bias", [P, 2, NC])

        def w_in(k, kd, c, m):
            at = kd * NIN * width + (NIN * c + m) * P
            return [w_split[:, k, hl, at:at + P] for hl in range(2)]

        def w_out(k, c):
            return [w_split[:, k, hl, WIN + c * D:WIN + (c + 1) * D] for hl in range(2)]

        wr, small = sb("wr", [P, KD, NE]), sb("small", [P, NE])
        if not gated:
            nw, b2, wtsT = sb("nw", [P, KD]), sb("b2", [NE, D]), sb("wtsT", [NE, TOK])
            square, ms, rms = sb("square", [P, GROUP, D]), sb("ms", [P, GROUP]), sb("rms", [P, GROUP])
        iota_i, iota = sb("iota_i", [P, NE], I32), sb("iota", [P, NE])
        work = sb("work", [P, 4, BLK])
        xn, h, act_out = work[:].rearrange("p a (b d) -> p (a b) d", d=D), work[:, 0:2], work[:, 2:4]
        xnT = sb("xnT", [P, 2, KD, TOK], F32R)
        wr_split = sb("wr_split", [P, KD, 2, NE], F32R)
        hT = sb("hT", [P, 2, 2 * NC - (1 if gated else 0), BLK], F32R)
        logits, top, topi, topf = sb("logits", [P, NT, NE]), sb("top", [P, NT, 8]), sb("topi", [P, NT, 8], U32), sb("topf", [P, NT, 8])
        dl, rw1, rw2 = sb("dl", [P, NT]), sb("rw1", [P, NT]), sb("rw2", [P, NT])
        wt1, wt2, wts, wcol = sb("wt1", [P, NT, NE]), sb("wt2", [P, NT, NE]), sb("wts", [P, NT, NE]), sb("wcol", [P, 2, NT])
        (s_loaded, stats, stats_ready, rstd_ready, xn_ready, ms_ready, rms_ready, t_ready, xnT_ps, xnT_high, xnT_kept, logits_ps,
         iota_ready, step, top_ready, exp_ready, wts_ready, wcol_ready, act_ready, h_made, h_high, h_done, in_ps, down_ps,
         acc_done, wtsT_ps, wtsT_ready, bias_ps, w_loaded, w_taken, w_high, w_ready, wr_high, wr_ready) = semaphores(
            nc, ctx, tag, "s_loaded stats stats_ready rstd_ready xn_ready ms_ready rms_ready t_ready xnT_ps xnT_high xnT_kept "
            "logits_ps iota_ready step top_ready exp_ready wts_ready wcol_ready act_ready h_made h_high h_done in_ps down_ps "
            "acc_done wtsT_ps wtsT_ready bias_ps w_loaded w_taken w_high w_ready wr_high wr_ready")
        bank = sh.bank
        in_p = [[bank[0], bank[2]], [bank[1], bank[3]]]
        down_p = [bank[4], bank[5], bank[6], bank[7]]
        SMALL = [(wr, layer + "_wr"), (small, layer + "_small")] + ([] if gated else [(nw, layer + "_nw"), (b2, layer + "_b2")])
        n_step_bias = 10
        STEPS = 2 * NB
        block = ctx.enter_context(nc.Block())

        @block.sync
        def _(sp):
            for dst, name in SMALL:
                sp.dma_start(dst[:], d[name]).then_inc(s_loaded, 16)
            sp.dma_start(w_stage[:], d[layer + "_w"][:, 0]).then_inc(w_loaded, 16)
            with sp.Fori(0, NE - 1) as e:
                sp.wait_ge(w_ready, e + 1)
                sp.dma_start(w_stage[:], d[layer + "_w"][:, bass.ds(e + 1, 1), :].rearrange("p e w -> p (e w)")).then_inc(w_loaded, 16)

        @block.gpsimd
        def _(pool):
            pool.iota(iota_i[:], [[1, NE]], base=0, channel_multiplier=0).then_inc(iota_ready, 1)
            for g in range(NT // GROUP):
                layernorm_pool(pool, sh, stats_ready, rstd_ready, g, n=GROUP)
                if not gated:
                    pool.wait_ge(ms_ready, g + 1)
                    pool.tensor_tensor(rms[:], ms[:], sh.minus_half[:], ALU.pow).then_inc(rms_ready, 1)

            def split(e, k):
                pool.wait_ge(w_loaded, 16 * e + 16)
                pool.sem_inc(w_taken, 1)
                if not gated:
                    pool.tensor_copy(bias[:, k], w_stage[:, WCOLS:WCOLS + NC])
                pool.tensor_copy(w_split[:, k, 0], w_stage[:, 0:WCOLS]).then_inc(w_high, 1)
                pool.wait_ge(w_high, e + 1)
                pool.tensor_tensor(w_split[:, k, 1], w_stage[:, 0:WCOLS], w_split[:, k, 0].bitcast(F32), ALU.subtract).then_inc(w_ready, 1)

            split(0, 0)
            split(1, 1)
            with pool.Fori(1, NE // 2) as i:
                for k in range(2):
                    pool.wait_ge(down_ps, 2 * (STEPS * (i - 1) + (k + 1) * NB))
                    split(2 * i + k, k)

        @block.vector
        def _(dve):
            def statistics(g):
                layernorm_statistics(dve, sh, lambda t: x_tile(sh, g * GROUP + t), stats, stats_ready, g, n=GROUP)

            statistics(0)
            for g in range(NT // GROUP):
                xg = sh.X[:, g * GROUP * D:(g + 1) * GROUP * D]
                if g:
                    dve.wait_ge(xnT_ps, g * 2 * KD)
                layernorm_apply(dve, sh, lambda t: xg[:, t * D:(t + 1) * D], xn, rstd_ready, xn_ready, g, n=GROUP)
                if not gated:
                    dve.wait_ge(xn_ready, g + 1)
                    dve.tensor_tensor(xg, xg, xn.rearrange("p t d -> p (t d)"), ALU.add)
                if g + 1 < NT // GROUP:
                    statistics(g + 1)
                if not gated:
                    dve.wait_ge(t_ready, 2 * g + 1)
                    dve.tensor_scalar(ms[:], ms[:], 1.0 / D, RMS_EPS, ALU.mult, ALU.add).then_inc(ms_ready, 1)
                    dve.wait_ge(rms_ready, g + 1)
                    for t in range(GROUP):
                        ins = dve.tensor_scalar(xn[:, t], xn[:, t], rms[:, t:t + 1], None, ALU.mult)
                    ins.then_inc(t_ready, 1)
                if g == 0:
                    dve.wait_ge(s_loaded, 16 * len(SMALL))
                    dve.tensor_copy(wr_split[:, :, 0], wr[:]).then_inc(wr_high, 1)
                    dve.wait_ge(wr_high, 1)
                    dve.tensor_tensor(wr_split[:, :, 1], wr[:], wr_split[:, :, 0].bitcast(F32), ALU.subtract).then_inc(wr_ready, 1)
                for c in range(KD):
                    for n in range(2):
                        dve.wait_ge(xnT_high, (g * KD + c) * 2 + n + 1)
                        at = (g * 2 + n) * 512
                        dve.scalar_tensor_tensor(xnT[:, 1, c, at:at + 512], bank[2 * c + n][:], 1.0 if gated else nw[:, c:c + 1],
                                                 xnT[:, 0, c, at:at + 512].bitcast(F32), ALU.mult, ALU.subtract)\
                           .then_inc(xnT_kept, 1)
            if gated:
                dve.sem_inc(h_made, 2)
            n_step = [0]

            def link(ins):
                n_step[0] += 1
                ins.then_inc(step, 1)
                dve.wait_ge(step, n_step[0])

            dve.wait_ge(iota_ready, 1)
            dve.tensor_copy(iota[:], iota_i[:])
            dve.wait_ge(logits_ps, 1)
            parts = bank[7][:, 0:NT * 2 * NE].rearrange("p (t a e) -> p t a e", a=2, e=NE)
            link(dve.tensor_tensor(logits[:], parts[:, :, 0], small[:].unsqueeze(1).to_broadcast([P, NT, NE]), ALU.add))
            link(dve.tensor_tensor(logits[:], logits[:], parts[:, :, 1], ALU.add))
            for t in range(NT):
                ins = dve.max(top[:, t], logits[:, t])
            link(ins)
            for t in range(NT):
                ins = dve.max_index(topi[:, t], top[:, t], logits[:, t])
            link(ins)
            dve.tensor_copy(topf[:], topi[:])
            dve.tensor_tensor(dl[:], top[:, :, 1], top[:, :, 0], ALU.subtract).then_inc(top_ready, 1)
            dve.wait_ge(exp_ready, 1)
            link(dve.tensor_scalar(rw1[:], rw2[:], 1.0, None, ALU.add))
            link(dve.reciprocal(rw1[:], rw1[:]))
            link(dve.tensor_tensor(rw2[:], rw2[:], rw1[:], ALU.mult))
            over_e = lambda ap: ap.to_broadcast([P, NT, NE])
            iota_t = iota[:].unsqueeze(1).to_broadcast([P, NT, NE])
            dve.tensor_tensor(wt1[:], iota_t, over_e(topf[:, :, 0:1]), ALU.is_equal)
            link(dve.tensor_tensor(wt2[:], iota_t, over_e(topf[:, :, 1:2]), ALU.is_equal))
            dve.tensor_tensor(wt1[:], wt1[:], over_e(rw1[:].unsqueeze(2)), ALU.mult)
            link(dve.tensor_tensor(wt2[:], wt2[:], over_e(rw2[:].unsqueeze(2)), ALU.mult))
            link(dve.tensor_tensor(wts[:], wt1[:], wt2[:], ALU.add))
            if gated:
                link(dve.memset(wts[:, :, NE - 1:NE], 1.0))
            dve.tensor_scalar(wt1[:], wts[:], 1.0, None, ALU.mult).then_inc(wts_ready, 1)
            if not gated:
                for n in range(NT // 4):
                    dve.wait_ge(wtsT_ps, n + 1)
                    dve.tensor_copy(wtsT[:, n * 512:(n + 1) * 512], bank[4 + n][0:NE, :]).then_inc(wtsT_ready, 1)
                for n in range(NT // 2):
                    dve.wait_ge(bias_ps, n + 1)
                    link(dve.tensor_tensor(sh.X[:, n * 512:(n + 1) * 512], sh.X[:, n * 512:(n + 1) * 512], bank[n % 4][:], ALU.add))

            dve.wait_ge(wts_ready, 1)
            dve.sem_inc(acc_done, 4)
            dve.sem_inc(h_done, 2)
            with dve.Fori(0, NE // 2) as i:
                def accumulate(s, half):
                    a = 2 * s + half
                    dve.wait_ge(down_ps, 2 * STEPS * i + a + 1)
                    dve.wait_ge(acc_done, 2 * STEPS * i + a + 4)
                    for q in range(2):
                        tile = s % NB * 4 + 2 * half + q
                        xt = sh.X[:, tile * D:(tile + 1) * D]
                        ins = dve.scalar_tensor_tensor(xt, down_p[a % 4][:, q * D:(q + 1) * D], wcol[:, s // NB, tile:tile + 1],
                                                       xt, ALU.mult, ALU.add)
                    ins.then_inc(acc_done, 1)

                for s in range(STEPS):
                    if s % NB == 0:
                        dve.tensor_copy(wcol[:, s // NB], wts[:, :, bass.ds(2 * i + s // NB, 1)].rearrange("p t e -> p (t e)"))\
                           .then_inc(wcol_ready, 1)
                        dve.wait_ge(wcol_ready, 2 * i + s // NB + 1)
                    for c in range(NC):
                        j = s * NC + c
                        rows = slice(64, P) if packed[c] else slice(0, P)
                        if gated:
                            dve.wait_ge(act_ready, STEPS * NC * i + j + 1)
                            dve.wait_ge(h_done, STEPS * NC * i + j + 1)
                            if c == 0 and s >= 2:
                                dve.wait_ge(down_ps, 2 * STEPS * i + 2 * (s - 1))
                            dve.tensor_tensor(h[rows, c % 2], in_p[c % 2][0 if packed[c] else 1][rows, :], act_out[rows, c % 2],
                                              ALU.mult).then_inc(h_made, 1)
                        if s >= 1 and c in (2, 3):
                            accumulate(s - 1, c - 2)
                        dve.wait_ge(h_high, STEPS * NC * i + j + 1)
                        dve.tensor_tensor(hT[0:64, s % 2, 2 * c] if packed[c] else hT[:, s % 2, 2 * c + 1], h[rows, c % 2],
                                          hT[rows, s % 2, 2 * c].bitcast(F32), ALU.subtract).then_inc(h_done, 1)
                accumulate(STEPS - 1, 0)
                accumulate(STEPS - 1, 1)
            dve.wait_ge(acc_done, 4 + NE * NB * 2)

        @block.scalar
        def _(act):
            act.wait_ge(s_loaded, 16 * len(SMALL))
            for g in range(NT // GROUP):
                if not gated:
                    act.wait_ge(xn_ready, g + 1)
                    for t in range(GROUP):
                        ins = act.activation(square[:, t], xn[:, t], ACT.Square, accum_out=ms[:, t:t + 1])
                    ins.then_inc(t_ready, 1)
                for c in range(KD):
                    for n in range(2):
                        act.wait_ge(xnT_ps, (g * KD + c) * 2 + n + 1)
                        at = (g * 2 + n) * 512
                        act.activation(xnT[:, 0, c, at:at + 512], bank[2 * c + n][:], ACT.Copy,
                                       scale=1.0 if gated else nw[:, c:c + 1]).then_inc(xnT_high, 1)
            act.wait_ge(top_ready, 1)
            act.activation(rw2[:], dl[:], ACT.Exp).then_inc(exp_ready, 1)
            if not gated:
                act.sem_inc(h_made, 2)
            with act.Fori(0, NE // 2) as i:
                for s in range(STEPS):
                    for c in range(NC):
                        j = s * NC + c
                        act.wait_ge(in_ps, STEPS * NC * i + j + 1)
                        rows = slice(64, P) if packed[c] else slice(0, P)
                        if gated:
                            act.wait_ge(h_made, STEPS * NC * i + j + 1)
                            act.activation(act_out[rows, c % 2], in_p[c % 2][0][0:64 if packed[c] else P, :], ACT.Silu)\
                               .then_inc(act_ready, 1)
                        else:
                            act.wait_ge(h_done, STEPS * NC * i + j + 1)
                            if c == 0 and s >= 2:
                                act.wait_ge(down_ps, 2 * STEPS * i + 2 * (s - 1))
                            act.activation(h[:, c % 2], in_p[c % 2][0][:], ACT.Gelu, bias=bias[:, s // NB, c:c + 1])\
                               .then_inc(h_made, 1)
                        act.wait_ge(h_made, STEPS * NC * i + j + 3)
                        act.activation(hT[rows, s % 2, 2 * c], h[rows, c % 2], ACT.Copy).then_inc(h_high, 1)

        @block.tensor
        def _(pe):
            pe.wait_ge(s_loaded, 16 * len(SMALL))
            for g in range(NT // GROUP):
                pe.wait_ge(xn_ready if gated else t_ready, g + 1 if gated else 2 * g + 2)
                for c in range(KD):
                    for n in range(2):
                        if g:
                            pe.wait_ge(xnT_kept, ((g - 1) * KD + c) * 2 + n + 1)
                        for q in range(4):
                            ins = pe.transpose(bank[2 * c + n][:, q * P:(q + 1) * P], xn[:, 4 * n + q, c * P:(c + 1) * P], sh.ident[:])
                        ins.then_inc(xnT_ps, 1)
            pe.wait_ge(wr_ready, 1)
            pe.wait_ge(xnT_kept, NT // GROUP * 2 * KD)
            for t in range(NT):
                ins = product(pe, bank[7][:, t * 2 * NE:(t + 1) * 2 * NE],
                              [xnT[:, hl, c, t * P:(t + 1) * P] for c in range(KD) for hl in range(2)],
                              [wr_split[:, c].rearrange("p a e -> p (a e)") for c in range(KD) for hl in range(2)])
            ins.then_inc(logits_ps, 1)
            if not gated:
                pe.wait_ge(wts_ready, 1)
                for n in range(NT // 4):
                    for q in range(4):
                        ins = pe.transpose(bank[4 + n][0:NE, q * P:(q + 1) * P], wts[:, 4 * n + q], sh.ident[:])
                    ins.then_inc(wtsT_ps, 1)
                pe.wait_ge(wtsT_ready, NT // 4)
                for n in range(NT // 2):
                    if n >= 4:
                        pe.wait_ge(step, n_step_bias + n - 3)
                    for q in range(2):
                        t = 2 * n + q
                        ins = pe.matmul(bank[n % 4][:, q * D:(q + 1) * D], wtsT[:, t * P:(t + 1) * P], b2[:], start=True, stop=True)
                    ins.then_inc(bias_ps, 1)
                pe.wait_ge(step, n_step_bias + NT // 2)
            with pe.Fori(0, NE // 2) as i:
                def down(s):
                    pe.wait_ge(h_done, STEPS * NC * i + (s + 1) * NC + 2)
                    for half in range(2):
                        a = 2 * s + half
                        pe.wait_ge(acc_done, 2 * STEPS * i + a + 1)
                        for q in range(2):
                            tok = slice((2 * half + q) * P, (2 * half + q + 1) * P)
                            out = down_p[a % 4][:, q * D:(q + 1) * D]
                            for c in range(NC):
                                w = w_out(s // NB, c)
                                if packed[c]:
                                    for hl in range(2):
                                        ins = pe.matmul(out, hT[:, s % 2, 2 * c, tok], w[hl], start=False, stop=(hl == 1))
                                else:
                                    high, low = hT[:, s % 2, 2 * c, tok], hT[:, s % 2, 2 * c + 1, tok]
                                    pe.matmul(out, high, w[0], start=(c == 0), stop=False)
                                    pe.matmul(out, high, w[1], start=False, stop=False)
                                    ins = pe.matmul(out, low, w[0], start=False, stop=(c == NC - 1))
                        ins.then_inc(down_ps, 1)

                for s in range(STEPS):
                    if s % NB == 0:
                        pe.wait_ge(w_ready, 2 * i + s // NB + 1)
                    for c in range(NC):
                        j = s * NC + c
                        pe.wait_ge(h_made, STEPS * NC * i + j + 1)
                        for m in range(1 if packed[c] else NIN):
                            tok = slice(s % NB * BLK, (s % NB + 1) * BLK)
                            ins = product_split(pe, in_p[c % 2][m][:], [w_in(s // NB, k, c, m) for k in range(KD)],
                                                [[xnT[:, hl, k, tok] for hl in range(2)] for k in range(KD)])
                        ins.then_inc(in_ps, 1)
                        if c == 1 and s >= 1:
                            down(s - 1)
                down(STEPS - 1)

STAGES = [stage_l0_attention, stage_l0_ffn, stage_l1_attention, stage_l1_ffn,
          stage_l2_attention, stage_l2_ffn, stage_l3_attention, stage_l3_ffn]


def program(nc, d, out, n_stages=99):
    with ExitStack() as ctx:
        def sb(name, shape, dt=F32):
            return ctx.enter_context(nc.sbuf_tensor(name, shape, dt))

        sh = Shared()
        sh.X = sb("X", [P, NT * D])
        sh.ident, sh.ident16 = sb("ident", [P, P]), sb("ident16", [P, P], BF16)
        sh.ones, sh.minus_half = sb("ones", [P, P]), sb("minus_half", [P, GROUP])
        sh.bn6, sh.mv = sb("bn6", [P, GROUP, 6]), sb("mv", [P, GROUP, 2])
        sh.var, sh.rstd = sb("var", [P, GROUP]), sb("rstd", [P, GROUP])
        sh.bank = [ctx.enter_context(nc.psum_tensor(f"bank{i}", [P, 512], F32)) for i in range(8)]
        stage_start(nc, sh, d)
        for stage in STAGES[:n_stages]:
            stage(nc, sh, d)
        stored = ctx.enter_context(nc.semaphore("stored"))
        block = ctx.enter_context(nc.Block())

        @block.sync
        def _(sp):
            sp.dma_start(out, tiles(sh.X[:], NT)).then_inc(stored, 16)
            sp.wait_ge(stored, 16)


def laid_out(inputs):
    import numpy as np

    g = {k: np.asarray(v) for k, v in inputs.items()}

    def rows(w, n=None):
        k, n = w.shape
        return np.ascontiguousarray(w.reshape(k // P, P, n).transpose(1, 0, 2))

    def column(v):
        return np.ascontiguousarray(v.reshape(-1, P).T)

    def everywhere(v):
        return np.ascontiguousarray(np.broadcast_to(v.reshape(1, -1), (P, v.size)))

    def tokens(a):
        return rows(a.reshape(TOK, -1))

    def heads(w):
        w = w.reshape(w.shape[:-1] + (H, 1, DK0))
        return np.broadcast_to(w, w.shape[:-2] + (2, DK0)).reshape(w.shape[:-3] + (H * PAD0,))

    def padded(w):
        w = w.reshape(w.shape[:-1] + (H, DK0))
        return np.concatenate([w, np.zeros_like(w)], axis=-1).reshape(w.shape[:-2] + (H * PAD0,))

    a = {}
    a["x"] = tokens(g["x"])
    a["ctx"] = tokens(g["ctx_1024"])
    a["ctxT"] = np.ascontiguousarray(g["ctx_1024"].reshape(B, S, KD, P).transpose(3, 0, 2, 1).reshape(P, B * KD, S))
    a["mask"] = tokens(g["mask_BxSxS2_ik1"])
    p = "L0_xattn_"
    a["L0_wq"], a["L0_wk"] = rows(heads(g[p + "Wq"])), rows(heads(g[p + "Wk"]))
    a["L0_bq"], a["L0_bk"] = column(heads(g[p + "bq"])), column(heads(g[p + "bk"]))
    a["L0_wv"], a["L0_wo"] = rows(padded(g[p + "Wv"])), rows(padded(g[p + "Wo"].T).T)
    a["L0_bv"], a["L0_bo"] = everywhere(padded(g[p + "bv"])), everywhere(g[p + "bo"])
    a["L0_low_rows"] = np.where(np.arange(P) % PAD0 < DK0, 0, -1).astype(np.float32).reshape(P, 1)
    p = "L0_ffn_"
    a["L0_w1"], a["L0_w2"] = rows(g[p + "W1"].T).reshape(P, -1), rows(g[p + "W2"].T).reshape(P, -1)
    a["L0_b1"], a["L0_b2"] = everywhere(g[p + "b1"]), everywhere(g[p + "b2"])
    p = "L1_xattn_"
    ws = (g[p + "Wq"], g[p + "Wkv"][:, :INNER1], g[p + "Wkv"][:, INNER1:], g[p + "Wm"])
    a["L1_w"] = np.stack([rows(w).reshape(P, KD, M1, P).transpose(0, 2, 1, 3) for w in ws], axis=2)
    a["L1_wo"], a["L1_bo"] = rows(g[p + "Wo"]), everywhere(g[p + "bo"])
    a["L1_g"], a["L1_b"] = column(g[p + "ln_g"]), column(g[p + "ln_b"])
    p = "L1_ffn_"
    a["L1_gw1"], a["L1_gb1"] = rows(g[p + "gate_w1"].T), column(g[p + "gate_b1"])
    gw2T = g[p + "gate_w2"].T
    a["L1_gw2r"] = rows(np.repeat(gw2T, R1, axis=1))
    a["L1_gb2r"] = np.repeat(g[p + "gate_b2"], R1).reshape(P, 1)
    a["L1_gw2a"] = rows(np.concatenate([gw2T, np.zeros((D, 1), gw2T.dtype)], axis=1))
    a["L1_gb2a"] = np.concatenate([g[p + "gate_b2"], np.ones(1, gw2T.dtype)]).reshape(E1 + 1, 1)
    a["L1_tb1"] = np.concatenate([g[p + "Tb1"], g[p + "b1"][None]])
    a["L1_tb2"] = np.concatenate([g[p + "Tb2"], g[p + "b2"][None]])
    a["L1_w1"], a["L1_w2"] = rows(g[p + "W1"].T), rows(g[p + "W2"].T)
    blocks = lambda w: np.ascontiguousarray(w.reshape(E1, -1, R1, w.shape[2]).transpose(0, 2, 1, 3)).reshape(P, -1)
    a["L1_tw1"], a["L1_tw2"] = blocks(g[p + "TW1"]), blocks(g[p + "TW2"])
    p = "L2_xattn_"
    for n in ("q", "k", "v", "g", "o"):
        a["L2_w" + n] = rows(g[p + "W" + n])
        a["L2_b" + n] = everywhere(g[p + "b" + n]) if n in "vo" else column(g[p + "b" + n])
    p = "L2_ffn_"
    wr = np.concatenate([g[p + "wr"].T, np.zeros((D, NE - E2), np.float32)], axis=1)
    a["L2_wr"] = rows(wr)
    a["L2_small"] = everywhere(np.concatenate([g[p + "rb"], np.full(NE - E2, NEVER, np.float32)]))

    def expert(w_in, w_out, tail=()):
        width = w_out.shape[1]
        whole = width // P * P
        cols = [w[c:c + P] for c in range(0, whole, P) for w in w_in] + [w[whole:] for w in w_in]
        out = np.concatenate([w_out.T[:whole], w_out.T[whole:], w_out.T[whole:]])
        return np.concatenate([rows(np.concatenate(cols).T).reshape(P, -1), rows(out).reshape(P, -1), *tail], axis=1)

    a["L2_w"] = np.stack([expert([g[p + "rg"][e], g[p + "ru"][e]], g[p + "rd"][e]) for e in range(E2)]
                         + [expert([g[p + "sg"], g[p + "su"]], g[p + "sd"])], axis=1)
    p = "L3_xattn_"
    a["L3_wl"], a["L3_bl"] = rows(g[p + "W_l"].T), everywhere(g[p + "b_l"])
    a["L3_wcq"], a["L3_wc"], a["L3_wqv"] = column(g[p + "w_cq"]), column(g[p + "w_c"]), column(g[p + "w_q"])
    a["L3_b3"] = everywhere(np.stack([g[p + "b_c"], g[p + "b_q"], g[p + "b_cq"]]))
    p = "L3_ffn_"
    a["L3_nw"], a["L3_wr"] = column(g[p + "norm_weight"]), rows(g[p + "gate_w"].T)
    a["L3_small"], a["L3_b2"] = np.zeros((P, NE), np.float32), g[p + "b2"]
    a["L3_w"] = np.stack([expert([g[p + "w1"][e]], g[p + "w2"][e], [column(g[p + "b1"][e])]) for e in range(E3)], axis=1)
    return {k: np.ascontiguousarray(v) for k, v in a.items()}


def kernel(**inputs):
    import numpy as np
    import concourse.bacc as bacc
    from concourse.bass_utils import run_bass_kernel_spmd

    nc = bacc.Bacc("TRN2", target_bir_lowering=False, num_devices=1)
    arrays = laid_out(inputs)
    d = {name: nc.dram_tensor("in_" + name, a.shape, mybir.dt.from_np(a.dtype), kind="ExternalInput").ap()
         for name, a in arrays.items()}
    out = nc.dram_tensor("out_x", (P, NT, D), F32, kind="ExternalOutput").ap()
    program(nc, d, out)
    r = run_bass_kernel_spmd(nc, [{"in_" + name: a for name, a in arrays.items()}], core_ids=[0])
    return np.ascontiguousarray(r.results[0]["out_x"].transpose(1, 0, 2)).reshape(B, S, D)
```
